# Optimizing a Trainium2 kernel written in Bass

```python
import numpy as np
import jax
import jax.numpy as jnp

def _softmax(x, axis=-1):
    return jax.nn.softmax(x, axis=axis)

def _gelu(x):
    return jax.nn.gelu(x, approximate=True)

def _silu(x):
    return jax.nn.silu(x)

def _sigmoid(x):
    return jax.nn.sigmoid(x)

def _layernorm(x, axis=-1, eps=1e-05):
    m = jnp.mean(x, axis=axis, keepdims=True)
    v = jnp.var(x, axis=axis, keepdims=True)
    return (x - m) / jnp.sqrt(v + eps)

def _scatter_add(tgt, idx, src, axis=0):
    return tgt.at[idx].add(src)

def _segment_sum(src, seg, n):
    return jax.ops.segment_sum(src, seg, n)
kernel_name = 'mk_xattn_ffn_d2_seqx_r4_f63f3b'

def setup_inputs(seed: int=0):
    np.random.seed(seed)
    _w = jnp.asarray

    def _rec_inputs():
        import jax
        import jax.numpy as jnp
        _rk = jax.random.key(seed)
        x = -0.000125 + 0.9999 * jax.random.normal(jax.random.fold_in(_rk, 1), (32, 128, 256), jnp.float32)
        _lenS = 128 - jax.random.randint(jax.random.fold_in(_rk, 7), (32,), 0, max(1, 128 // 4) + 1, jnp.int32)
        _lenS2 = 128 - jax.random.randint(jax.random.fold_in(_rk, 8), (32,), 0, max(1, 128 // 4) + 1, jnp.int32)
        _ctx_1024P = jax.random.normal(jax.random.fold_in(_rk, 11), (32, 16, 256), jnp.float32)
        _ctx_1024c = jax.random.dirichlet(jax.random.fold_in(_rk, 511), 0.3 * jnp.ones((16,), jnp.float32), (32, 128))
        _ctx_1024t = jnp.einsum('bsk,bkd->bsd', _ctx_1024c, _ctx_1024P)
        _ctx_1024t = _ctx_1024t * jax.lax.rsqrt(jnp.mean(jnp.square(_ctx_1024t)) + 1e-12) * 0.953939
        ctx_1024 = -1.52775e-05 + 0.999936 * (_ctx_1024t + 0.3 * jax.random.normal(jax.random.fold_in(_rk, 611), (32, 128, 256), jnp.float32))
        return (x, ctx_1024)
    x, ctx_1024 = _rec_inputs()

    def _L0_xattn_setup():
        import jax, jax.numpy as jnp
        import numpy as np
        import math
        B, L, D, H = (8, 1024, 256, 16)
        DK = D // H
        FACTOR = 1

        def _linear(x, W, b):
            return jnp.einsum('bld,od->blo', x, W) + b
        rng = jax.random.key(seed)
        ks = jax.random.split(rng, 11)
        s = 0.02
        return {'query': jax.random.normal(ks[0], (B, L, D), jnp.float32), 'key': jax.random.normal(ks[1], (B, L, D), jnp.float32), 'value': jax.random.normal(ks[2], (B, L, D), jnp.float32), 'Wq': jax.random.normal(ks[3], (D, D), jnp.float32) * s, 'bq': jax.random.normal(ks[4], (D,), jnp.float32) * s, 'Wk': jax.random.normal(ks[5], (D, D), jnp.float32) * s, 'bk': jax.random.normal(ks[6], (D,), jnp.float32) * s, 'Wv': jax.random.normal(ks[7], (D, D), jnp.float32) * s, 'bv': jax.random.normal(ks[8], (D,), jnp.float32) * s, 'Wo': jax.random.normal(ks[9], (D, D), jnp.float32) * s, 'bo': jax.random.normal(ks[10], (D,), jnp.float32) * s}
    _L0_xattn_all = _L0_xattn_setup()
    _L0_xattn_in = {k: v for k, v in _L0_xattn_all.items() if k in ('Wq', 'bq', 'Wk', 'bk', 'Wv', 'bv', 'Wo', 'bo')}
    del _L0_xattn_all

    def _L0_ffn_setup():
        import jax, jax.numpy as jnp
        import numpy as np
        B, N, D = (4, 512, 256)
        SPARSITY = 0.01
        key = jax.random.key(seed)
        k1, k2, k3 = jax.random.split(key, 3)
        x = jax.random.normal(k1, (B, N, D), dtype=jnp.float32)
        spatial = jax.random.normal(k2, (D, D), dtype=jnp.float32) * 0.02
        freq = jnp.fft.fft(spatial, axis=-1)
        k = int(D * SPARSITY)
        mag = jnp.abs(freq)
        kth = jax.lax.top_k(mag, k)[0][:, -1:]
        w_sparse = jnp.where(mag >= kth, freq, 0.0 + 0j)
        bias = jax.random.normal(k3, (D,), dtype=jnp.float32) * 0.01
        return {'x': x, 'w_freq_real': jnp.real(w_sparse).astype(jnp.float32), 'w_freq_imag': jnp.imag(w_sparse).astype(jnp.float32), 'bias': bias}
    _L0_ffn_all = _L0_ffn_setup()
    _L0_ffn_in = {k: v for k, v in _L0_ffn_all.items() if k in ('w_freq_real', 'w_freq_imag', 'bias')}
    del _L0_ffn_all

    def _L1_xattn_setup():
        import jax, jax.numpy as jnp
        import numpy as np
        H, P = (16, 4)
        B, L, D = (2, 1024, 256)
        rng = jax.random.key(seed)
        ks = jax.random.split(rng, 12)
        w = lambda k, shape, s=0.02: jax.random.normal(k, shape, jnp.float32) * s
        return {'query': jax.random.normal(ks[0], (B, L, D), jnp.float32), 'key': jax.random.normal(ks[1], (B, L, D), jnp.float32), 'value': jax.random.normal(ks[2], (B, L, D), jnp.float32), 'w_qk': w(ks[3], (D, 2 * D)), 'b_qk': jnp.zeros((2 * D,), jnp.float32), 'w_value': w(ks[4], (D, D)), 'b_value': jnp.zeros((D,), jnp.float32), 'w_off': w(ks[5], (D, H * P * 2)), 'b_off': w(ks[6], (H * P * 2,), 0.3), 'w_attw': w(ks[7], (D, H * P)), 'b_attw': jnp.zeros((H * P,), jnp.float32), 'w_out': w(ks[8], (D, D)), 'b_out': jnp.zeros((D,), jnp.float32)}
    _L1_xattn_all = _L1_xattn_setup()
    _L1_xattn_in = {k: v for k, v in _L1_xattn_all.items() if k in ('w_qk', 'b_qk', 'w_value', 'b_value', 'w_off', 'b_off', 'w_attw', 'b_attw', 'w_out', 'b_out')}
    del _L1_xattn_all

    def _L1_ffn_setup():
        import jax, jax.numpy as jnp
        import numpy as np
        BLOCK = 32
        W_BITS = 4
        ACT_BITS = 16

        def act_qdq(x):
            qmax = 2.0 ** (ACT_BITS - 1) - 1.0
            scale = jnp.maximum(jnp.max(jnp.abs(x)) / qmax, 1e-12)
            return jnp.clip(jnp.round(x / scale), -qmax - 1.0, qmax) * scale

        def fixed_qdq_u16(x):
            scale = 1.0 / 65536.0
            return jnp.clip(jnp.round(x / scale), 0.0, 65535.0) * scale

        def lpbq_dequant(w):
            O, I = w.shape
            qmax = 2.0 ** (W_BITS - 1) - 1.0
            wb = w.reshape(O, I // BLOCK, BLOCK)
            s = jnp.maximum(jnp.max(jnp.abs(wb), axis=-1, keepdims=True) / qmax, 1e-12)
            wq = jnp.clip(jnp.round(wb / s), -qmax - 1.0, qmax) * s
            return wq.reshape(O, I)
        key = jax.random.key(seed)
        k1, k2, k3, k4 = jax.random.split(key, 4)
        B, S, H, I = (2, 1024, 256, 768)
        x = jax.random.normal(k1, (B, S, H), jnp.float32)
        w_gate = jax.random.normal(k2, (I, H), jnp.float32) * 0.02
        w_up = jax.random.normal(k3, (I, H), jnp.float32) * 0.02
        w_down = jax.random.normal(k4, (H, I), jnp.float32) * 0.02
        return {'x': x, 'w_gate': w_gate, 'w_up': w_up, 'w_down': w_down}
    _L1_ffn_all = _L1_ffn_setup()
    _L1_ffn_in = {k: v for k, v in _L1_ffn_all.items() if k in ('w_gate', 'w_up', 'w_down')}
    del _L1_ffn_all
    return {'x': x, 'ctx_1024': ctx_1024, 'L0_xattn_Wq': _L0_xattn_in['Wq'], 'L0_xattn_bq': _L0_xattn_in['bq'], 'L0_xattn_Wk': _L0_xattn_in['Wk'], 'L0_xattn_bk': _L0_xattn_in['bk'], 'L0_xattn_Wv': _L0_xattn_in['Wv'], 'L0_xattn_bv': _L0_xattn_in['bv'], 'L0_xattn_Wo': _L0_xattn_in['Wo'], 'L0_xattn_bo': _L0_xattn_in['bo'], 'L0_ffn_w_freq_real': _L0_ffn_in['w_freq_real'], 'L0_ffn_w_freq_imag': _L0_ffn_in['w_freq_imag'], 'L0_ffn_bias': _L0_ffn_in['bias'], 'L1_xattn_w_qk': _L1_xattn_in['w_qk'], 'L1_xattn_b_qk': _L1_xattn_in['b_qk'], 'L1_xattn_w_value': _L1_xattn_in['w_value'], 'L1_xattn_b_value': _L1_xattn_in['b_value'], 'L1_xattn_w_off': _L1_xattn_in['w_off'], 'L1_xattn_b_off': _L1_xattn_in['b_off'], 'L1_xattn_w_attw': _L1_xattn_in['w_attw'], 'L1_xattn_b_attw': _L1_xattn_in['b_attw'], 'L1_xattn_w_out': _L1_xattn_in['w_out'], 'L1_xattn_b_out': _L1_xattn_in['b_out'], 'L1_ffn_w_gate': _L1_ffn_in['w_gate'], 'L1_ffn_w_up': _L1_ffn_in['w_up'], 'L1_ffn_w_down': _L1_ffn_in['w_down']}

def reference(x, ctx_1024, L0_xattn_Wq, L0_xattn_bq, L0_xattn_Wk, L0_xattn_bk, L0_xattn_Wv, L0_xattn_bv, L0_xattn_Wo, L0_xattn_bo, L0_ffn_w_freq_real, L0_ffn_w_freq_imag, L0_ffn_bias, L1_xattn_w_qk, L1_xattn_b_qk, L1_xattn_w_value, L1_xattn_b_value, L1_xattn_w_off, L1_xattn_b_off, L1_xattn_w_attw, L1_xattn_b_attw, L1_xattn_w_out, L1_xattn_b_out, L1_ffn_w_gate, L1_ffn_w_up, L1_ffn_w_down):
    import jax
    import jax.numpy as jnp

    def _L0_xattn_ref(query, key, value, Wq, bq, Wk, bk, Wv, bv, Wo, bo):
        import jax, jax.numpy as jnp
        import numpy as np
        import math
        B, L, D, H = (8, 1024, 256, 16)
        DK = D // H
        FACTOR = 1

        def _linear(x, W, b):
            return jnp.einsum('bld,od->blo', x, W) + b
        Bx, Lx, _ = query.shape
        Q = _linear(query, Wq, bq).reshape(Bx, Lx, H, DK).transpose(0, 2, 1, 3)
        K = _linear(key, Wk, bk).reshape(Bx, Lx, H, DK).transpose(0, 2, 1, 3)
        V = _linear(value, Wv, bv).reshape(Bx, Lx, H, DK).transpose(0, 2, 1, 3)
        Qf = jnp.fft.rfft(Q, axis=2)
        Kf = jnp.fft.rfft(K, axis=2)
        corr = jnp.fft.irfft(Qf * jnp.conj(Kf), n=Lx, axis=2)
        corr_mean = corr.mean(axis=-1)
        top_k = max(1, int(FACTOR * math.log(Lx + 1)))
        top_k = min(top_k, Lx)
        top_w, top_idx = jax.lax.top_k(corr_mean, top_k)
        top_w = jax.nn.softmax(top_w, axis=-1)
        pos = jnp.arange(Lx)
        out = jnp.zeros_like(V)
        for i in range(top_k):
            gidx = (pos[None, None, :] - top_idx[:, :, i, None]) % Lx
            rolled = jnp.take_along_axis(V, gidx[..., None], axis=2)
            out = out + top_w[:, :, i, None, None] * rolled
        out = out.transpose(0, 2, 1, 3).reshape(Bx, Lx, D)
        out = _linear(out, Wo, bo)
        return out

    def _L0_ffn_ref(x, w_freq_real, w_freq_imag, bias):
        import jax, jax.numpy as jnp
        import numpy as np
        B, N, D = (4, 512, 256)
        SPARSITY = 0.01
        w = jax.lax.complex(w_freq_real, w_freq_imag)
        x_freq = jnp.fft.fft(x, axis=-1)
        y_freq = jnp.einsum('bnd,do->bno', x_freq, w)
        y = jnp.real(jnp.fft.ifft(y_freq, axis=-1))
        return y + bias

    def _L1_xattn_ref(query, key, value, w_qk, b_qk, w_value, b_value, w_off, b_off, w_attw, b_attw, w_out, b_out):
        import jax, jax.numpy as jnp
        import numpy as np
        H, P = (16, 4)
        B, L, D = value.shape
        Dh = D // H
        _qk = query @ w_qk + b_qk
        v = (value @ w_value + b_value).reshape(B, L, H, Dh).transpose(0, 2, 1, 3)
        off = (query @ w_off + b_off).reshape(B, L, H, P, 2)
        attw = jax.nn.softmax((query @ w_attw + b_attw).reshape(B, L, H, P), axis=-1)
        ref_y = jnp.linspace(0.0, 1.0, L)
        sx = jnp.clip(off[..., 0], 0.0, 1.0)
        sy = jnp.clip(ref_y[None, :, None, None] + off[..., 1], 0.0, 1.0)
        ix = ((sx + 1.0) * L - 1.0) * 0.5
        iy = ((sy + 1.0) * 1.0 - 1.0) * 0.5
        x0 = jnp.floor(ix)
        fx = ix - x0
        x0i = x0.astype(jnp.int32)
        x1i = x0i + 1
        m0 = ((x0i >= 0) & (x0i < L)).astype(v.dtype)
        m1 = ((x1i >= 0) & (x1i < L)).astype(v.dtype)
        y0 = jnp.floor(iy)
        fy = iy - y0
        hy = jnp.where(y0 == 0.0, 1.0 - fy, 0.0) + jnp.where(y0 == -1.0, fy, 0.0)
        tr = lambda a: a.transpose(0, 2, 1, 3)

        def gather(idx):
            idxc = jnp.clip(idx, 0, L - 1).reshape(B, H, L * P, 1)
            return jnp.take_along_axis(v, idxc, axis=2).reshape(B, H, L, P, Dh)
        val0 = gather(tr(x0i))
        val1 = gather(tr(x1i))
        wx0 = tr((1.0 - fx) * m0 * hy)
        wx1 = tr(fx * m1 * hy)
        sampled = val0 * wx0[..., None] + val1 * wx1[..., None]
        out = jnp.einsum('bhlpd,bhlp->blhd', sampled, tr(attw)).reshape(B, L, D)
        return out @ w_out + b_out

    def _L1_ffn_ref(x, w_gate, w_up, w_down):
        import jax, jax.numpy as jnp
        import numpy as np
        BLOCK = 32
        W_BITS = 4
        ACT_BITS = 16

        def act_qdq(x):
            qmax = 2.0 ** (ACT_BITS - 1) - 1.0
            scale = jnp.maximum(jnp.max(jnp.abs(x)) / qmax, 1e-12)
            return jnp.clip(jnp.round(x / scale), -qmax - 1.0, qmax) * scale

        def fixed_qdq_u16(x):
            scale = 1.0 / 65536.0
            return jnp.clip(jnp.round(x / scale), 0.0, 65535.0) * scale

        def lpbq_dequant(w):
            O, I = w.shape
            qmax = 2.0 ** (W_BITS - 1) - 1.0
            wb = w.reshape(O, I // BLOCK, BLOCK)
            s = jnp.maximum(jnp.max(jnp.abs(wb), axis=-1, keepdims=True) / qmax, 1e-12)
            wq = jnp.clip(jnp.round(wb / s), -qmax - 1.0, qmax) * s
            return wq.reshape(O, I)
        x = act_qdq(x)
        up = act_qdq(x @ lpbq_dequant(w_up).T)
        gate = act_qdq(x @ lpbq_dequant(w_gate).T)
        sig = fixed_qdq_u16(jax.nn.sigmoid(gate))
        gate = act_qdq(gate * sig)
        o = act_qdq(gate * up)
        return o @ lpbq_dequant(w_down).T
    x = x + _L0_xattn_ref(_layernorm(x, axis=-1), ctx_1024, ctx_1024, L0_xattn_Wq, L0_xattn_bq, L0_xattn_Wk, L0_xattn_bk, L0_xattn_Wv, L0_xattn_bv, L0_xattn_Wo, L0_xattn_bo)
    x = x + _L0_ffn_ref(_layernorm(x, axis=-1), L0_ffn_w_freq_real, L0_ffn_w_freq_imag, L0_ffn_bias)
    x = x + _L1_xattn_ref(_layernorm(x, axis=-1), ctx_1024, ctx_1024, L1_xattn_w_qk, L1_xattn_b_qk, L1_xattn_w_value, L1_xattn_b_value, L1_xattn_w_off, L1_xattn_b_off, L1_xattn_w_attw, L1_xattn_b_attw, L1_xattn_w_out, L1_xattn_b_out)
    x = x + _L1_ffn_ref(_layernorm(x, axis=-1), L1_ffn_w_gate, L1_ffn_w_up, L1_ffn_w_down)
    return x

_drawn_inputs = setup_inputs


def setup_inputs(seed=0):
    import zlib

    import numpy as np

    out = dict(_drawn_inputs(seed))
    spreads = {'L1_xattn_b_qk': (0.0, 0.1),
     'L1_xattn_b_value': (0.0, 0.432),
     'L1_xattn_b_attw': (0.0, 0.8),
     'L1_xattn_b_out': (0.0, 0.1)}
    factors = {'L0_xattn_bq': 8.0,
     'L0_xattn_bk': 8.0,
     'L0_xattn_bv': 8.0,
     'L0_xattn_bo': 2.693,
     'L0_ffn_bias': 6.238,
     'L1_xattn_w_off': 3.045,
     'L1_xattn_b_off': 3.019,
     'L1_xattn_w_attw': 8.0}
    for name, (base, spread) in spreads.items():
        noise = np.random.default_rng([zlib.crc32(name.encode()), seed]).standard_normal(out[name].shape)
        drawn = base * np.exp(spread * noise) if base else spread * noise
        out[name] = jnp.asarray(drawn.astype(out[name].dtype))
    for name, factor in factors.items():
        out[name] = (out[name] * factor).astype(out[name].dtype)
    return out
```

```python
from contextlib import ExitStack

import numpy as np

import concourse.bass as bass
from concourse import mybir

F32 = mybir.dt.float32
BF16 = mybir.dt.bfloat16
I16 = mybir.dt.int16
U32 = mybir.dt.uint32
ALU = mybir.AluOpType
ACT = mybir.ActivationFunctionType
AX = mybir.AxisListType

B, L, D = 32, 128, 256
H, DH = 16, 16
DC = D // 128
NP = 4
TOPK = 4
I = 768
IC = I // 128
WBLK = 32
QUAD = 4
NQ = B // QUAD
GRP = 8
HP = H * NP
UNITS = 8
JH = L // 2
LN_EPS = 1e-5
MAGIC = 1.5 * 2.0 ** 23
QMAX = 32767.0
WMAX = 7.0


def constants():
    t = np.arange(L)
    f = np.arange(L // 2)
    w = 2 * np.pi * np.outer(t, f) / L
    fwd = np.zeros((L, L))
    fwd[:, :64] = np.cos(w)
    fwd[:, 64] = np.cos(np.pi * t)
    fwd[:, 65:] = np.sin(w[:, 1:])
    swp = np.concatenate([fwd[:, 64:], fwd[:, :64]], 1)
    cos2, sin2 = 2 * np.cos(w).T, 2 * np.sin(w).T
    cos2[0] = 1
    nyq = np.cos(np.pi * t)
    ma = np.concatenate([cos2, nyq[None], cos2[1:]]) / (L * DH)
    mb = np.concatenate([-sin2, np.zeros((1, L)), sin2[1:]]) / (L * DH)
    ia = np.concatenate([cos2, nyq[None], -cos2[1:]]) / L
    ib = np.concatenate([sin2, np.zeros((1, L)), sin2[1:]]) / L
    big = np.stack([fwd, swp, ma, mb, ia, ib, np.eye(L)], 1).astype(np.float32)

    n = np.arange(D)
    a = 2 * np.pi * (np.outer(n, n) % D) / D
    four = np.stack([np.cos(a), np.sin(a), -np.sin(a), np.cos(a) / D, -np.sin(a) / D])
    four = four.reshape(5, DC, 128, D).transpose(2, 0, 1, 3).astype(np.float32)

    small = np.zeros((12, 4, 128), np.float32)
    small[0:3, 0, 0] = L
    small[0:3, 1, :] = 1
    j = 64 + np.arange(JH)
    for g in range(2):
        cols = slice(g * JH, (g + 1) * JH)
        small[(g * 2) * 3:(g * 2) * 3 + 3, 2, cols] = 1
        small[(g * 2 + 1) * 3:(g * 2 + 1) * 3 + 3, 2, cols] = 1 - j
        small[(g * 2) * 3:(g * 2) * 3 + 3, 3, cols] = -1
        small[(g * 2 + 1) * 3:(g * 2 + 1) * 3 + 3, 3, cols] = 1 + j

    mask = np.zeros((QUAD, H, D + QUAD), np.float32)
    for h in range(H):
        mask[:, h, h * DH:(h + 1) * DH] = 1
    for b in range(QUAD):
        mask[b, :, D + b] = 1
    mask = mask.reshape(QUAD * H, D + QUAD)

    col = np.zeros((128, 129), np.float32)
    col[:, 0] = np.linspace(0.0, 1.0, L)
    col[:, 1:] = np.arange(128)
    return {"c_big": big, "c_four": four, "c_small": small, "c_mask": mask, "c_col": col}


BIASES = [("bq", D), ("bk", D), ("bv", D), ("bo", D), ("bf", D), ("bout", D), ("bval", D),
          ("boff", 2 * HP), ("batt", HP)]
NBIAS = sum(n for _, n in BIASES)
BAT = {}
_o = 0
for _n, _w in BIASES:
    BAT[_n] = _o
    _o += _w


def staggered(engine, n, steps):
    lag = max(k for k, _ in steps)
    head = lag + 2 + (lag % 2)
    turns = max(0, (n - head) // 2)

    def tick(t, parity, peeled):
        for k, step in steps:
            if not peeled or 0 <= t - k < n:
                step(t - k, (parity - k) % 2)

    for t in range(head):
        tick(t, t % 2, True)
    if turns:
        with engine.Fori(0, turns) as i:
            for u in range(2):
                tick(i * 2 + (head + u), u, False)
    for t in range(head + 2 * turns, n + lag):
        tick(t, t % 2, True)


def late(b, k):
    return not isinstance(b, int) or b >= k


def at(b, n=1):
    return bass.ds(b, n) if not isinstance(b, int) else slice(b, b + n)


def build(nc, x, ctx_in, wq, wk, wv, wo, bq, bk, bv, bo, wfr, wfi, bf, wval, bval, woff, boff,
          watt, batt, wout, bout, wgate, wup, wdown, c_big, c_four, c_small, c_mask, c_col, out):
    xr = x.rearrange("b l d -> l b d")
    cr = ctx_in.rearrange("b l d -> l b d")
    outr = out.rearrange("b l d -> l b d")
    with ExitStack() as ctx:
        def sem(name):
            return ctx.enter_context(nc.semaphore(name))

        def sb(name, shape, dt=F32, scope=ctx):
            return scope.enter_context(nc.sbuf_tensor(name, shape, dt))

        bank = [ctx.enter_context(nc.psum_tensor(f"bank{i}", [128, 512], F32)) for i in range(8)]

        big = sb("big", [128, 7, 128])
        FWD, SWP, MA, MB, IA, IB, IDN = (big[:, i, :] for i in range(7))
        stats = sb("stats", [128, B, 6])
        lnt = sb("lnt", [128, 5, B])
        rstd, nmr = sb("rstd", [128, B]), sb("nmr", [128, B])
        half = sb("half", [128, B])
        sampling = ExitStack()
        down_a = sb("down_a", [128, 2, QUAD * L], F32, sampling)
        sampling.close()
        xn = sb("xn", [128, 2, D])
        tr_sb = sb("tr_sb", [128, 2, DC, 128])
        peak = sb("peak", [128, 5, 64])
        unit = sb("unit", [128, 8, 8])
        wgT = sb("wgT", [128, DC, I])
        wuT = sb("wuT", [128, DC, I])
        wdT = sb("wdT", [128, IC, D])

        ffn = ExitStack()
        x_place = ExitStack()
        x_sb = sb("x_sb", [128, B, D], F32, x_place)
        x_place.close()
        up16 = sb("up16", [128, IC, B * L], I16, ffn)
        wide = sb("wide", [128, IC, B * L], F32, ffn)
        xnorm = ExitStack()
        xqT = sb("xqT", [128, DC, B * L], I16, xnorm)
        xqs = sb("xqs", [128, 2, DC, QUAD * L], F32, xnorm)
        xnorm.close()
        sig = sb("sig", [128, 2, IC, 256], F32, ffn)
        hid = sb("hid", [128, 4, IC, 128], F32, ffn)
        ffn.close()

        x_again = sb("x_again", [128, B, D])
        small_f = sb("small_f", [12, 4, 128])
        small = sb("small", [12, 4, 128], BF16)
        dc3, ones3 = small[0:3, 0, :], small[0:3, 1, :]
        selP, selM = small[:, 2, :], small[:, 3, :]
        mask = sb("mask", [QUAD * H, D + QUAD])
        col = sb("col", [128, 129])
        refy, iota = col[:, 0:1], col[:, 1:129]
        bias3 = sb("bias3", [3, NBIAS], BF16)
        after0 = ExitStack()
        vz = sb("vz", [128, 2, QUAD, D], F32, after0)
        attT = sb("attT", [128, DC, QUAD * L], F32, after0)
        after0.close()
        wT = sb("wT", [128, 4, DC, D])
        fold = sb("fold", [128, DC, D])
        wl1 = sb("wl1", [128, DC, 3 * HP])
        wval_sb = sb("wval_sb", [128, DC, D])
        wout_sb = sb("wout_sb", [128, DC, D])

        lay0 = ExitStack()
        c_sb = sb("c_sb", [128, B, D], F32, lay0)
        split = ExitStack()
        brow = sb("brow", [1, NBIAS], F32, split)
        bres = sb("bres", [1, NBIAS], F32, split)
        bpart = sb("bpart", [1, 3, NBIAS], BF16, split)
        split.close()
        vhat = sb("vhat", [128, B, D], F32, lay0)
        cst = sb("cst", [128, 2, D], F32, lay0)
        fold_place = ExitStack()
        pqT = sb("pqT", [128, 2, DC, D], F32, fold_place)
        fold_place.close()
        ft_sb = sb("ft_sb", [128, 2, 4, 128], F32, lay0)
        q_sb = sb("q_sb", [128, 2, D], F32, lay0)
        ab = sb("ab", [128, 2, 2, D], F32, lay0)
        deq = sb("deq", [128, 3, I * D // 128], F32, lay0)
        dsc = sb("dsc", [128, 3, 3, I * D // 128 // WBLK], F32, lay0)
        setup = ExitStack()
        wnat = sb("wnat", [128, 4, DC, D], F32, setup)
        fnat = sb("fnat", [128, 2, DC, D], F32, setup)
        four = sb("four", [128, 5, DC, D], F32, setup)
        onat = sb("onat", [128, DC, 2 * HP], F32, setup)
        setup.close()
        sab = sb("sab", [128, 2, B * H], F32, lay0)
        corr = sb("corr", [128, 4, L], F32, lay0)
        top8 = sb("top8", [128, 4, 8], F32, lay0)
        idx8 = sb("idx8", [128, 4, 8], U32, lay0)
        idxf = sb("idxf", [128, 4, TOPK], F32, lay0)
        w4 = sb("w4", [128, 4, TOPK], F32, lay0)
        z4 = sb("z4", [128, 2, 4], F32, lay0)
        hot = sb("hot", [128, TOPK, L], F32, lay0)
        wrow = sb("wrow", [128, 4, L], F32, lay0)
        wcol = sb("wcol", [128, 4 * L], F32, lay0)
        what = sb("what", [128, 2, B * H], F32, lay0)
        oT = sb("oT", [128, 2, DC, 128], F32, lay0)
        lay0.close()

        lay1 = ExitStack()
        ctx_place = ExitStack()
        parts_sb = sb("parts_sb", [128, NQ, 3, QUAD * L], BF16, ctx_place)
        resid = sb("resid", [128, QUAD * L], F32, ctx_place)
        v63m = sb("v63m", [QUAD * H, D], F32, ctx_place)
        w63m = sb("w63m", [QUAD * H, QUAD, L], F32, ctx_place)
        ctx_place.close()
        sb("ctx_keep", [128, B, D], F32, lay1)
        v_sb = sb("v_sb", [128, B, D], F32, lay1)
        v63 = sb("v63", [QUAD * H, NQ, D], F32, lay1)
        w63T = sb("w63T", [QUAD * H, NQ, L], F32, lay1)
        weigh = ExitStack()
        turn = ExitStack()
        cdup = sb("cdup", [128, 2, DC, 128], F32, turn)
        cst1 = sb("cst1", [128, 2, D], F32, turn)
        turn.close()
        ccx = sb("ccx", [128, GRP, 2 * HP], F32, weigh)
        ctx63 = sb("ctx63", [128, DC, B * H], F32, weigh)
        off = sb("off", [128, B, 3 * HP], F32, weigh)
        tx, ty, te, tc, td = (sb(n, [128, GRP, HP], F32, weigh) for n in ("tx", "ty", "te", "tc", "td"))
        ts = sb("ts", [128, 3, GRP * H], F32, weigh)
        w63 = sb("w63", [128, GRP * H], F32, weigh)
        weigh.close()
        sample = ExitStack()
        rows = sb("rows", [12, 2, 16, QUAD * L], BF16, sample)
        hat = sb("hat", [128, 4, QUAD * L], F32, sample)
        down_b = sb("down_b", [128, 2, QUAD * L], F32, sample)
        down = [down_a[:, 0, :], down_a[:, 1, :], down_b[:, 0, :], down_b[:, 1, :]]
        sample.close()
        lay1.close()

        load_c, load_x = sem("load_c"), [sem(f"load_x{i}") for i in range(8)]
        load_w, load_ctx, load_b = sem("load_w"), [sem(f"load_ctx{i}") for i in range(8)], sem("load_b")
        load_f = sem("load_f")
        half_set = sem("half_set")
        small_cast, bias_split, bias_placed = sem("small_cast"), sem("bias_split"), sem("bias_placed")
        wt_done, wt_copied = sem("wt_done"), sem("wt_copied")
        fold_mm, fold_copied = sem("fold_mm"), sem("fold_copied")
        l1_laid = sem("l1_laid")
        bn_done, ln_step, pow_done, ln_ready = sem("bn_done"), sem("ln_step"), sem("pow_done"), sem("ln_ready")
        ctx_staged = sem("ctx_staged")
        xn_ready, ft_done, ft_copied = sem("xn_ready"), sem("ft_done"), sem("ft_copied")
        proj_done, q_copied, v_copied = sem("proj_done"), sem("q_copied"), sem("v_copied")
        prod_done, sab_done = sem("prod_done"), sem("sab_done")
        corr_done, corr_copied, dve_b = sem("corr_done"), sem("corr_copied"), sem("dve_b")
        d4_ready, exp4_done, wrow_done = sem("d4_ready"), sem("exp4_done"), sem("wrow_done")
        wtr_done, wcol_done, what_mm, what_done = sem("wtr_done"), sem("wcol_done"), sem("what_mm"), sem("what_done")
        pa_done, pb_done, inv_done, oT_copied = sem("pa_done"), sem("pb_done"), sem("inv_done"), sem("oT_copied")
        wo_done, x1_done = sem("wo_done"), sem("x1_done")
        xn2_ready, tr2_done, tr2_copied, mm2_done, x2_done = (
            sem("xn2_ready"), sem("tr2_done"), sem("tr2_copied"), sem("mm2_done"), sem("x2_done"))
        stored = sem("stored")
        load_g, deq_step, gw_turned, gw_kept = sem("load_g"), sem("deq_step"), sem("gw_turned"), sem("gw_kept")
        spilled, reloaded = sem("spilled"), sem("reloaded")
        xn4_done, xpeak, xq_ready, xq_turned, xq_kept = (
            sem("xn4_done"), sem("xpeak"), sem("xq_ready"), sem("xq_turned"), sem("xq_kept"))
        peak_col, peak_all, unit_step = sem("peak_col"), sem("peak_all"), sem("unit_step")
        xqs_ready, hid_mm, hid_kept, hid_peak = sem("xqs_ready"), sem("hid_mm"), sem("hid_kept"), sem("hid_peak")
        up_round, up_kept = sem("up_round"), sem("up_kept")
        g_round, g_whole, sig_done, sig_round, sig_whole, g2_done, g2_peak = (
            sem("g_round"), sem("g_whole"), sem("sig_done"), sem("sig_round"), sem("sig_whole"), sem("g2_done"), sem("g2_peak"))
        g2_round, o_done, o_peak = sem("g2_round"), sem("o_done"), sem("o_peak")
        o_round, o_whole, down_out, y_done = sem("o_round"), sem("o_whole"), sem("down_out"), sem("y_done")
        spill = nc.dram_tensor("x_spill", (B, L, D), F32, kind="Internal").ap().rearrange("b l d -> l b d")
        ctx1_staged, xn3_ready, tr3_done, tr3_copied = sem("ctx1_staged"), sem("xn3_ready"), sem("tr3_done"), sem("tr3_copied")
        mm3_done, v_kept, off_kept = sem("mm3_done"), sem("v_kept"), sem("off_kept")
        v63_mm, v63_kept = sem("v63_mm"), sem("v63_kept")
        wstep, logit_ready, exp_done = sem("wstep"), sem("logit_ready"), sem("exp_done")
        ccx_ready, w63_ready = sem("ccx_ready"), sem("w63_ready")
        ccx_turned, w63_turned, hi_done, res_done, mid_done, lo_done, w63_kept = (
            sem("ccx_turned"), sem("w63_turned"), sem("hi_done"), sem("res_done"), sem("mid_done"), sem("lo_done"), sem("w63_kept"))
        rows_loaded = [sem("rows_loaded0"), sem("rows_loaded1")]
        edge_ready, edge_used = sem("edge_ready"), sem("edge_used")
        down_mm, up_mm, down_done, hat_done, taken = (
            sem("down_mm"), sem("up_mm"), sem("down_done"), sem("hat_done"), sem("taken"))
        attT_copied, out_mm, x3_done, vz_clear, vz_ready = (
            sem("attT_copied"), sem("out_mm"), sem("x3_done"), sem("vz_clear"), sem("vz_ready"))

        def at_seq(b):
            return bass.ds(b * L, L) if not isinstance(b, int) else slice(b * L, (b + 1) * L)

        def at_tokens(t):
            return bass.ds(t * QUAD * L, QUAD * L) if not isinstance(t, int) else slice(t * QUAD * L, (t + 1) * QUAD * L)

        def at_piece(t):
            return bass.ds(t * 256, 256) if not isinstance(t, int) else slice(t * 256, (t + 1) * 256)

        def xnorm_sb(b):
            first = (IC * B * L - B * D) + b * D
            return wide[:].rearrange("p c t -> p (c t)")[:, slice(first, first + D) if isinstance(b, int) else bass.ds(first, D)]

        block = ctx.enter_context(nc.Block())
        XL = B // 8

        @block.sync
        def _(sp):
            for i in range(8):
                sp.dma_start(x_sb[:, i * XL:(i + 1) * XL, :], xr[:, i * XL:(i + 1) * XL, :]).then_inc(load_x[i], 16)
            for i in range(8):
                sp.dma_start(c_sb[:, i * XL:(i + 1) * XL, :], cr[:, i * XL:(i + 1) * XL, :]).then_inc(load_ctx[i], 16)
            def load_rows(q, hh):
                if late(q, 1):
                    sp.wait_ge(up_mm, (q - 1) * 32 + 16 * hh + 16)
                for g in range(2):
                    for k in range(2):
                        r = (g * 2 + k) * 3
                        p = k * HP + hh * 32 + g
                        for part in range(3):
                            sp.dma_start(rows[r + part:r + part + 1, hh, :, :],
                                         parts_sb[p:p + 31:2, at(q), part, :]).then_inc(rows_loaded[hh], 16)

            sp.wait_ge(lo_done, NQ)
            sp.wait_ge(off_kept, B)
            sp.wait_ge(w63_turned, B // GRP)
            load_rows(0, 0)
            load_rows(0, 1)
            with sp.Fori(1, NQ) as q:
                load_rows(q, 0)
                load_rows(q, 1)
            sp.wait_ge(x3_done, 2 * NQ)
            sp.dma_start(spill, x_sb[:]).then_inc(spilled, 16)
            sp.wait_ge(spilled, 16)
            sp.wait_ge(o_done, 2 * NQ)
            for i in range(8):
                sp.dma_start(x_sb[:, i * XL:(i + 1) * XL, :], spill[:, i * XL:(i + 1) * XL, :]).then_inc(reloaded, 16)
            for i in range(8):
                sp.wait_ge(y_done, (i + 1) * XL)
                sp.dma_start(outr[:, i * XL:(i + 1) * XL, :], x_sb[:, i * XL:(i + 1) * XL, :]).then_inc(stored, 16)
            sp.wait_ge(stored, 16 * 8)

        @block.gpsimd
        def _(pool):
            nc.gpsimd.memset(half[:], -0.5).then_inc(half_set, 1)
            pool.wait_ge(load_b, 16 * len(BIASES))
            parts = [bpart[:, k, :] for k in range(3)]
            nc.gpsimd.tensor_copy(parts[0], brow[:]).then_inc(bias_split, 1)
            pool.wait_ge(bias_split, 1)
            nc.gpsimd.tensor_tensor(bres[:], brow[:], parts[0], ALU.subtract).then_inc(bias_split, 1)
            pool.wait_ge(bias_split, 2)
            nc.gpsimd.tensor_copy(parts[1], bres[:]).then_inc(bias_split, 1)
            pool.wait_ge(bias_split, 3)
            nc.gpsimd.tensor_tensor(parts[2], bres[:], parts[1], ALU.subtract).then_inc(bias_split, 1)
            pool.wait_ge(bias_split, 4)
            pool.dma_start(bias3[:], bpart[:]).then_inc(bias_placed, 16)

            def rstd_pow(n):
                pool.wait_ge(ln_step, 6 * n)
                pool.wait_ge(half_set, 1)
                nc.gpsimd.tensor_tensor(rstd[:], lnt[:, 4, :], half[:], ALU.pow).then_inc(pow_done, 1)

            rstd_pow(1)

            pool.wait_ge(load_w, 16 * 8)
            ov = onat[:].rearrange("p c (n k) -> p c k n", k=2)
            nc.gpsimd.tensor_copy(wl1[:, :, 0:HP], ov[:, :, 0, :]).then_inc(l1_laid, 1)
            nc.gpsimd.tensor_copy(wl1[:, :, HP:2 * HP], ov[:, :, 1, :]).then_inc(l1_laid, 1)

            def stage_ctx(b, s):
                if isinstance(b, int):
                    pool.wait_ge(load_ctx[b // XL], 16)
                if late(b, 2):
                    pool.wait_ge(ft_done, b - 1)
                nc.gpsimd.tensor_copy(cst[:, s, :], c_sb[:, at(b), :]).then_inc(ctx_staged, 1)

            for i in range(8):
                pool.wait_ge(load_ctx[i], 16)
            staggered(pool, B, [(0, stage_ctx)])

            def product_b(b, s):
                if late(b, 2):
                    pool.wait_ge(inv_done, b - 1)
                nc.gpsimd.tensor_tensor(
                    ab[:, s, 1, :].rearrange("p (h d) -> p h d", h=H),
                    vhat[:, at(b), :].rearrange("p o (h d) -> p (o h) d", h=H),
                    what[:, 1, at(b * H, H)].unsqueeze(2).broadcast_to([128, H, DH]),
                    ALU.mult).then_inc(pb_done, 1)

            pool.wait_ge(what_done, 2)
            staggered(pool, B, [(0, product_b)])
            rstd_pow(2)
            rstd_pow(3)

            def stage_ctx1(b, s):
                if late(b, 2):
                    pool.wait_ge(tr3_done, b - 1)
                nc.gpsimd.tensor_copy(cst1[:, s, :], c_sb[:, at(b), :]).then_inc(ctx1_staged, 1)

            pool.wait_ge(wo_done, B)
            nc.gpsimd.memset(vz[:], 0.0).then_inc(vz_clear, 1)
            staggered(pool, B, [(0, stage_ctx1)])

            with pool.Fori(0, NQ) as q:
                pool.wait_ge(mid_done, q + 1)
                nc.gpsimd.tensor_tensor(parts_sb[:, at(q), 2, :], resid[:], parts_sb[:, at(q), 1, :], ALU.subtract).then_inc(lo_done, 1)

            pool.wait_ge(v63_kept, NQ)
            pool.wait_ge(w63_kept, NQ)
            pool.wait_ge(lo_done, NQ)
            pool.wait_ge(v_kept, B)
            pool.wait_ge(vz_clear, 1)

            def part_heads(q, c):
                if late(q, 1):
                    pool.wait_ge(taken, (q - 1) * 2 * UNITS + (c + 1) * UNITS)
                for r in range(2):
                    def heads(a):
                        return a[:, :, c * 128:(c + 1) * 128].rearrange("p b (m r d) -> p b m r d", r=2, d=DH)[:, :, :, r, :]
                    nc.gpsimd.tensor_copy(heads(vz[:, r]), heads(v_sb[:, at(q * QUAD, QUAD), :])).then_inc(vz_ready, 1)

            def edge(q):
                part_heads(q, 0)
                if late(q, 1):
                    pool.wait_ge(edge_used, 2 * q)
                nc.gpsimd.tensor_tensor(v63m[:], v63[:, at(q), :].rearrange("p o d -> p (o d)"), mask[:, 0:D], ALU.mult).then_inc(edge_ready, 1)
                nc.gpsimd.tensor_tensor(w63m[:], w63T[:, at(q), :].broadcast_to([QUAD * H, QUAD, L]),
                                        mask[:, D:].unsqueeze(2).broadcast_to([QUAD * H, QUAD, L]), ALU.mult).then_inc(edge_ready, 1)
                part_heads(q, 1)

            edge(0)
            with pool.Fori(1, NQ) as q:
                edge(q)

            rstd_pow(4)

            def all_peak(n):
                pool.wait_ge(peak_col, n + 1)
                nc.gpsimd.partition_all_reduce(unit[:, n, 1:2], unit[:, n, 0:1], 128, bass.bass_isa.ReduceOp.max).then_inc(peak_all, 1)

            def widen(t, s):
                if late(t, 2):
                    pool.wait_ge(hid_mm, (t - 1) * IC)
                nc.gpsimd.tensor_copy(xqs[:, s], xqT[:, :, at_tokens(t % NQ if isinstance(t, int) else t)]).then_inc(xqs_ready, 1)

            all_peak(0)
            pool.wait_ge(xq_kept, B)
            for t in range(NQ):
                widen(t, t % 2)
            all_peak(1)
            for t in range(NQ, 2 * NQ):
                widen(t, t % 2)
            for n in range(2, 5):
                all_peak(n)

        @block.scalar
        def _(act):
            act.dma_start(big[:], c_big).then_inc(load_c, 16)
            act.dma_start(small_f[:], c_small).then_inc(load_c, 16)
            act.dma_start(col[:], c_col).then_inc(load_c, 16)
            act.dma_start(mask[:], c_mask).then_inc(load_c, 16)
            for i, w in enumerate((wq, wk, wv, wo)):
                act.dma_start(wnat[:, i], w.rearrange("(c p) d -> p c d", p=128)).then_inc(load_w, 16)
            for name, src in (("bq", bq), ("bk", bk), ("bv", bv), ("bo", bo), ("bf", bf), ("bval", bval), ("bout", bout)):
                act.dma_start(brow[:, BAT[name]:BAT[name] + D], src.rearrange("(a n) -> a n", a=1)).then_inc(load_b, 16)
            act.dma_start(brow[:, BAT["boff"]:BAT["boff"] + 2 * HP].rearrange("a (k n) -> a k n", k=2),
                          boff.rearrange("(a n k) -> a k n", a=1, k=2),
                          allow_slow_non_contiguous=True).then_inc(load_b, 16)
            act.dma_start(brow[:, BAT["batt"]:BAT["batt"] + HP], batt.rearrange("(a n) -> a n", a=1)).then_inc(load_b, 16)
            act.dma_start(onat[:], woff.rearrange("(c p) n -> p c n", p=128)).then_inc(load_w, 16)
            act.dma_start(wl1[:, :, 2 * HP:], watt.rearrange("(c p) n -> p c n", p=128)).then_inc(load_w, 16)
            act.dma_start(wval_sb[:], wval.rearrange("(c p) n -> p c n", p=128)).then_inc(load_w, 16)
            act.dma_start(wout_sb[:], wout.rearrange("(c p) n -> p c n", p=128)).then_inc(load_w, 16)
            act.dma_start(four[:], c_four).then_inc(load_f, 16)
            act.dma_start(fnat[:, 0], wfr.rearrange("(c p) n -> p c n", p=128)).then_inc(load_f, 16)
            act.dma_start(fnat[:, 1], wfi.rearrange("(c p) n -> p c n", p=128)).then_inc(load_f, 16)

            act.dma_start(deq[:, 0].rearrange("p (c d) -> p c d", d=D), wgate.rearrange("(c p) d -> p c d", p=128)).then_inc(load_g, 16)
            act.dma_start(deq[:, 1].rearrange("p (c d) -> p c d", d=D), wup.rearrange("(c p) d -> p c d", p=128)).then_inc(load_g, 16)
            act.dma_start(deq[:, 2].rearrange("p (c d) -> p c d", d=I), wdown.rearrange("(c p) d -> p c d", p=128)).then_inc(load_g, 16)

            for i in range(4):
                act.wait_ge(wt_done, i + 1)
                nc.scalar.activation(wT[:, i], bank[i][:].rearrange("p (c o) -> p c o", c=DC), ACT.Copy).then_inc(wt_copied, 1)
            for i in range(2):
                act.wait_ge(fold_mm, i + 1)
                nc.scalar.activation(pqT[:, i], bank[4 + i][:].rearrange("p (c o) -> p c o", c=DC), ACT.Copy).then_inc(fold_copied, 1)
            act.wait_ge(fold_mm, 3)
            nc.scalar.activation(fold[:], bank[6][:].rearrange("p (c o) -> p c o", c=DC), ACT.Copy).then_inc(fold_copied, 1)

            def copy_ft(b, s):
                act.wait_ge(ft_done, b + 1)
                if late(b, 2):
                    act.wait_ge(proj_done, b - 1)
                nc.scalar.activation(ft_sb[:, s].rearrange("p c t -> p (c t)"), bank[s][:], ACT.Copy).then_inc(ft_copied, 1)

            def copy_qv(b, s):
                act.wait_ge(proj_done, b + 1)
                if late(b, 2):
                    act.wait_ge(prod_done, b - 1)
                nc.scalar.activation(q_sb[:, s, :], bank[2 + s][:, 0:D], ACT.Copy).then_inc(q_copied, 1)
                nc.scalar.activation(vhat[:, at(b), :].rearrange("p o d -> p (o d)"), bank[4 + s][:, 0:D], ACT.Copy).then_inc(v_copied, 1)

            staggered(act, B, [(0, copy_ft), (1, copy_qv)])

            for i in range(9):
                act.wait_ge(gw_turned, i + 1)
                nc.scalar.activation((wgT, wuT, wdT)[i // 3][:].rearrange("p c o -> p (c o)")[:, (i % 3) * 512:(i % 3 + 1) * 512],
                                     bank[6 + i % 2][:], ACT.Copy).then_inc(gw_kept, 1)

            act.wait_ge(d4_ready, 1)
            nc.scalar.activation(w4[:], w4[:], ACT.Exp).then_inc(exp4_done, 1)
            act.wait_ge(wtr_done, 1)
            nc.scalar.activation(wcol[:], bank[1][:], ACT.Copy).then_inc(wcol_done, 1)
            for i in range(2):
                act.wait_ge(what_mm, i + 1)
                nc.scalar.activation(what[:, i, :], bank[2 + i][:], ACT.Copy).then_inc(what_done, 1)

            def copy_oT(b, s):
                act.wait_ge(inv_done, b + 1)
                if late(b, 2):
                    act.wait_ge(wo_done, b - 1)
                nc.scalar.activation(oT[:, s].rearrange("p c t -> p (c t)"), bank[4 + s][:, 0:D], ACT.Copy).then_inc(oT_copied, 1)

            staggered(act, B, [(0, copy_oT)])

            def copy_tr2(b, s):
                act.wait_ge(tr2_done, b + 1)
                if late(b, 2):
                    act.wait_ge(mm2_done, b - 1)
                nc.scalar.activation(tr_sb[:, s].rearrange("p c t -> p (c t)"), bank[s][:, 0:D], ACT.Copy).then_inc(tr2_copied, 1)

            staggered(act, B, [(0, copy_tr2)])

            def copy_tr3(b, s):
                act.wait_ge(tr3_done, b + 1)
                if late(b, 2):
                    act.wait_ge(mm3_done, b - 1)
                nc.scalar.activation(tr_sb[:, s].rearrange("p c t -> p (c t)"), bank[s][:, 0:D], ACT.Copy).then_inc(tr3_copied, 1)
                cT = bank[s][:, D:].rearrange("p (c t) -> p c t", c=DC)
                nc.scalar.activation(cdup[:, s].rearrange("p c (g j) -> p c g j", g=2),
                                     cT[:, :, JH:].unsqueeze(2).broadcast_to([128, DC, 2, JH]), ACT.Copy).then_inc(tr3_copied, 1)
                nc.scalar.activation(ctx63[:, :, at(b * H, H)], cT[:, :, JH - 1:JH].broadcast_to([128, DC, H]), ACT.Copy).then_inc(tr3_copied, 1)

            def keep_v(b, s):
                act.wait_ge(mm3_done, b + 1)
                nc.scalar.activation(v_sb[:, at(b), :].rearrange("p o d -> p (o d)"), bank[2 + s][:, 0:D], ACT.Copy).then_inc(v_kept, 1)

            staggered(act, B, [(0, copy_tr3), (1, keep_v)])
            for q in range(NQ):
                act.wait_ge(v63_mm, q + 1)
                nc.scalar.activation(v63[:, q, :], bank[4 + q % 2][0:QUAD * H, 0:D], ACT.Copy).then_inc(v63_kept, 1)

            with act.Fori(0, B // GRP) as g:
                act.wait_ge(logit_ready, g + 1)
                nc.scalar.activation(te[:], te[:], ACT.Exp).then_inc(exp_done, 1)
                for u in range(2):
                    q = g * 2 + u
                    act.wait_ge(ccx_turned, q + 1)
                    nc.scalar.activation(parts_sb[:, at(q), 0, :].rearrange("p o t -> p (o t)"), bank[u][:], ACT.Copy).then_inc(hi_done, 1)
                    act.wait_ge(res_done, q + 1)
                    nc.scalar.activation(parts_sb[:, at(q), 1, :].rearrange("p o t -> p (o t)"), resid[:], ACT.Copy).then_inc(mid_done, 1)
                act.wait_ge(w63_turned, g + 1)
                for u in range(2):
                    nc.scalar.activation(w63T[:, at(g * 2 + u), :].rearrange("p o t -> p (o t)"),
                                         bank[2][u * QUAD * H:(u + 1) * QUAD * H, 0:L], ACT.Copy).then_inc(w63_kept, 1)

            def sample_act(q):
                for c in range(DC):
                    for u in range(UNITS):
                        for i in range(2):
                            n = (q * DC + c) * 2 * UNITS + 2 * u + i
                            act.wait_ge(down_mm, n + 1)
                            if c or u >= 2 or late(q, 1):
                                act.wait_ge(hat_done, n - 3)
                            nc.scalar.activation(down[(u % 2) * 2 + i], bank[2 + i][:], ACT.Relu).then_inc(down_done, 1)
                        if u == 1 and c == 1:
                            keep_attT(q, 0)
                        if u == 1 and c == 0 and late(q, 1):
                            keep_attT(q - 1, 1)

            def keep_attT(q, c):
                act.wait_ge(taken, (q * DC + c + 1) * UNITS)
                if c == 0 and late(q, 1):
                    act.wait_ge(out_mm, 2 * q)
                nc.scalar.activation(attT[:, c, :], bank[4 + c][:], ACT.Copy).then_inc(attT_copied, 1)

            sample_act(0)
            with act.Fori(1, NQ) as q:
                sample_act(q)
            keep_attT(NQ - 1, 1)

            def keep_xq(b, s):
                act.wait_ge(xq_turned, b + 1)
                nc.scalar.activation(xqT[:, :, at_seq(b)], bank[s][:, 0:D].rearrange("p (c t) -> p c t", c=DC),
                                     ACT.Copy, bias=-MAGIC).then_inc(xq_kept, 1)

            staggered(act, B, [(0, keep_xq)])

            act.wait_ge(xq_kept, B)

            def fresh_tokens(t):
                return bass.ds(act.snap(t * (QUAD * L)), QUAD * L)

            def keep_hidden(t, n0):
                if n0:
                    act.wait_ge(up_kept, t + 1)
                for oc in range(IC):
                    n = n0 + t * IC + oc
                    act.wait_ge(hid_mm, n + 1)
                    tokens = at_tokens(t) if oc else fresh_tokens(t)
                    nc.scalar.activation(wide[:, oc, tokens], bank[2 + oc][:], ACT.Copy).then_inc(hid_kept, 1)

            def keep_up(t):
                act.wait_ge(up_round, t + 1)
                nc.scalar.activation(up16[:, :, at_tokens(t)], wide[:, :, at_tokens(t)], ACT.Copy, bias=-MAGIC).then_inc(up_kept, 1)

            with act.Fori(0, NQ) as t:
                keep_hidden(t, 0)
            act.wait_ge(spilled, 16)
            with act.Fori(0, NQ) as t:
                keep_up(t)
                keep_hidden(t, NQ * IC)

            def whole_gate(t, s):
                act.wait_ge(g_round, t + 1)
                g = wide[:, :, at_piece(t)]
                nc.scalar.activation(g, g, ACT.Copy, bias=-MAGIC).then_inc(g_whole, 1)

            def sigmoid(t, s):
                act.wait_ge(g_whole, t + 1)
                if late(t, 2):
                    act.wait_ge(g2_done, t - 1)
                nc.scalar.activation(sig[:, s], wide[:, :, at_piece(t)], ACT.Sigmoid, scale=unit[:, 2, 2:3]).then_inc(sig_done, 1)

            def round_sigmoid(t, s):
                act.wait_ge(sig_done, t + 1)
                nc.scalar.activation(sig[:, s], sig[:, s], ACT.Copy, scale=65536.0, bias=MAGIC).then_inc(sig_round, 1)

            staggered(act, 2 * NQ, [(0, whole_gate), (3, round_sigmoid), (2, sigmoid)])

            def round_g2(t, s):
                g = wide[:, :, at_piece(t)]
                nc.scalar.activation(g, g, ACT.Identity, scale=unit[:, 3, 3:4], bias=unit[:, 7, 0:1]).then_inc(g2_round, 1)

            act.wait_ge(unit_step, 1 + 4 * 5)
            staggered(act, 2 * NQ, [(0, round_g2)])

            def round_o(b, s):
                if late(b, 2):
                    act.wait_ge(o_whole, b - 1)
                nc.scalar.activation(hid[:, 2 + s], wide[:, :, at_seq(b)], ACT.Identity, scale=unit[:, 4, 3:4], bias=unit[:, 7, 0:1]).then_inc(o_round, 1)

            act.wait_ge(unit_step, 1 + 5 * 5)
            staggered(act, B, [(0, round_o)])

        @block.tensor
        def _(pe):
            mm = nc.tensor.matmul

            pe.wait_ge(load_c, 64)
            pe.wait_ge(load_w, 16 * 8)
            for i in range(4):
                for oc in range(DC):
                    for dc in range(DC):
                        last = nc.tensor.transpose(bank[i][:, dc * D + oc * 128:dc * D + oc * 128 + 128],
                                                   wnat[:, i, oc, dc * 128:(dc + 1) * 128], IDN)
                last.then_inc(wt_done, 1)
            pe.wait_ge(load_f, 48)
            C_, S_, NS_, CD, NSD = (four[:, k] for k in range(5))
            wr, wi = fnat[:, 0], fnat[:, 1]
            for i, terms in enumerate((((wr, C_), (wi, S_)), ((wi, C_), (wr, NS_)))):
                for kc in range(DC):
                    for n, (w, m) in enumerate(terms):
                        for c in range(DC):
                            last = mm(bank[4 + i][:, kc * D:(kc + 1) * D], w[:, c, kc * 128:(kc + 1) * 128], m[:, c, :],
                                      start=(n == 0 and c == 0), stop=(n == 1 and c == DC - 1))
                last.then_inc(fold_mm, 1)
            pe.wait_ge(fold_copied, 2)
            for ncn in range(DC):
                for i, m in enumerate((CD, NSD)):
                    for c in range(DC):
                        last = mm(bank[6][:, ncn * D:(ncn + 1) * D], pqT[:, i, c, ncn * 128:(ncn + 1) * 128], m[:, c, :],
                                  start=(i == 0 and c == 0), stop=(i == 1 and c == DC - 1))
            last.then_inc(fold_mm, 1)
            pe.wait_ge(wt_copied, 4)
            pe.wait_ge(fold_copied, 3)
            pe.wait_ge(small_cast, 1)
            pe.wait_ge(bias_placed, 16)

            def transform(b, s):
                pe.wait_ge(xn_ready, b + 1)
                pe.wait_ge(ctx_staged, b + 1)
                if late(b, 2):
                    pe.wait_ge(ft_copied, b - 1)
                for c in range(DC):
                    mm(bank[s][:, c * 128:(c + 1) * 128], xn[:, s, c * 128:(c + 1) * 128], FWD, start=True, stop=True)
                for c in range(DC):
                    last = mm(bank[s][:, D + c * 128:D + (c + 1) * 128], cst[:, s, c * 128:(c + 1) * 128], FWD,
                              start=True, stop=True)
                last.then_inc(ft_done, 1)

            def project(b, s):
                pe.wait_ge(ft_copied, b + 1)
                if late(b, 2):
                    pe.wait_ge(prod_done, b - 1)
                    pe.wait_ge(v_copied, b - 1)
                mm(bank[2 + s][:], dc3, bias3[:, BAT["bq"]:BAT["bq"] + 2 * D], start=True, stop=False)
                for i in range(2):
                    for c in range(DC):
                        mm(bank[2 + s][:, i * D:(i + 1) * D], ft_sb[:, s, i * DC + c, :], wT[:, i, c, :],
                           start=False, stop=(i == 1 and c == DC - 1))
                mm(bank[4 + s][:, 0:D], dc3, bias3[:, BAT["bv"]:BAT["bv"] + D], start=True, stop=False)
                for c in range(DC):
                    last = mm(bank[4 + s][:, 0:D], ft_sb[:, s, DC + c, :], wT[:, 2, c, :], start=False, stop=(c == DC - 1))
                last.then_inc(proj_done, 1)

            staggered(pe, B, [(0, transform), (1, project)])

            pe.wait_ge(deq_step, 7 * 3)
            blocks = ([(w, c, oc, D) for w in range(2) for c in range(DC) for oc in range(IC)]
                      + [(2, ic, oc, I) for ic in range(IC) for oc in range(DC)])
            for i in range(9):
                if i >= 2:
                    pe.wait_ge(gw_kept, i - 1)
                for k in range(4):
                    w, c, oc, width = blocks[i * 4 + k]
                    last = nc.tensor.transpose(bank[6 + i % 2][:, k * 128:(k + 1) * 128],
                                               deq[:, w, oc * width + c * 128:oc * width + (c + 1) * 128], IDN)
                last.then_inc(gw_turned, 1)

            pe.wait_ge(sab_done, B)
            for k in range(4):
                mm(bank[0][:, k * L:(k + 1) * L], sab[:, 0, k * 128:(k + 1) * 128], MA, start=True, stop=False)
                last = mm(bank[0][:, k * L:(k + 1) * L], sab[:, 1, k * 128:(k + 1) * 128], MB, start=False, stop=True)
            last.then_inc(corr_done, 1)
            pe.wait_ge(wrow_done, 4)
            for k in range(4):
                last = nc.tensor.transpose(bank[1][:, k * 128:(k + 1) * 128], wrow[:, k, :], IDN)
            last.then_inc(wtr_done, 1)
            pe.wait_ge(wcol_done, 1)
            for i, m in enumerate((FWD, SWP)):
                mm(bank[2 + i][:], m, wcol[:], start=True, stop=True).then_inc(what_mm, 1)

            def inverse(b, s):
                pe.wait_ge(pa_done, b + 1)
                pe.wait_ge(pb_done, b + 1)
                if late(b, 2):
                    pe.wait_ge(oT_copied, b - 1)
                for c in range(DC):
                    mm(bank[4 + s][:, c * 128:(c + 1) * 128], ab[:, s, 0, c * 128:(c + 1) * 128], IA, start=True, stop=False)
                    last = mm(bank[4 + s][:, c * 128:(c + 1) * 128], ab[:, s, 1, c * 128:(c + 1) * 128], IB, start=False, stop=True)
                last.then_inc(inv_done, 1)

            def project_out(b, s):
                pe.wait_ge(oT_copied, b + 1)
                if late(b, 2):
                    pe.wait_ge(x1_done, b - 1)
                mm(bank[6 + s][:, 0:D], ones3, bias3[:, BAT["bo"]:BAT["bo"] + D], start=True, stop=False)
                for c in range(DC):
                    last = mm(bank[6 + s][:, 0:D], oT[:, s, c, :], wT[:, 3, c, :], start=False, stop=(c == DC - 1))
                last.then_inc(wo_done, 1)

            staggered(pe, B, [(0, inverse), (1, project_out)])

            def turn2(b, s):
                pe.wait_ge(xn2_ready, b + 1)
                if late(b, 2):
                    pe.wait_ge(tr2_copied, b - 1)
                for c in range(DC):
                    last = nc.tensor.transpose(bank[s][:, c * 128:(c + 1) * 128], xn[:, s, c * 128:(c + 1) * 128], IDN)
                last.then_inc(tr2_done, 1)

            def frequency_ffn(b, s):
                pe.wait_ge(tr2_copied, b + 1)
                if late(b, 2):
                    pe.wait_ge(x2_done, b - 1)
                mm(bank[2 + s][:, 0:D], ones3, bias3[:, BAT["bf"]:BAT["bf"] + D], start=True, stop=False)
                for c in range(DC):
                    last = mm(bank[2 + s][:, 0:D], tr_sb[:, s, c, :], fold[:, c, :], start=False, stop=(c == DC - 1))
                last.then_inc(mm2_done, 1)

            staggered(pe, B, [(0, turn2), (1, frequency_ffn)])

            def turn3(b, s):
                pe.wait_ge(xn3_ready, b + 1)
                pe.wait_ge(ctx1_staged, b + 1)
                if late(b, 2):
                    pe.wait_ge(tr3_copied, 3 * (b - 1))
                for i, src in enumerate((xn, cst1)):
                    for c in range(DC):
                        last = nc.tensor.transpose(bank[s][:, i * D + c * 128:i * D + (c + 1) * 128],
                                                   src[:, s, c * 128:(c + 1) * 128], IDN)
                last.then_inc(tr3_done, 1)

            def project3(b, s):
                pe.wait_ge(tr3_copied, 3 * (b + 1))
                if late(b, 2):
                    pe.wait_ge(v_kept, b - 1)
                    pe.wait_ge(off_kept, b - 1)
                mm(bank[2 + s][:, 0:D + 3 * HP], ones3, bias3[:, BAT["bval"]:BAT["bval"] + D + 3 * HP], start=True, stop=False)
                for c in range(DC):
                    mm(bank[2 + s][:, 0:D], cdup[:, s, c, :], wval_sb[:, c, :], start=False, stop=False)
                for c in range(DC):
                    last = mm(bank[2 + s][:, D:D + 3 * HP], tr_sb[:, s, c, :], wl1[:, c, :], start=False, stop=(c == DC - 1))
                last.then_inc(mm3_done, 1)

            pe.wait_ge(l1_laid, 2)
            staggered(pe, B, [(0, turn3), (1, project3)])
            for q in range(NQ):
                if q >= 2:
                    pe.wait_ge(v63_kept, q - 1)
                o = bank[4 + q % 2][0:QUAD * H, 0:D]
                mm(o, ones3[:, 0:QUAD * H], bias3[:, BAT["bval"]:BAT["bval"] + D], start=True, stop=False)
                for c in range(DC):
                    last = mm(o, ctx63[:, c, q * QUAD * H:(q + 1) * QUAD * H], wval_sb[:, c, :], start=False, stop=(c == DC - 1))
                last.then_inc(v63_mm, 1)

            pe.wait_ge(off_kept, B)

            def turn_points(g):
                pe.wait_ge(ccx_ready, g + 1)
                for u in range(2):
                    if late(g, 1):
                        pe.wait_ge(res_done, g * 2)
                    for b in range(QUAD):
                        last = nc.tensor.transpose(bank[u][:, b * 128:(b + 1) * 128], ccx[:, u * QUAD + b, :], IDN)
                    last.then_inc(ccx_turned, 1)
                pe.wait_ge(w63_ready, g + 1)
                if late(g, 1):
                    pe.wait_ge(w63_kept, g * 2)
                nc.tensor.transpose(bank[2][:, 0:L], w63[:], IDN).then_inc(w63_turned, 1)

            turn_points(0)
            with pe.Fori(1, B // GRP) as g:
                turn_points(g)

            def of_unit(u, i):
                m, r, pp = 2 * (u % 2) + i, u // 4, (u // 2) % 2
                return m, r, (2 * m + r) * 2 + pp

            def sides(q, c, u):
                for i in range(2):
                    n = (q * DC + c) * 2 * UNITS + 2 * u + i
                    row = rows[:, c, of_unit(u, i)[2], :]
                    if c or u or late(q, 1):
                        pe.wait_ge(down_done, n - 1)
                    mm(bank[2 + i][:], selM, row, start=True, stop=True).then_inc(down_mm, 1)
                    if c or u or late(q, 1):
                        pe.wait_ge(hat_done, n - 1)
                    mm(bank[i][:], selP, row, start=True, stop=True).then_inc(up_mm, 1)

            def take(q, c, u):
                pe.wait_ge(hat_done, (q * DC + c) * 2 * UNITS + 2 * u + 2)
                for b in range(QUAD):
                    for i in range(2):
                        m, r, _ = of_unit(u, i)
                        w = c * 128 + 32 * m
                        last = mm(bank[4 + c][32 * m:32 * m + 32, b * 128:(b + 1) * 128], vz[:, r, b, w:w + 32],
                                  hat[:, (u % 2) * 2 + i, b * 128:(b + 1) * 128],
                                  start=False, stop=(u >= UNITS - 2 and b == QUAD - 1), skip_group_check=True)
                last.then_inc(taken, 1)

            def project_att(q):
                pe.wait_ge(attT_copied, 2 * q + 2)
                if late(q, 1):
                    pe.wait_ge(x3_done, 2 * q)
                for i in range(2):
                    mm(bank[6 + i][:].rearrange("p (b d) -> p b d", b=2), ones3,
                       bias3[:, BAT["bout"]:BAT["bout"] + D].unsqueeze(1).broadcast_to([3, 2, D]), start=True, stop=False)
                    for b in range(2):
                        for c in range(DC):
                            last = mm(bank[6 + i][:, b * D:(b + 1) * D], attT[:, c, (2 * i + b) * L:(2 * i + b + 1) * L], wout_sb[:, c, :],
                                      start=False, stop=(b == 1 and c == DC - 1))
                    last.then_inc(out_mm, 1)

            def sample_pe(q):
                for c in range(DC):
                    if c == 0:
                        pe.wait_ge(rows_loaded[0], 192 * (q + 1))
                        sides(q, 0, 0)
                        pe.wait_ge(edge_ready, 2 * q + 2)
                    if late(q, 1):
                        pe.wait_ge(attT_copied, 2 * (q - 1) + c + 1)
                    mm(bank[4 + c][:], v63m[:, c * 128:(c + 1) * 128], w63m[:].rearrange("p b t -> p (b t)"),
                       start=True, stop=True).then_inc(edge_used, 1)
                    for u in range(UNITS):
                        if u + 1 < UNITS:
                            sides(q, c, u + 1)
                        elif c == 0:
                            pe.wait_ge(rows_loaded[1], 192 * (q + 1))
                            sides(q, 1, 0)
                        if u % 4 == 0:
                            pe.wait_ge(vz_ready, 4 * q + 2 * c + u // 4 + 1)
                        take(q, c, u)
                        if c == 0 and u == 4 and late(q, 1):
                            project_att(q - 1)

            pe.wait_ge(v63_kept, NQ)
            pe.wait_ge(w63_kept, NQ)
            pe.wait_ge(res_done, NQ)
            pe.wait_ge(v_kept, B)
            sample_pe(0)
            with pe.Fori(1, NQ) as q:
                sample_pe(q)
            project_att(NQ - 1)

            pe.wait_ge(attT_copied, 2 * NQ)

            def turn_xq(b, s):
                pe.wait_ge(xq_ready, b + 1)
                if late(b, 2):
                    pe.wait_ge(xq_kept, b - 1)
                for c in range(DC):
                    last = nc.tensor.transpose(bank[s][:, c * 128:(c + 1) * 128], xn[:, s, c * 128:(c + 1) * 128], IDN)
                last.then_inc(xq_turned, 1)

            staggered(pe, B, [(0, turn_xq)])

            def hidden(t, s, w):
                pe.wait_ge(xqs_ready, t + 1)
                for oc in range(IC):
                    if late(t, 1):
                        pe.wait_ge(hid_kept, (t - 1) * IC + oc + 1)
                    for c in range(DC):
                        last = mm(bank[2 + oc][:], w[:, c, oc * 128:(oc + 1) * 128], xqs[:, s, c, :], start=(c == 0), stop=(c == DC - 1))
                    last.then_inc(hid_mm, 1)

            for t in range(2):
                hidden(t, t, wuT)
            with pe.Fori(1, NQ // 2) as i:
                for u in range(2):
                    hidden(i * 2 + u, u, wuT)
            with pe.Fori(NQ // 2, NQ) as i:
                for u in range(2):
                    hidden(i * 2 + u, u, wgT)

            def down_product(b, s):
                pe.wait_ge(o_whole, b + 1)
                if late(b, 2):
                    pe.wait_ge(y_done, b - 1)
                for ic in range(IC):
                    last = mm(bank[s][:, 0:D], hid[:, s, ic, :], wdT[:, ic, :], start=(ic == 0), stop=(ic == IC - 1))
                last.then_inc(down_out, 1)

            pe.wait_ge(hid_kept, 2 * NQ * IC)
            staggered(pe, B, [(0, down_product)])

        @block.vector
        def _(dve):
            V = nc.vector

            def moments(b):
                V.bn_stats(stats[:, at(b), :].rearrange("p o s -> p (o s)"), x_sb[:, at(b), :].rearrange("p o d -> p (o d)")).then_inc(bn_done, 1)

            def ln_finish(n):
                me, ve, mo, vo = (stats[:, :, k] for k in (1, 2, 4, 5))
                dve.wait_ge(bn_done, B * n)
                k = 6 * (n - 1)
                V.tensor_tensor(lnt[:, 0, :], me, mo, ALU.add).then_inc(ln_step, 1)
                V.tensor_tensor(lnt[:, 1, :], me, mo, ALU.subtract).then_inc(ln_step, 1)
                V.tensor_tensor(lnt[:, 2, :], ve, vo, ALU.add).then_inc(ln_step, 1)
                dve.wait_ge(ln_step, k + 2)
                V.scalar_tensor_tensor(lnt[:, 3, :], lnt[:, 1, :], 0.25, lnt[:, 1, :], ALU.mult, ALU.mult).then_inc(ln_step, 1)
                dve.wait_ge(ln_step, k + 4)
                V.scalar_tensor_tensor(lnt[:, 2, :], lnt[:, 2, :], 1.0 / D, lnt[:, 3, :], ALU.mult, ALU.add).then_inc(ln_step, 1)
                dve.wait_ge(ln_step, k + 5)
                V.tensor_scalar(lnt[:, 4, :], lnt[:, 2, :], LN_EPS, None, ALU.add).then_inc(ln_step, 1)
                dve.wait_ge(pow_done, n)
                V.scalar_tensor_tensor(nmr[:], lnt[:, 0, :], -0.5, rstd[:], ALU.mult, ALU.mult).then_inc(ln_ready, 1)
                dve.wait_ge(ln_ready, n)

            def normalise(b, s, ready):
                V.tensor_scalar(xn[:, s, :], x_sb[:, at(b), :].rearrange("p o d -> p (o d)"), rstd[:, at(b)], nmr[:, at(b)],
                                ALU.mult, ALU.add).then_inc(ready, 1)

            for b in range(B):
                if b % XL == 0:
                    dve.wait_ge(load_x[b // XL], 16)
                moments(b)
            ln_finish(1)
            dve.wait_ge(load_c, 64)
            V.tensor_copy(small[:], small_f[:]).then_inc(small_cast, 1)

            dve.wait_ge(load_g, 48)
            ws = [deq[:, w].rearrange("p (n k) -> p n k", k=WBLK) for w in range(3)]
            NB_ = I * D // 128 // WBLK

            def spread(a):
                return a.unsqueeze(2).broadcast_to([128, NB_, WBLK])

            for w in range(3):
                V.tensor_reduce(dsc[:, w, 0, :], ws[w], AX.X, ALU.max, apply_absolute_value=True).then_inc(deq_step, 1)
            for w in range(3):
                dve.wait_ge(deq_step, w + 1)
                V.tensor_scalar(dsc[:, w, 1, :], dsc[:, w, 0, :], 1.0 / WMAX, 1e-12, ALU.mult, ALU.max).then_inc(deq_step, 1)
            for w in range(3):
                dve.wait_ge(deq_step, 3 + w + 1)
                V.reciprocal(dsc[:, w, 2, :], dsc[:, w, 1, :]).then_inc(deq_step, 1)
            for w in range(3):
                dve.wait_ge(deq_step, 6 + w + 1)
                V.tensor_tensor(ws[w], ws[w], spread(dsc[:, w, 2, :]), ALU.mult).then_inc(deq_step, 1)
            for w in range(3):
                dve.wait_ge(deq_step, 9 + w + 1)
                V.tensor_scalar(ws[w], ws[w], MAGIC, MAGIC, ALU.add, ALU.subtract).then_inc(deq_step, 1)
            for w in range(3):
                dve.wait_ge(deq_step, 12 + w + 1)
                V.tensor_scalar(ws[w], ws[w], WMAX, -WMAX - 1.0, ALU.min, ALU.max).then_inc(deq_step, 1)
            for w in range(3):
                dve.wait_ge(deq_step, 15 + w + 1)
                V.tensor_tensor(ws[w], ws[w], spread(dsc[:, w, 1, :]), ALU.mult).then_inc(deq_step, 1)

            def norm0(b, s):
                if late(b, 2):
                    dve.wait_ge(ft_done, b - 1)
                normalise(b, s, xn_ready)

            def products(b, s):
                dve.wait_ge(q_copied, b + 1)
                if late(b, 2):
                    dve.wait_ge(sab_done, b - 1)
                q, k = q_sb[:, s, :], bank[2 + s][:, D:2 * D]
                V.tensor_tensor(ab[:, s, 0, :], q, k, ALU.mult)
                V.tensor_tensor(ab[0:64, s, 1, :], q[0:64], k[64:128], ALU.mult)
                V.tensor_tensor(ab[64:128, s, 1, :], q[64:128], k[0:64], ALU.mult).then_inc(prod_done, 1)

            def head_sums(b, s):
                dve.wait_ge(prod_done, b + 1)
                V.tensor_reduce(sab[:, :, at(b * H, H)], ab[:, s].rearrange("p a (h d) -> p a h d", h=H), AX.X, ALU.add).then_inc(sab_done, 1)

            staggered(dve, B, [(0, norm0), (2, products), (3, head_sums)])

            dve.wait_ge(corr_done, 1)
            V.tensor_copy(corr[:], bank[0][:].rearrange("p (k t) -> p k t", k=4)).then_inc(dve_b, 1)
            dve.wait_ge(dve_b, 1)
            for k in range(4):
                V.max(top8[:, k, :], corr[:, k, :]).then_inc(dve_b, 1)
            for k in range(4):
                dve.wait_ge(dve_b, 2 + k)
                V.max_index(idx8[:, k, :], top8[:, k, :], corr[:, k, :]).then_inc(dve_b, 1)
            V.tensor_tensor(w4[:], top8[:, :, 0:TOPK], top8[:, :, 0:1].broadcast_to([128, 4, TOPK]), ALU.subtract).then_inc(d4_ready, 1)
            dve.wait_ge(dve_b, 9)
            V.tensor_copy(idxf[:], idx8[:, :, 0:TOPK])
            dve.wait_ge(exp4_done, 1)
            V.tensor_reduce(z4[:, 0, :], w4[:], AX.X, ALU.add).then_inc(dve_b, 1)
            dve.wait_ge(dve_b, 10)
            V.reciprocal(z4[:, 1, :], z4[:, 0, :]).then_inc(dve_b, 1)
            dve.wait_ge(dve_b, 11)
            V.tensor_tensor(w4[:], w4[:], z4[:, 1, :].unsqueeze(2).broadcast_to([128, 4, TOPK]), ALU.mult).then_inc(dve_b, 1)
            for k in range(4):
                dve.wait_ge(dve_b, 12 + k)
                if k:
                    dve.wait_ge(wrow_done, k)
                for i in range(TOPK):
                    last = V.tensor_scalar(hot[:, i, :], iota, idxf[:, k, i:i + 1], w4[:, k, i:i + 1], ALU.is_equal, ALU.mult)
                last.then_inc(dve_b, 1)
                dve.wait_ge(dve_b, 13 + k)
                V.tensor_reduce(wrow[:, k, :], hot[:].rearrange("p i t -> p t i"), AX.X, ALU.add).then_inc(wrow_done, 1)

            def product_a(b, s):
                if late(b, 2):
                    dve.wait_ge(inv_done, b - 1)
                V.tensor_tensor(ab[:, s, 0, :].rearrange("p (h d) -> p h d", h=H),
                                vhat[:, at(b), :].rearrange("p o (h d) -> p (o h) d", h=H),
                                what[:, 0, at(b * H, H)].unsqueeze(2).broadcast_to([128, H, DH]),
                                ALU.mult).then_inc(pa_done, 1)

            def add_x(b, s, done, source, landed):
                dve.wait_ge(done, b + 1)
                xb = x_sb[:, at(b), :].rearrange("p o d -> p (o d)")
                V.tensor_tensor(xb, source[:, 0:D], xb, ALU.add).then_inc(landed, 1)

            def moments_of(landed):
                def step(b, s):
                    dve.wait_ge(landed, b + 1)
                    moments(b)
                return step

            dve.wait_ge(what_done, 2)
            dve.wait_ge(v_copied, B)
            staggered(dve, B, [(0, product_a), (2, lambda b, s: add_x(b, s, wo_done, bank[6 + s], x1_done)), (3, moments_of(x1_done))])
            ln_finish(2)

            def norm2(b, s):
                if late(b, 2):
                    dve.wait_ge(tr2_done, b - 1)
                normalise(b, s, xn2_ready)

            staggered(dve, B, [(0, norm2), (2, lambda b, s: add_x(b, s, mm2_done, bank[2 + s], x2_done)), (3, moments_of(x2_done))])
            ln_finish(3)

            def norm3(b, s):
                if late(b, 2):
                    dve.wait_ge(tr3_done, b - 1)
                normalise(b, s, xn3_ready)

            def keep_off(b, s):
                dve.wait_ge(mm3_done, b + 1)
                dve.wait_ge(v_kept, b + 1)
                V.tensor_copy(off[:, at(b), :].rearrange("p o n -> p (o n)"), bank[2 + s][:, D:D + 3 * HP]).then_inc(off_kept, 1)

            staggered(dve, B, [(0, norm3), (2, keep_off)])
            dve.wait_ge(off_kept, B)
            dve.wait_ge(mm3_done, B)

            NS = 13

            def sampling_weights(g):
                o = off[:, at(g * GRP, GRP), :]
                offx, offy, att = o[:, :, 0:HP], o[:, :, HP:2 * HP], o[:, :, 2 * HP:]
                att4 = att.rearrange("p b (h k) -> p b h k", k=NP)

                def heads(a):
                    return a.rearrange("p (b h) -> p b h", b=GRP).unsqueeze(3).broadcast_to([128, GRP, H, NP])

                def point(a):
                    return a.rearrange("p b (h k) -> p b h k", k=NP)

                def after(k):
                    if k or late(g, 1):
                        dve.wait_ge(wstep, g * NS + k)

                after(0)
                V.tensor_reduce(ts[:, 0, :].rearrange("p (b h) -> p b h", b=GRP), att4, AX.X, ALU.max).then_inc(wstep, 1)
                V.tensor_scalar(tx[:], offx, 0.0, 1.0, ALU.max, ALU.min).then_inc(wstep, 1)
                V.tensor_scalar(ty[:], offy, refy, 0.0, ALU.add, ALU.max).then_inc(wstep, 1)
                after(1)
                V.tensor_tensor(point(te[:]), att4, heads(ts[:, 0, :]), ALU.subtract).then_inc(logit_ready, 1)
                after(2)
                V.tensor_scalar(tx[:], tx[:], 1.0, L / 2.0, ALU.add, ALU.mult).then_inc(wstep, 1)
                after(3)
                V.tensor_scalar(ty[:], ty[:], 1.0, 1.0, ALU.min, ALU.add).then_inc(wstep, 1)
                after(4)
                V.tensor_scalar(tx[:], tx[:], 0.5, None, ALU.subtract).then_inc(wstep, 1)
                after(5)
                V.tensor_scalar(ty[:], ty[:], 1.0, -0.5, ALU.subtract, ALU.mult).then_inc(wstep, 1)
                after(6)
                V.tensor_scalar(td[:], tx[:], -1.0, JH * 1.0, ALU.mult, ALU.add).then_inc(wstep, 1)
                dve.wait_ge(exp_done, g + 1)
                V.tensor_reduce(ts[:, 1, :].rearrange("p (b h) -> p b h", b=GRP), point(te[:]), AX.X, ALU.add).then_inc(wstep, 1)
                after(9)
                V.reciprocal(ts[:, 2, :], ts[:, 1, :]).then_inc(wstep, 1)
                after(10)
                V.tensor_tensor(point(te[:]), point(te[:]), heads(ts[:, 2, :]), ALU.mult).then_inc(wstep, 1)
                after(11)
                if late(g, 1):
                    dve.wait_ge(ccx_turned, g * 2)
                V.scalar_tensor_tensor(ccx[:, :, HP:], ty[:], 1.0, te[:], ALU.add, ALU.mult).then_inc(wstep, 1)
                after(12)
                V.tensor_tensor(ccx[:, :, 0:HP], ccx[:, :, HP:], tx[:], ALU.mult).then_inc(ccx_ready, 1)
                V.scalar_tensor_tensor(tc[:], td[:], 0.0, ccx[:, :, HP:], ALU.max, ALU.mult).then_inc(wstep, 1)
                after(13)
                if late(g, 1):
                    dve.wait_ge(w63_turned, g)
                V.tensor_reduce(w63[:].rearrange("p (b h) -> p b h", b=GRP), point(tc[:]), AX.X, ALU.add).then_inc(w63_ready, 1)
                for u in range(2):
                    q = g * 2 + u
                    dve.wait_ge(hi_done, q + 1)
                    if u or late(g, 1):
                        dve.wait_ge(lo_done, q)
                    V.tensor_tensor(resid[:], bank[u][:], parts_sb[:, at(q), 0, :].rearrange("p o t -> p (o t)"), ALU.subtract).then_inc(res_done, 1)

            sampling_weights(0)
            with dve.Fori(1, B // GRP) as g:
                sampling_weights(g)

            def sample_dve(q):
                for c in range(DC):
                    for u in range(UNITS):
                        for i in range(2):
                            n = (q * DC + c) * 2 * UNITS + 2 * u + i
                            dve.wait_ge(up_mm, n + 1)
                            dve.wait_ge(down_done, n + 1)
                            if i == 0 and (c or u >= 2 or late(q, 1)):
                                dve.wait_ge(taken, (q * DC + c) * UNITS + u - 1)
                            k = (u % 2) * 2 + i
                            V.scalar_tensor_tensor(hat[:, k, :], bank[i][:], 0.0, down[k], ALU.max, ALU.min).then_inc(hat_done, 1)
                        if late(q, 1) and c == 0:
                            if u == 6:
                                add_out(q - 1)
                            if u == 7:
                                moments_out(q - 1)

            def add_out(q):
                for i in range(2):
                    dve.wait_ge(out_mm, 2 * q + i + 1)
                    xb = x_sb[:, at(q * QUAD + 2 * i, 2), :]
                    V.tensor_tensor(xb, bank[6 + i][:].rearrange("p (b d) -> p b d", b=2), xb, ALU.add).then_inc(x3_done, 1)

            def moments_out(q):
                dve.wait_ge(x3_done, 2 * q + 2)
                for b in range(QUAD):
                    moments(q * QUAD + b)

            sample_dve(0)
            with dve.Fori(1, NQ) as q:
                sample_dve(q)
            add_out(NQ - 1)
            moments_out(NQ - 1)

            ln_finish(4)
            V.memset(unit[:, 5:8, :], 1.0).then_inc(unit_step, 1)
            dve.wait_ge(unit_step, 1)
            V.memset(unit[:, 7, 0:1], MAGIC)

            def norm4(b, s):
                V.tensor_scalar(xnorm_sb(b), x_sb[:, at(b), :].rearrange("p o d -> p (o d)"), rstd[:, at(b)], nmr[:, at(b)],
                                ALU.mult, ALU.add).then_inc(xn4_done, 1)

            def peak4(b, s):
                dve.wait_ge(xn4_done, b + 1)
                V.tensor_reduce(peak[:, 0, at(b)], xnorm_sb(b), AX.X, ALU.max, apply_absolute_value=True).then_inc(xpeak, 1)

            staggered(dve, B, [(0, norm4), (1, peak4)])

            def make_unit(n, count):
                V.tensor_reduce(unit[:, n, 0:1], peak[:, n, 0:count], AX.X, ALU.max).then_inc(peak_col, 1)
                dve.wait_ge(peak_all, n + 1)
                raw = unit[:, 5, n:n + 1]
                k = n * 5 + 1
                V.tensor_tensor(unit[:, n, 4:5], unit[:, n, 1:2], raw, ALU.mult).then_inc(unit_step, 1)
                dve.wait_ge(unit_step, k + 1)
                V.tensor_scalar(unit[:, n, 2:3], unit[:, n, 4:5], 1.0 / QMAX, 1e-12, ALU.mult, ALU.max).then_inc(unit_step, 1)
                dve.wait_ge(unit_step, k + 2)
                V.reciprocal(unit[:, n, 5:6], unit[:, n, 2:3]).then_inc(unit_step, 1)
                dve.wait_ge(unit_step, k + 3)
                V.tensor_tensor(unit[:, n, 3:4], unit[:, n, 5:6], raw, ALU.mult).then_inc(unit_step, 1)
                if n == 0:
                    V.tensor_copy(unit[:, 5, 1:3], unit[:, 0, 2:3].broadcast_to([128, 2])).then_inc(unit_step, 1)
                elif n == 2:
                    V.tensor_scalar(unit[:, 5, 3:4], unit[:, 2, 2:3], 1.0 / 65536, None, ALU.mult).then_inc(unit_step, 1)
                elif n == 3:
                    V.tensor_tensor(unit[:, 5, 4:5], unit[:, 3, 2:3], unit[:, 1, 2:3], ALU.mult).then_inc(unit_step, 1)
                else:
                    V.tensor_copy(unit[:, 6, n:n + 1], unit[:, n, 2:3]).then_inc(unit_step, 1)
                dve.wait_ge(unit_step, k + 5)

            dve.wait_ge(xpeak, B)
            make_unit(0, B)

            def quantise_x(b, s):
                if late(b, 2):
                    dve.wait_ge(xq_turned, b - 1)
                V.tensor_scalar(xn[:, s, :], xnorm_sb(b), unit[:, 0, 3:4], MAGIC, ALU.mult, ALU.add).then_inc(xq_ready, 1)

            staggered(dve, B, [(0, quantise_x)])

            def peak_hidden(t, n):
                dve.wait_ge(hid_kept, ((n - 1) * NQ + t + 1) * IC)
                V.tensor_reduce(peak[:, n, at(t)], wide[:, :, at_tokens(t)], AX.XY, ALU.max, apply_absolute_value=True).then_inc(hid_peak, 1)

            with dve.Fori(0, NQ) as t:
                peak_hidden(t, 1)
            dve.wait_ge(hid_peak, NQ)
            make_unit(1, NQ)

            def round_up(t):
                g = wide[:, :, at_tokens(t)]
                V.tensor_scalar(g, g, unit[:, 1, 3:4], MAGIC, ALU.mult, ALU.add).then_inc(up_round, 1)

            round_up(0)
            with dve.Fori(1, NQ) as t:
                round_up(t)
                peak_hidden(t - 1, 2)
            peak_hidden(NQ - 1, 2)
            dve.wait_ge(hid_peak, 2 * NQ)
            make_unit(2, NQ)

            def round_gate(t, s):
                g = wide[:, :, at_piece(t)]
                V.tensor_scalar(g, g, unit[:, 2, 3:4], MAGIC, ALU.mult, ALU.add).then_inc(g_round, 1)

            def whole_sigmoid(t, s):
                dve.wait_ge(sig_round, t + 1)
                V.tensor_scalar(sig[:, s], sig[:, s], MAGIC, 65535.0, ALU.subtract, ALU.min).then_inc(sig_whole, 1)

            def gated(t, s):
                dve.wait_ge(sig_whole, t + 1)
                g = wide[:, :, at_piece(t)]
                V.scalar_tensor_tensor(g, sig[:, s], 0.0, g, ALU.max, ALU.mult).then_inc(g2_done, 1)

            def peak_gated(t, s):
                dve.wait_ge(g2_done, t + 1)
                V.tensor_reduce(peak[:, 3, at(t)], wide[:, :, at_piece(t)], AX.XY, ALU.max, apply_absolute_value=True).then_inc(g2_peak, 1)

            staggered(dve, 2 * NQ, [(0, round_gate), (5, gated), (4, whole_sigmoid), (6, peak_gated)])
            dve.wait_ge(g2_peak, 2 * NQ)
            make_unit(3, 2 * NQ)

            def hidden_product(t, s):
                dve.wait_ge(g2_round, t + 1)
                g = wide[:, :, at_piece(t)]
                V.scalar_tensor_tensor(g, g, MAGIC, up16[:, :, at_piece(t)], ALU.subtract, ALU.mult).then_inc(o_done, 1)

            def peak_product(t, s):
                dve.wait_ge(o_done, t + 1)
                V.tensor_reduce(peak[:, 4, at(t)], wide[:, :, at_piece(t)], AX.XY, ALU.max, apply_absolute_value=True).then_inc(o_peak, 1)

            staggered(dve, 2 * NQ, [(0, hidden_product), (1, peak_product)])
            dve.wait_ge(o_peak, 2 * NQ)
            make_unit(4, 2 * NQ)

            def whole_hidden(b, s):
                dve.wait_ge(o_round, b + 1)
                if late(b, 2):
                    dve.wait_ge(down_out, b - 1)
                V.tensor_scalar(hid[:, s], hid[:, 2 + s], MAGIC, None, ALU.subtract).then_inc(o_whole, 1)

            def add_y(b, s):
                dve.wait_ge(down_out, b + 1)
                xb = x_sb[:, at(b), :].rearrange("p o d -> p (o d)")
                V.scalar_tensor_tensor(xb, bank[s][:, 0:D], unit[:, 4, 2:3], xb, ALU.mult, ALU.add).then_inc(y_done, 1)

            dve.wait_ge(reloaded, 16 * 8)
            staggered(dve, B, [(0, whole_hidden), (2, add_y)])


_INS = ["x", "ctx_1024", "L0_xattn_Wq", "L0_xattn_Wk", "L0_xattn_Wv", "L0_xattn_Wo", "L0_xattn_bq", "L0_xattn_bk",
        "L0_xattn_bv", "L0_xattn_bo", "L0_ffn_w_freq_real", "L0_ffn_w_freq_imag", "L0_ffn_bias", "L1_xattn_w_value",
        "L1_xattn_b_value", "L1_xattn_w_off", "L1_xattn_b_off", "L1_xattn_w_attw", "L1_xattn_b_attw", "L1_xattn_w_out",
        "L1_xattn_b_out", "L1_ffn_w_gate", "L1_ffn_w_up", "L1_ffn_w_down"]


def kernel(**inputs):
    import concourse.bacc as _bacc
    from concourse.bass_utils import run_bass_kernel_spmd as _run

    nc = _bacc.Bacc("TRN2", target_bir_lowering=False, num_devices=1)
    arrays, args = {}, []
    named = [(n, np.ascontiguousarray(inputs[n])) for n in _INS] + list(constants().items())
    for name, a in named:
        arrays[f"in_{name}_dram"] = a
        args.append(nc.dram_tensor(f"in_{name}_dram", a.shape, mybir.dt.from_np(a.dtype), kind="ExternalInput").ap())
    args.append(nc.dram_tensor("out_0_dram", (B, L, D), F32, kind="ExternalOutput").ap())
    build(nc, *args)
    return _run(nc, [arrays], core_ids=[0]).results[0]["out_0_dram"]
```

```python
from contextlib import ExitStack

import numpy as np

import concourse.bass as bass
from concourse import mybir

F32 = mybir.dt.float32
BF16 = mybir.dt.bfloat16
I16 = mybir.dt.int16
U32 = mybir.dt.uint32
ALU = mybir.AluOpType
ACT = mybir.ActivationFunctionType
AX = mybir.AxisListType

B, L, D = 32, 128, 256
H, DH = 16, 16
DC = D // 128
NP = 4
TOPK = 4
I = 768
IC = I // 128
WBLK = 32
QUAD = 4
NQ = B // QUAD
GRP = 8
HP = H * NP
PT = 16
HB = HP // PT
ROWS = 3 * 2 * PT
UNITS = 8
JH = L // 2
LN_EPS = 1e-5
MAGIC = 1.5 * 2.0 ** 23
QMAX = 32767.0
WMAX = 7.0


def constants():
    t = np.arange(L)
    f = np.arange(L // 2)
    w = 2 * np.pi * np.outer(t, f) / L
    fwd = np.zeros((L, L))
    fwd[:, :64] = np.cos(w)
    fwd[:, 64] = np.cos(np.pi * t)
    fwd[:, 65:] = np.sin(w[:, 1:])
    swp = np.concatenate([fwd[:, 64:], fwd[:, :64]], 1)
    cos2, sin2 = 2 * np.cos(w).T, 2 * np.sin(w).T
    cos2[0] = 1
    nyq = np.cos(np.pi * t)
    ma = np.concatenate([cos2, nyq[None], cos2[1:]]) / (L * DH)
    mb = np.concatenate([-sin2, np.zeros((1, L)), sin2[1:]]) / (L * DH)
    ia = np.concatenate([cos2, nyq[None], -cos2[1:]]) / L
    ib = np.concatenate([sin2, np.zeros((1, L)), sin2[1:]]) / L
    big = np.stack([fwd, swp, ma, mb, ia, ib, np.eye(L)], 1).astype(np.float32)

    n = np.arange(D)
    a = 2 * np.pi * (np.outer(n, n) % D) / D
    four = np.stack([np.cos(a), np.sin(a), -np.sin(a), np.cos(a) / D, -np.sin(a) / D])
    four = four.reshape(5, DC, 128, D).transpose(2, 0, 1, 3).astype(np.float32)

    small = np.zeros((3, 2, 128), np.float32)
    small[:, 0, 0] = L
    small[:, 1, :] = 1

    sel = np.zeros((3, 2, PT, PT // 2, 2, 2, JH), np.float32)
    j = L - JH + np.arange(JH)
    for n in range(PT // 2):
        for g in range(2):
            sel[:, 0, 2 * n + g, n, 0, g] = 1
            sel[:, 1, 2 * n + g, n, 0, g] = 1 - j
            sel[:, 0, 2 * n + g, n, 1, g] = -1
            sel[:, 1, 2 * n + g, n, 1, g] = 1 + j
    sel = sel.reshape(ROWS, PT // 2, 2, 128)

    mask = np.zeros((QUAD, H, D + QUAD), np.float32)
    for h in range(H):
        mask[:, h, h * DH:(h + 1) * DH] = 1
    for b in range(QUAD):
        mask[b, :, D + b] = 1
    mask = mask.reshape(QUAD * H, D + QUAD)

    col = np.zeros((128, 129), np.float32)
    col[:, 0] = np.linspace(0.0, 1.0, L)
    col[:, 1:] = np.arange(128)
    return {"c_big": big, "c_four": four, "c_small": small, "c_sel": sel, "c_mask": mask, "c_col": col}


BIASES = [("bq", D), ("bk", D), ("bv", D), ("bo", D), ("bf", D), ("bout", D), ("bval", D),
          ("boff", 2 * HP), ("batt", HP)]
NBIAS = sum(n for _, n in BIASES)
BAT = {}
_o = 0
for _n, _w in BIASES:
    BAT[_n] = _o
    _o += _w


def staggered(engine, n, steps):
    lag = max(k for k, _ in steps)
    head = lag + 2 + (lag % 2)
    turns = max(0, (n - head) // 2)

    def tick(t, parity, peeled):
        for k, step in steps:
            if not peeled or 0 <= t - k < n:
                step(t - k, (parity - k) % 2)

    for t in range(head):
        tick(t, t % 2, True)
    if turns:
        with engine.Fori(0, turns) as i:
            for u in range(2):
                tick(i * 2 + (head + u), u, False)
    for t in range(head + 2 * turns, n + lag):
        tick(t, t % 2, True)


def late(b, k):
    return not isinstance(b, int) or b >= k


def at(b, n=1):
    return bass.ds(b, n) if not isinstance(b, int) else slice(b, b + n)


def build(nc, x, ctx_in, wq, wk, wv, wo, bq, bk, bv, bo, wfr, wfi, bf, wval, bval, woff, boff,
          watt, batt, wout, bout, wgate, wup, wdown, c_big, c_four, c_small, c_sel, c_mask, c_col, out):
    xr = x.rearrange("b l d -> l b d")
    cr = ctx_in.rearrange("b l d -> l b d")
    outr = out.rearrange("b l d -> l b d")
    with ExitStack() as ctx:
        def sem(name):
            return ctx.enter_context(nc.semaphore(name))

        def sb(name, shape, dt=F32, scope=ctx):
            return scope.enter_context(nc.sbuf_tensor(name, shape, dt))

        bank = [ctx.enter_context(nc.psum_tensor(f"bank{i}", [128, 512], F32)) for i in range(8)]

        big = sb("big", [128, 7, 128])
        FWD, SWP, MA, MB, IA, IB, IDN = (big[:, i, :] for i in range(7))
        stats = sb("stats", [128, B, 6])
        lnt = sb("lnt", [128, 5, B])
        rstd, nmr = sb("rstd", [128, B]), sb("nmr", [128, B])
        half = sb("half", [128, B])
        sampling = ExitStack()
        down_a = sb("down_a", [128, 2, QUAD * L], F32, sampling)
        sampling.close()
        edge_place = ExitStack()
        w63 = sb("w63", [128, B * H], F32, edge_place)
        edge_place.close()
        xn = sb("xn", [128, 2, D])
        tr_sb = sb("tr_sb", [128, 2, DC, 128])
        peak = sb("peak", [128, 5, 64])
        unit = sb("unit", [128, 8, 8])
        wgT = sb("wgT", [128, DC, I])
        wuT = sb("wuT", [128, DC, I])
        wdT = sb("wdT", [128, IC, D])

        ffn = ExitStack()
        x_place = ExitStack()
        x_sb = sb("x_sb", [128, B, D], F32, x_place)
        x_place.close()
        up16 = sb("up16", [128, IC, B * L], I16, ffn)
        wide = sb("wide", [128, IC, B * L], F32, ffn)
        xnorm = ExitStack()
        xqT = sb("xqT", [128, DC, B * L], I16, xnorm)
        xqs = sb("xqs", [128, 2, DC, QUAD * L], F32, xnorm)
        xnorm.close()
        sig = sb("sig", [128, 2, IC, 256], F32, ffn)
        hid = sb("hid", [128, 4, IC, 128], F32, ffn)
        ffn.close()

        x_again = sb("x_again", [128, B, D])
        small_f = sb("small_f", [3, 2, 128])
        small = sb("small", [3, 2, 128], BF16)
        dc3, ones3 = small[:, 0, :], small[:, 1, :]
        idn16 = sb("idn16", [128, 128], BF16)
        mask = sb("mask", [QUAD * H, D + QUAD])
        col = sb("col", [128, 129])
        refy, iota = col[:, 0:1], col[:, 1:129]
        bias3 = sb("bias3", [3, NBIAS], BF16)
        after0 = ExitStack()
        sel_place = ExitStack()
        sel_f = sb("sel_f", [ROWS, PT // 2, 2, 128], F32, sel_place)
        sel_place.close()
        parts_place = ExitStack()
        parts = sb("parts", [128, GRP * HB, 3, 2 * PT], BF16, parts_place)
        parts_place.close()
        vz = sb("vz", [128, 2, QUAD, D], F32, after0)
        attT = sb("attT", [128, DC, QUAD * L], F32, after0)
        after0.close()
        wT = sb("wT", [128, 4, DC, D])
        fold = sb("fold", [128, DC, D])
        wl1 = sb("wl1", [128, DC, 3 * HP])
        wval_sb = sb("wval_sb", [128, DC, D])
        wout_sb = sb("wout_sb", [128, DC, D])

        lay0 = ExitStack()
        c_sb = sb("c_sb", [128, B, D], F32, lay0)
        split = ExitStack()
        brow = sb("brow", [1, NBIAS], F32, split)
        bres = sb("bres", [1, NBIAS], F32, split)
        bpart = sb("bpart", [1, 3, NBIAS], BF16, split)
        split.close()
        vhat = sb("vhat", [128, B, D], F32, lay0)
        cst = sb("cst", [128, 2, D], F32, lay0)
        fold_place = ExitStack()
        pqT = sb("pqT", [128, 2, DC, D], F32, fold_place)
        fold_place.close()
        ft_sb = sb("ft_sb", [128, 2, 4, 128], F32, lay0)
        q_sb = sb("q_sb", [128, 2, D], F32, lay0)
        ab = sb("ab", [128, 2, 2, D], F32, lay0)
        deq = sb("deq", [128, 3, I * D // 128], F32, lay0)
        dsc = sb("dsc", [128, 3, 3, I * D // 128 // WBLK], F32, lay0)
        setup = ExitStack()
        wnat = sb("wnat", [128, 4, DC, D], F32, setup)
        fnat = sb("fnat", [128, 2, DC, D], F32, setup)
        four = sb("four", [128, 5, DC, D], F32, setup)
        onat = sb("onat", [128, DC, 2 * HP], F32, setup)
        setup.close()
        sab = sb("sab", [128, 2, B * H], F32, lay0)
        corr = sb("corr", [128, 4, L], F32, lay0)
        top8 = sb("top8", [128, 4, 8], F32, lay0)
        idx8 = sb("idx8", [128, 4, 8], U32, lay0)
        idxf = sb("idxf", [128, 4, TOPK], F32, lay0)
        w4 = sb("w4", [128, 4, TOPK], F32, lay0)
        z4 = sb("z4", [128, 2, 4], F32, lay0)
        hot = sb("hot", [128, TOPK, L], F32, lay0)
        wrow = sb("wrow", [128, 4, L], F32, lay0)
        wcol = sb("wcol", [128, 4 * L], F32, lay0)
        what = sb("what", [128, 2, B * H], F32, lay0)
        oT = sb("oT", [128, 2, DC, 128], F32, lay0)
        lay0.close()

        lay1 = ExitStack()
        ctx_place = ExitStack()
        rows = sb("rows", [ROWS, HB, NQ, QUAD * L], BF16, ctx_place)
        ctx_place.close()
        sb("ctx_keep", [128, B, D], F32, lay1)
        v_sb = sb("v_sb", [128, B, D], F32, lay1)
        v63 = sb("v63", [QUAD * H, NQ, D], F32, lay1)
        w63T = sb("w63T", [QUAD * H, NQ, L], F32, lay1)
        sel = sb("sel", [ROWS, PT // 2, 2, 128], BF16, lay1)
        weigh = ExitStack()
        turn = ExitStack()
        cdup = sb("cdup", [128, 2, DC, 128], F32, turn)
        cst1 = sb("cst1", [128, 2, D], F32, turn)
        turn.close()
        ccx = sb("ccx", [128, GRP, 2 * HP], F32, weigh)
        ctx63 = sb("ctx63", [128, DC, B * H], F32, weigh)
        off = sb("off", [128, B, 3 * HP], F32, weigh)
        tx, ty, te, tc, td = (sb(n, [128, GRP, HP], F32, weigh) for n in ("tx", "ty", "te", "tc", "td"))
        ts = sb("ts", [128, 3, GRP * H], F32, weigh)
        weigh.close()
        sample = ExitStack()
        v63m = sb("v63m", [QUAD * H, D], F32, sample)
        w63m = sb("w63m", [QUAD * H, QUAD, L], F32, sample)
        hat = sb("hat", [128, 4, QUAD * L], F32, sample)
        down_b = sb("down_b", [128, 2, QUAD * L], F32, sample)
        down = [down_a[:, 0, :], down_a[:, 1, :], down_b[:, 0, :], down_b[:, 1, :]]
        sample.close()
        lay1.close()

        load_c, load_x = sem("load_c"), [sem(f"load_x{i}") for i in range(8)]
        load_w, load_ctx, load_b = sem("load_w"), [sem(f"load_ctx{i}") for i in range(8)], sem("load_b")
        load_f = sem("load_f")
        half_set = sem("half_set")
        small_cast, bias_split, bias_placed = sem("small_cast"), sem("bias_split"), sem("bias_placed")
        wt_done, wt_copied = sem("wt_done"), sem("wt_copied")
        fold_mm, fold_copied = sem("fold_mm"), sem("fold_copied")
        l1_laid = sem("l1_laid")
        bn_done, ln_step, pow_done, ln_ready = sem("bn_done"), sem("ln_step"), sem("pow_done"), sem("ln_ready")
        ctx_staged = sem("ctx_staged")
        xn_ready, ft_done, ft_copied = sem("xn_ready"), sem("ft_done"), sem("ft_copied")
        proj_done, q_copied, v_copied = sem("proj_done"), sem("q_copied"), sem("v_copied")
        prod_done, sab_done = sem("prod_done"), sem("sab_done")
        corr_done, corr_copied, dve_b = sem("corr_done"), sem("corr_copied"), sem("dve_b")
        d4_ready, exp4_done, wrow_done = sem("d4_ready"), sem("exp4_done"), sem("wrow_done")
        wtr_done, wcol_done, what_mm, what_done = sem("wtr_done"), sem("wcol_done"), sem("what_mm"), sem("what_done")
        pa_done, pb_done, inv_done, oT_copied = sem("pa_done"), sem("pb_done"), sem("inv_done"), sem("oT_copied")
        wo_done, x1_done = sem("wo_done"), sem("x1_done")
        xn2_ready, tr2_done, tr2_copied, mm2_done, x2_done = (
            sem("xn2_ready"), sem("tr2_done"), sem("tr2_copied"), sem("mm2_done"), sem("x2_done"))
        stored = sem("stored")
        load_g, deq_step, gw_turned, gw_kept = sem("load_g"), sem("deq_step"), sem("gw_turned"), sem("gw_kept")
        spilled, reloaded = sem("spilled"), sem("reloaded")
        xn4_done, xpeak, xq_ready, xq_turned, xq_kept = (
            sem("xn4_done"), sem("xpeak"), sem("xq_ready"), sem("xq_turned"), sem("xq_kept"))
        peak_col, peak_all, unit_step = sem("peak_col"), sem("peak_all"), sem("unit_step")
        xqs_ready, hid_mm, hid_kept, hid_peak = sem("xqs_ready"), sem("hid_mm"), sem("hid_kept"), sem("hid_peak")
        up_round, up_kept = sem("up_round"), sem("up_kept")
        g_round, g_whole, sig_done, sig_round, sig_whole, g2_done, g2_peak = (
            sem("g_round"), sem("g_whole"), sem("sig_done"), sem("sig_round"), sem("sig_whole"), sem("g2_done"), sem("g2_peak"))
        g2_round, o_done, o_peak = sem("g2_round"), sem("o_done"), sem("o_peak")
        o_round, o_whole, down_out, y_done = sem("o_round"), sem("o_whole"), sem("down_out"), sem("y_done")
        spill = nc.dram_tensor("x_spill", (B, L, D), F32, kind="Internal").ap().rearrange("b l d -> l b d")
        ctx1_staged, xn3_ready, tr3_done, tr3_copied = sem("ctx1_staged"), sem("xn3_ready"), sem("tr3_done"), sem("tr3_copied")
        mm3_done, v_kept, off_kept = sem("mm3_done"), sem("v_kept"), sem("off_kept")
        v63_mm, v63_kept = sem("v63_mm"), sem("v63_kept")
        wstep, logit_ready, exp_done = sem("wstep"), sem("logit_ready"), sem("exp_done")
        ccx_ready, w63_ready = sem("ccx_ready"), sem("w63_ready")
        load_sel, sel_ready = sem("load_sel"), sem("sel_ready")
        parts_turned, w63_turned, hi_done, res_done, mid_done, lo_done, w63_kept = (
            sem("parts_turned"), sem("w63_turned"), sem("hi_done"), sem("res_done"), sem("mid_done"), sem("lo_done"), sem("w63_kept"))
        rows_kept = [sem("rows_kept_act"), sem("rows_kept_dve")]
        edge_ready, edge_used = sem("edge_ready"), sem("edge_used")
        down_mm, up_mm, down_done, hat_done, taken = (
            sem("down_mm"), sem("up_mm"), sem("down_done"), sem("hat_done"), sem("taken"))
        attT_copied, out_mm, x3_done, vz_clear, vz_ready = (
            sem("attT_copied"), sem("out_mm"), sem("x3_done"), sem("vz_clear"), sem("vz_ready"))

        def at_seq(b):
            return bass.ds(b * L, L) if not isinstance(b, int) else slice(b * L, (b + 1) * L)

        def at_tokens(t):
            return bass.ds(t * QUAD * L, QUAD * L) if not isinstance(t, int) else slice(t * QUAD * L, (t + 1) * QUAD * L)

        def at_piece(t):
            return bass.ds(t * 256, 256) if not isinstance(t, int) else slice(t * 256, (t + 1) * 256)

        def xnorm_sb(b):
            first = (IC * B * L - B * D) + b * D
            return wide[:].rearrange("p c t -> p (c t)")[:, slice(first, first + D) if isinstance(b, int) else bass.ds(first, D)]

        ccx_blocks = ccx[:].rearrange("p b (n k t) -> p (b n) k t", n=HB, k=2)
        ccx_rows = ccx[:].rearrange("p b (n r) -> p (b n) r", n=HB)

        def keep_rows(engine, g, u):
            engine.wait_ge(parts_turned, g * 2 + u + 1)
            for n in range(HB):
                out_rows = rows[:, n, at(g * 2 + u), :].rearrange("p o t -> p (o t)")
                if u == 0:
                    nc.scalar.activation(out_rows, bank[n][0:ROWS, :], ACT.Copy).then_inc(rows_kept[0], 1)
                else:
                    nc.vector.tensor_copy(out_rows, bank[HB + n][0:ROWS, :]).then_inc(rows_kept[1], 1)

        block = ctx.enter_context(nc.Block())
        XL = B // 8

        @block.sync
        def _(sp):
            for i in range(8):
                sp.dma_start(x_sb[:, i * XL:(i + 1) * XL, :], xr[:, i * XL:(i + 1) * XL, :]).then_inc(load_x[i], 16)
            for i in range(8):
                sp.dma_start(c_sb[:, i * XL:(i + 1) * XL, :], cr[:, i * XL:(i + 1) * XL, :]).then_inc(load_ctx[i], 16)
            sp.wait_ge(wo_done, B)
            sp.dma_start(sel_f[:], c_sel).then_inc(load_sel, 16)
            sp.wait_ge(x3_done, 2 * NQ)
            sp.dma_start(spill, x_sb[:]).then_inc(spilled, 16)
            sp.wait_ge(spilled, 16)
            sp.wait_ge(o_done, 2 * NQ)
            for i in range(8):
                sp.dma_start(x_sb[:, i * XL:(i + 1) * XL, :], spill[:, i * XL:(i + 1) * XL, :]).then_inc(reloaded, 16)
            for i in range(8):
                sp.wait_ge(y_done, (i + 1) * XL)
                sp.dma_start(outr[:, i * XL:(i + 1) * XL, :], x_sb[:, i * XL:(i + 1) * XL, :]).then_inc(stored, 16)
            sp.wait_ge(stored, 16 * 8)

        @block.gpsimd
        def _(pool):
            nc.gpsimd.memset(half[:], -0.5).then_inc(half_set, 1)
            pool.wait_ge(load_b, 16 * len(BIASES))
            split3 = [bpart[:, k, :] for k in range(3)]
            nc.gpsimd.tensor_copy(split3[0], brow[:]).then_inc(bias_split, 1)
            pool.wait_ge(bias_split, 1)
            nc.gpsimd.tensor_tensor(bres[:], brow[:], split3[0], ALU.subtract).then_inc(bias_split, 1)
            pool.wait_ge(bias_split, 2)
            nc.gpsimd.tensor_copy(split3[1], bres[:]).then_inc(bias_split, 1)
            pool.wait_ge(bias_split, 3)
            nc.gpsimd.tensor_tensor(split3[2], bres[:], split3[1], ALU.subtract).then_inc(bias_split, 1)
            pool.wait_ge(bias_split, 4)
            pool.dma_start(bias3[:], bpart[:]).then_inc(bias_placed, 16)

            def rstd_pow(n):
                pool.wait_ge(ln_step, 6 * n)
                pool.wait_ge(half_set, 1)
                nc.gpsimd.tensor_tensor(rstd[:], lnt[:, 4, :], half[:], ALU.pow).then_inc(pow_done, 1)

            rstd_pow(1)

            pool.wait_ge(load_w, 16 * 8)
            ov = onat[:].rearrange("p c (n k) -> p c k n", k=2)
            nc.gpsimd.tensor_copy(wl1[:, :, 0:HP], ov[:, :, 0, :]).then_inc(l1_laid, 1)
            nc.gpsimd.tensor_copy(wl1[:, :, HP:2 * HP], ov[:, :, 1, :]).then_inc(l1_laid, 1)

            def stage_ctx(b, s):
                if isinstance(b, int):
                    pool.wait_ge(load_ctx[b // XL], 16)
                if late(b, 2):
                    pool.wait_ge(ft_done, b - 1)
                nc.gpsimd.tensor_copy(cst[:, s, :], c_sb[:, at(b), :]).then_inc(ctx_staged, 1)

            for i in range(8):
                pool.wait_ge(load_ctx[i], 16)
            staggered(pool, B, [(0, stage_ctx)])

            def product_b(b, s):
                if late(b, 2):
                    pool.wait_ge(inv_done, b - 1)
                nc.gpsimd.tensor_tensor(
                    ab[:, s, 1, :].rearrange("p (h d) -> p h d", h=H),
                    vhat[:, at(b), :].rearrange("p o (h d) -> p (o h) d", h=H),
                    what[:, 1, at(b * H, H)].unsqueeze(2).broadcast_to([128, H, DH]),
                    ALU.mult).then_inc(pb_done, 1)

            pool.wait_ge(what_done, 2)
            staggered(pool, B, [(0, product_b)])
            rstd_pow(2)
            rstd_pow(3)

            def stage_ctx1(b, s):
                if late(b, 2):
                    pool.wait_ge(tr3_done, b - 1)
                nc.gpsimd.tensor_copy(cst1[:, s, :], c_sb[:, at(b), :]).then_inc(ctx1_staged, 1)

            staggered(pool, B, [(0, stage_ctx1)])
            pool.wait_ge(load_sel, 16)
            nc.gpsimd.tensor_copy(sel[:], sel_f[:]).then_inc(sel_ready, 1)

            with pool.Fori(0, B // GRP) as g:
                pool.wait_ge(mid_done, g + 1)
                nc.gpsimd.tensor_tensor(parts[:, :, 2, :], ccx_rows, parts[:, :, 1, :], ALU.subtract).then_inc(lo_done, 1)
            pool.wait_ge(parts_turned, 2 * (B // GRP))
            nc.gpsimd.memset(vz[:], 0.0).then_inc(vz_clear, 1)

            pool.wait_ge(v63_kept, NQ)
            pool.wait_ge(w63_kept, 2)
            pool.wait_ge(v_kept, B)
            pool.wait_ge(vz_clear, 1)

            def part_heads(q, c):
                if late(q, 1):
                    pool.wait_ge(taken, (q - 1) * 2 * UNITS + (c + 1) * UNITS)
                for r in range(2):
                    def heads(a):
                        return a[:, :, c * 128:(c + 1) * 128].rearrange("p b (m r d) -> p b m r d", r=2, d=DH)[:, :, :, r, :]
                    nc.gpsimd.tensor_copy(heads(vz[:, r]), heads(v_sb[:, at(q * QUAD, QUAD), :])).then_inc(vz_ready, 1)

            def edge(q):
                part_heads(q, 0)
                if late(q, 1):
                    pool.wait_ge(edge_used, 2 * q)
                nc.gpsimd.tensor_tensor(v63m[:], v63[:, at(q), :].rearrange("p o d -> p (o d)"), mask[:, 0:D], ALU.mult).then_inc(edge_ready, 1)
                nc.gpsimd.tensor_tensor(w63m[:], w63T[:, at(q), :].broadcast_to([QUAD * H, QUAD, L]),
                                        mask[:, D:].unsqueeze(2).broadcast_to([QUAD * H, QUAD, L]), ALU.mult).then_inc(edge_ready, 1)
                part_heads(q, 1)

            edge(0)
            with pool.Fori(1, NQ) as q:
                edge(q)

            rstd_pow(4)

            def all_peak(n):
                pool.wait_ge(peak_col, n + 1)
                nc.gpsimd.partition_all_reduce(unit[:, n, 1:2], unit[:, n, 0:1], 128, bass.bass_isa.ReduceOp.max).then_inc(peak_all, 1)

            def widen(t, s):
                if late(t, 2):
                    pool.wait_ge(hid_mm, (t - 1) * IC)
                nc.gpsimd.tensor_copy(xqs[:, s], xqT[:, :, at_tokens(t % NQ if isinstance(t, int) else t)]).then_inc(xqs_ready, 1)

            all_peak(0)
            pool.wait_ge(xq_kept, B)
            for t in range(NQ):
                widen(t, t % 2)
            all_peak(1)
            for t in range(NQ, 2 * NQ):
                widen(t, t % 2)
            for n in range(2, 5):
                all_peak(n)

        @block.scalar
        def _(act):
            act.dma_start(big[:], c_big).then_inc(load_c, 16)
            act.dma_start(small_f[:], c_small).then_inc(load_c, 16)
            act.dma_start(col[:], c_col).then_inc(load_c, 16)
            act.dma_start(mask[:], c_mask).then_inc(load_c, 16)
            for i, w in enumerate((wq, wk, wv, wo)):
                act.dma_start(wnat[:, i], w.rearrange("(c p) d -> p c d", p=128)).then_inc(load_w, 16)
            for name, src in (("bq", bq), ("bk", bk), ("bv", bv), ("bo", bo), ("bf", bf), ("bval", bval), ("bout", bout)):
                act.dma_start(brow[:, BAT[name]:BAT[name] + D], src.rearrange("(a n) -> a n", a=1)).then_inc(load_b, 16)
            act.dma_start(brow[:, BAT["boff"]:BAT["boff"] + 2 * HP].rearrange("a (k n) -> a k n", k=2),
                          boff.rearrange("(a n k) -> a k n", a=1, k=2),
                          allow_slow_non_contiguous=True).then_inc(load_b, 16)
            act.dma_start(brow[:, BAT["batt"]:BAT["batt"] + HP], batt.rearrange("(a n) -> a n", a=1)).then_inc(load_b, 16)
            act.dma_start(onat[:], woff.rearrange("(c p) n -> p c n", p=128)).then_inc(load_w, 16)
            act.dma_start(wl1[:, :, 2 * HP:], watt.rearrange("(c p) n -> p c n", p=128)).then_inc(load_w, 16)
            act.dma_start(wval_sb[:], wval.rearrange("(c p) n -> p c n", p=128)).then_inc(load_w, 16)
            act.dma_start(wout_sb[:], wout.rearrange("(c p) n -> p c n", p=128)).then_inc(load_w, 16)
            act.dma_start(four[:], c_four).then_inc(load_f, 16)
            act.dma_start(fnat[:, 0], wfr.rearrange("(c p) n -> p c n", p=128)).then_inc(load_f, 16)
            act.dma_start(fnat[:, 1], wfi.rearrange("(c p) n -> p c n", p=128)).then_inc(load_f, 16)

            act.dma_start(deq[:, 0].rearrange("p (c d) -> p c d", d=D), wgate.rearrange("(c p) d -> p c d", p=128)).then_inc(load_g, 16)
            act.dma_start(deq[:, 1].rearrange("p (c d) -> p c d", d=D), wup.rearrange("(c p) d -> p c d", p=128)).then_inc(load_g, 16)
            act.dma_start(deq[:, 2].rearrange("p (c d) -> p c d", d=I), wdown.rearrange("(c p) d -> p c d", p=128)).then_inc(load_g, 16)

            for i in range(4):
                act.wait_ge(wt_done, i + 1)
                nc.scalar.activation(wT[:, i], bank[i][:].rearrange("p (c o) -> p c o", c=DC), ACT.Copy).then_inc(wt_copied, 1)
            for i in range(2):
                act.wait_ge(fold_mm, i + 1)
                nc.scalar.activation(pqT[:, i], bank[4 + i][:].rearrange("p (c o) -> p c o", c=DC), ACT.Copy).then_inc(fold_copied, 1)
            act.wait_ge(fold_mm, 3)
            nc.scalar.activation(fold[:], bank[6][:].rearrange("p (c o) -> p c o", c=DC), ACT.Copy).then_inc(fold_copied, 1)

            def copy_ft(b, s):
                act.wait_ge(ft_done, b + 1)
                if late(b, 2):
                    act.wait_ge(proj_done, b - 1)
                nc.scalar.activation(ft_sb[:, s].rearrange("p c t -> p (c t)"), bank[s][:], ACT.Copy).then_inc(ft_copied, 1)

            def copy_qv(b, s):
                act.wait_ge(proj_done, b + 1)
                if late(b, 2):
                    act.wait_ge(prod_done, b - 1)
                nc.scalar.activation(q_sb[:, s, :], bank[2 + s][:, 0:D], ACT.Copy).then_inc(q_copied, 1)
                nc.scalar.activation(vhat[:, at(b), :].rearrange("p o d -> p (o d)"), bank[4 + s][:, 0:D], ACT.Copy).then_inc(v_copied, 1)

            staggered(act, B, [(0, copy_ft), (1, copy_qv)])

            for i in range(9):
                act.wait_ge(gw_turned, i + 1)
                nc.scalar.activation((wgT, wuT, wdT)[i // 3][:].rearrange("p c o -> p (c o)")[:, (i % 3) * 512:(i % 3 + 1) * 512],
                                     bank[6 + i % 2][:], ACT.Copy).then_inc(gw_kept, 1)

            act.wait_ge(d4_ready, 1)
            nc.scalar.activation(w4[:], w4[:], ACT.Exp).then_inc(exp4_done, 1)
            act.wait_ge(wtr_done, 1)
            nc.scalar.activation(wcol[:], bank[1][:], ACT.Copy).then_inc(wcol_done, 1)
            for i in range(2):
                act.wait_ge(what_mm, i + 1)
                nc.scalar.activation(what[:, i, :], bank[2 + i][:], ACT.Copy).then_inc(what_done, 1)

            def copy_oT(b, s):
                act.wait_ge(inv_done, b + 1)
                if late(b, 2):
                    act.wait_ge(wo_done, b - 1)
                nc.scalar.activation(oT[:, s].rearrange("p c t -> p (c t)"), bank[4 + s][:, 0:D], ACT.Copy).then_inc(oT_copied, 1)

            staggered(act, B, [(0, copy_oT)])

            def copy_tr2(b, s):
                act.wait_ge(tr2_done, b + 1)
                if late(b, 2):
                    act.wait_ge(mm2_done, b - 1)
                nc.scalar.activation(tr_sb[:, s].rearrange("p c t -> p (c t)"), bank[s][:, 0:D], ACT.Copy).then_inc(tr2_copied, 1)

            staggered(act, B, [(0, copy_tr2)])

            def copy_tr3(b, s):
                act.wait_ge(tr3_done, b + 1)
                if late(b, 2):
                    act.wait_ge(mm3_done, b - 1)
                nc.scalar.activation(tr_sb[:, s].rearrange("p c t -> p (c t)"), bank[s][:, 0:D], ACT.Copy).then_inc(tr3_copied, 1)
                cT = bank[s][:, D:].rearrange("p (c t) -> p c t", c=DC)
                nc.scalar.activation(cdup[:, s].rearrange("p c (g j) -> p c g j", g=2),
                                     cT[:, :, JH:].unsqueeze(2).broadcast_to([128, DC, 2, JH]), ACT.Copy).then_inc(tr3_copied, 1)
                nc.scalar.activation(ctx63[:, :, at(b * H, H)], cT[:, :, JH - 1:JH].broadcast_to([128, DC, H]), ACT.Copy).then_inc(tr3_copied, 1)

            def keep_v(b, s):
                act.wait_ge(mm3_done, b + 1)
                nc.scalar.activation(v_sb[:, at(b), :].rearrange("p o d -> p (o d)"), bank[2 + s][:, 0:D], ACT.Copy).then_inc(v_kept, 1)

            staggered(act, B, [(0, copy_tr3), (1, keep_v)])
            for q in range(NQ):
                act.wait_ge(v63_mm, q + 1)
                nc.scalar.activation(v63[:, q, :], bank[4 + q % 2][0:QUAD * H, 0:D], ACT.Copy).then_inc(v63_kept, 1)

            act.wait_ge(sel_ready, 1)
            act.wait_ge(v63_mm, NQ)

            def part_act(g):
                act.wait_ge(logit_ready, g + 1)
                nc.scalar.activation(te[:], te[:], ACT.Exp).then_inc(exp_done, 1)
                act.wait_ge(ccx_ready, g + 1)
                if late(g, 1):
                    act.wait_ge(parts_turned, 2 * g)
                nc.scalar.activation(parts[:, :, 0, :], ccx_rows, ACT.Copy).then_inc(hi_done, 1)
                act.wait_ge(res_done, g + 1)
                nc.scalar.activation(parts[:, :, 1, :], ccx_rows, ACT.Copy).then_inc(mid_done, 1)
                keep_rows(act, g, 0)

            part_act(0)
            with act.Fori(1, B // GRP) as g:
                part_act(g)
            act.wait_ge(w63_turned, 1)
            for u in range(2):
                nc.scalar.activation(w63T[:].rearrange("p (g u) t -> p g u t", u=2)[:, :, u, :],
                                     bank[0][u * QUAD * H:(u + 1) * QUAD * H, :].rearrange("p (g t) -> p g t", t=L), ACT.Copy).then_inc(w63_kept, 1)

            def sample_act(q):
                for c in range(DC):
                    for u in range(UNITS):
                        for i in range(2):
                            n = (q * DC + c) * 2 * UNITS + 2 * u + i
                            act.wait_ge(down_mm, n + 1)
                            if c or u >= 2 or late(q, 1):
                                act.wait_ge(hat_done, n - 3)
                            nc.scalar.activation(down[(u % 2) * 2 + i], bank[6 + i][:], ACT.Relu).then_inc(down_done, 1)
                        if u == 3 and c == 1:
                            keep_attT(q, 0)
                        if u == 3 and c == 0 and late(q, 1):
                            keep_attT(q - 1, 1)

            def keep_attT(q, c):
                act.wait_ge(taken, (q * DC + c + 1) * UNITS)
                if c == 0 and late(q, 1):
                    act.wait_ge(out_mm, 2 * q)
                nc.scalar.activation(attT[:, c, :], bank[4 + c][:], ACT.Copy).then_inc(attT_copied, 1)

            sample_act(0)
            with act.Fori(1, NQ) as q:
                sample_act(q)
            keep_attT(NQ - 1, 1)

            def keep_xq(b, s):
                act.wait_ge(xq_turned, b + 1)
                nc.scalar.activation(xqT[:, :, at_seq(b)], bank[s][:, 0:D].rearrange("p (c t) -> p c t", c=DC),
                                     ACT.Copy, bias=-MAGIC).then_inc(xq_kept, 1)

            staggered(act, B, [(0, keep_xq)])

            act.wait_ge(xq_kept, B)

            def fresh_tokens(t):
                return bass.ds(act.snap(t * (QUAD * L)), QUAD * L)

            def keep_hidden(t, n0):
                if n0:
                    act.wait_ge(up_kept, t + 1)
                for oc in range(IC):
                    n = n0 + t * IC + oc
                    act.wait_ge(hid_mm, n + 1)
                    tokens = at_tokens(t) if oc else fresh_tokens(t)
                    nc.scalar.activation(wide[:, oc, tokens], bank[2 + oc][:], ACT.Copy).then_inc(hid_kept, 1)

            def keep_up(t):
                act.wait_ge(up_round, t + 1)
                nc.scalar.activation(up16[:, :, at_tokens(t)], wide[:, :, at_tokens(t)], ACT.Copy, bias=-MAGIC).then_inc(up_kept, 1)

            with act.Fori(0, NQ) as t:
                keep_hidden(t, 0)
            act.wait_ge(spilled, 16)
            with act.Fori(0, NQ) as t:
                keep_up(t)
                keep_hidden(t, NQ * IC)

            def whole_gate(t, s):
                act.wait_ge(g_round, t + 1)
                g = wide[:, :, at_piece(t)]
                nc.scalar.activation(g, g, ACT.Copy, bias=-MAGIC).then_inc(g_whole, 1)

            def sigmoid(t, s):
                act.wait_ge(g_whole, t + 1)
                if late(t, 2):
                    act.wait_ge(g2_done, t - 1)
                nc.scalar.activation(sig[:, s], wide[:, :, at_piece(t)], ACT.Sigmoid, scale=unit[:, 2, 2:3]).then_inc(sig_done, 1)

            def round_sigmoid(t, s):
                act.wait_ge(sig_done, t + 1)
                nc.scalar.activation(sig[:, s], sig[:, s], ACT.Copy, scale=65536.0, bias=MAGIC).then_inc(sig_round, 1)

            staggered(act, 2 * NQ, [(0, whole_gate), (3, round_sigmoid), (2, sigmoid)])

            def round_g2(t, s):
                g = wide[:, :, at_piece(t)]
                nc.scalar.activation(g, g, ACT.Identity, scale=unit[:, 3, 3:4], bias=unit[:, 7, 0:1]).then_inc(g2_round, 1)

            act.wait_ge(unit_step, 1 + 4 * 5)
            staggered(act, 2 * NQ, [(0, round_g2)])

            def round_o(b, s):
                if late(b, 2):
                    act.wait_ge(o_whole, b - 1)
                nc.scalar.activation(hid[:, 2 + s], wide[:, :, at_seq(b)], ACT.Identity, scale=unit[:, 4, 3:4], bias=unit[:, 7, 0:1]).then_inc(o_round, 1)

            act.wait_ge(unit_step, 1 + 5 * 5)
            staggered(act, B, [(0, round_o)])

        @block.tensor
        def _(pe):
            mm = nc.tensor.matmul

            pe.wait_ge(load_c, 64)
            pe.wait_ge(load_w, 16 * 8)
            for i in range(4):
                for oc in range(DC):
                    for dc in range(DC):
                        last = nc.tensor.transpose(bank[i][:, dc * D + oc * 128:dc * D + oc * 128 + 128],
                                                   wnat[:, i, oc, dc * 128:(dc + 1) * 128], IDN)
                last.then_inc(wt_done, 1)
            pe.wait_ge(load_f, 48)
            C_, S_, NS_, CD, NSD = (four[:, k] for k in range(5))
            wr, wi = fnat[:, 0], fnat[:, 1]
            for i, terms in enumerate((((wr, C_), (wi, S_)), ((wi, C_), (wr, NS_)))):
                for kc in range(DC):
                    for n, (w, m) in enumerate(terms):
                        for c in range(DC):
                            last = mm(bank[4 + i][:, kc * D:(kc + 1) * D], w[:, c, kc * 128:(kc + 1) * 128], m[:, c, :],
                                      start=(n == 0 and c == 0), stop=(n == 1 and c == DC - 1))
                last.then_inc(fold_mm, 1)
            pe.wait_ge(fold_copied, 2)
            for ncn in range(DC):
                for i, m in enumerate((CD, NSD)):
                    for c in range(DC):
                        last = mm(bank[6][:, ncn * D:(ncn + 1) * D], pqT[:, i, c, ncn * 128:(ncn + 1) * 128], m[:, c, :],
                                  start=(i == 0 and c == 0), stop=(i == 1 and c == DC - 1))
            last.then_inc(fold_mm, 1)
            pe.wait_ge(wt_copied, 4)
            pe.wait_ge(fold_copied, 3)
            pe.wait_ge(small_cast, 2)
            pe.wait_ge(bias_placed, 16)

            def transform(b, s):
                pe.wait_ge(xn_ready, b + 1)
                pe.wait_ge(ctx_staged, b + 1)
                if late(b, 2):
                    pe.wait_ge(ft_copied, b - 1)
                for c in range(DC):
                    mm(bank[s][:, c * 128:(c + 1) * 128], xn[:, s, c * 128:(c + 1) * 128], FWD, start=True, stop=True)
                for c in range(DC):
                    last = mm(bank[s][:, D + c * 128:D + (c + 1) * 128], cst[:, s, c * 128:(c + 1) * 128], FWD,
                              start=True, stop=True)
                last.then_inc(ft_done, 1)

            def project(b, s):
                pe.wait_ge(ft_copied, b + 1)
                if late(b, 2):
                    pe.wait_ge(prod_done, b - 1)
                    pe.wait_ge(v_copied, b - 1)
                mm(bank[2 + s][:], dc3, bias3[:, BAT["bq"]:BAT["bq"] + 2 * D], start=True, stop=False)
                for i in range(2):
                    for c in range(DC):
                        mm(bank[2 + s][:, i * D:(i + 1) * D], ft_sb[:, s, i * DC + c, :], wT[:, i, c, :],
                           start=False, stop=(i == 1 and c == DC - 1))
                mm(bank[4 + s][:, 0:D], dc3, bias3[:, BAT["bv"]:BAT["bv"] + D], start=True, stop=False)
                for c in range(DC):
                    last = mm(bank[4 + s][:, 0:D], ft_sb[:, s, DC + c, :], wT[:, 2, c, :], start=False, stop=(c == DC - 1))
                last.then_inc(proj_done, 1)

            staggered(pe, B, [(0, transform), (1, project)])

            pe.wait_ge(deq_step, 7 * 3)
            blocks = ([(w, c, oc, D) for w in range(2) for c in range(DC) for oc in range(IC)]
                      + [(2, ic, oc, I) for ic in range(IC) for oc in range(DC)])
            for i in range(9):
                if i >= 2:
                    pe.wait_ge(gw_kept, i - 1)
                for k in range(4):
                    w, c, oc, width = blocks[i * 4 + k]
                    last = nc.tensor.transpose(bank[6 + i % 2][:, k * 128:(k + 1) * 128],
                                               deq[:, w, oc * width + c * 128:oc * width + (c + 1) * 128], IDN)
                last.then_inc(gw_turned, 1)

            pe.wait_ge(sab_done, B)
            for k in range(4):
                mm(bank[0][:, k * L:(k + 1) * L], sab[:, 0, k * 128:(k + 1) * 128], MA, start=True, stop=False)
                last = mm(bank[0][:, k * L:(k + 1) * L], sab[:, 1, k * 128:(k + 1) * 128], MB, start=False, stop=True)
            last.then_inc(corr_done, 1)
            pe.wait_ge(wrow_done, 4)
            for k in range(4):
                last = nc.tensor.transpose(bank[1][:, k * 128:(k + 1) * 128], wrow[:, k, :], IDN)
            last.then_inc(wtr_done, 1)
            pe.wait_ge(wcol_done, 1)
            for i, m in enumerate((FWD, SWP)):
                mm(bank[2 + i][:], m, wcol[:], start=True, stop=True).then_inc(what_mm, 1)

            def inverse(b, s):
                pe.wait_ge(pa_done, b + 1)
                pe.wait_ge(pb_done, b + 1)
                if late(b, 2):
                    pe.wait_ge(oT_copied, b - 1)
                for c in range(DC):
                    mm(bank[4 + s][:, c * 128:(c + 1) * 128], ab[:, s, 0, c * 128:(c + 1) * 128], IA, start=True, stop=False)
                    last = mm(bank[4 + s][:, c * 128:(c + 1) * 128], ab[:, s, 1, c * 128:(c + 1) * 128], IB, start=False, stop=True)
                last.then_inc(inv_done, 1)

            def project_out(b, s):
                pe.wait_ge(oT_copied, b + 1)
                if late(b, 2):
                    pe.wait_ge(x1_done, b - 1)
                mm(bank[6 + s][:, 0:D], ones3, bias3[:, BAT["bo"]:BAT["bo"] + D], start=True, stop=False)
                for c in range(DC):
                    last = mm(bank[6 + s][:, 0:D], oT[:, s, c, :], wT[:, 3, c, :], start=False, stop=(c == DC - 1))
                last.then_inc(wo_done, 1)

            staggered(pe, B, [(0, inverse), (1, project_out)])

            def turn2(b, s):
                pe.wait_ge(xn2_ready, b + 1)
                if late(b, 2):
                    pe.wait_ge(tr2_copied, b - 1)
                for c in range(DC):
                    last = nc.tensor.transpose(bank[s][:, c * 128:(c + 1) * 128], xn[:, s, c * 128:(c + 1) * 128], IDN)
                last.then_inc(tr2_done, 1)

            def frequency_ffn(b, s):
                pe.wait_ge(tr2_copied, b + 1)
                if late(b, 2):
                    pe.wait_ge(x2_done, b - 1)
                mm(bank[2 + s][:, 0:D], ones3, bias3[:, BAT["bf"]:BAT["bf"] + D], start=True, stop=False)
                for c in range(DC):
                    last = mm(bank[2 + s][:, 0:D], tr_sb[:, s, c, :], fold[:, c, :], start=False, stop=(c == DC - 1))
                last.then_inc(mm2_done, 1)

            staggered(pe, B, [(0, turn2), (1, frequency_ffn)])

            def turn3(b, s):
                pe.wait_ge(xn3_ready, b + 1)
                pe.wait_ge(ctx1_staged, b + 1)
                if late(b, 2):
                    pe.wait_ge(tr3_copied, 3 * (b - 1))
                for i, src in enumerate((xn, cst1)):
                    for c in range(DC):
                        last = nc.tensor.transpose(bank[s][:, i * D + c * 128:i * D + (c + 1) * 128],
                                                   src[:, s, c * 128:(c + 1) * 128], IDN)
                last.then_inc(tr3_done, 1)

            def project3(b, s):
                pe.wait_ge(tr3_copied, 3 * (b + 1))
                if late(b, 2):
                    pe.wait_ge(v_kept, b - 1)
                    pe.wait_ge(off_kept, b - 1)
                mm(bank[2 + s][:, 0:D + 3 * HP], ones3, bias3[:, BAT["bval"]:BAT["bval"] + D + 3 * HP], start=True, stop=False)
                for c in range(DC):
                    mm(bank[2 + s][:, 0:D], cdup[:, s, c, :], wval_sb[:, c, :], start=False, stop=False)
                for c in range(DC):
                    last = mm(bank[2 + s][:, D:D + 3 * HP], tr_sb[:, s, c, :], wl1[:, c, :], start=False, stop=(c == DC - 1))
                last.then_inc(mm3_done, 1)

            pe.wait_ge(l1_laid, 2)
            staggered(pe, B, [(0, turn3), (1, project3)])
            for q in range(NQ):
                if q >= 2:
                    pe.wait_ge(v63_kept, q - 1)
                o = bank[4 + q % 2][0:QUAD * H, 0:D]
                mm(o, ones3[:, 0:QUAD * H], bias3[:, BAT["bval"]:BAT["bval"] + D], start=True, stop=False)
                for c in range(DC):
                    last = mm(o, ctx63[:, c, q * QUAD * H:(q + 1) * QUAD * H], wval_sb[:, c, :], start=False, stop=(c == DC - 1))
                last.then_inc(v63_mm, 1)

            pe.wait_ge(off_kept, B)
            pe.wait_ge(v63_kept, NQ)
            pe.wait_ge(v_kept, B)

            def turn_parts(g):
                pe.wait_ge(lo_done, g + 1)
                for u in range(2):
                    if late(g, 1):
                        pe.wait_ge(rows_kept[u], g * HB)
                    for n in range(HB):
                        for b in range(QUAD):
                            last = mm(bank[HB * u + n][0:ROWS, b * L:(b + 1) * L],
                                      parts[:, (u * QUAD + b) * HB + n, :, :].rearrange("p a r -> p (a r)"), idn16[:],
                                      start=(b == 0), stop=(b == QUAD - 1))
                    last.then_inc(parts_turned, 1)

            turn_parts(0)
            with pe.Fori(1, B // GRP) as g:
                turn_parts(g)
            pe.wait_ge(w63_ready, B // GRP)
            pe.wait_ge(rows_kept[0], HB * B // GRP)
            for g in range(B // GRP):
                last = nc.tensor.transpose(bank[0][:, g * 128:(g + 1) * 128], w63[:, g * 128:(g + 1) * 128], IDN)
            last.then_inc(w63_turned, 1)

            def of_unit(u, i):
                m, r, pp = 2 * (u % 2) + i, u // 4, (u // 2) % 2
                return m, r, pp

            def sides(q, c, u):
                for i in range(2):
                    n = (q * DC + c) * 2 * UNITS + 2 * u + i
                    m, r, pp = of_unit(u, i)
                    pair = (2 * (m % 2) + r) * 2 + pp
                    row = rows[:, 2 * c + m // 2, at(q), :].rearrange("p o t -> p (o t)")
                    if c or u or late(q, 1):
                        pe.wait_ge(down_done, n - 1)
                    mm(bank[6 + i][:], sel[:, pair, 1, :], row, start=True, stop=True).then_inc(down_mm, 1)
                    if c or u >= 2 or late(q, 1):
                        pe.wait_ge(hat_done, n - 3)
                    mm(bank[(u % 2) * 2 + i][:], sel[:, pair, 0, :], row, start=True, stop=True).then_inc(up_mm, 1)

            def take(q, c, u):
                pe.wait_ge(hat_done, (q * DC + c) * 2 * UNITS + 2 * u + 2)
                for b in range(QUAD):
                    for i in range(2):
                        m, r, _ = of_unit(u, i)
                        w = c * 128 + 32 * m
                        last = mm(bank[4 + c][32 * m:32 * m + 32, b * 128:(b + 1) * 128], vz[:, r, b, w:w + 32],
                                  hat[:, (u % 2) * 2 + i, b * 128:(b + 1) * 128],
                                  start=False, stop=(u >= UNITS - 2 and b == QUAD - 1), skip_group_check=True)
                last.then_inc(taken, 1)

            def project_att(q, i):
                pe.wait_ge(attT_copied, 2 * q + 2)
                if i:
                    pe.wait_ge(x3_done, 2 * q + 1)
                mm(bank[5][:].rearrange("p (b d) -> p b d", b=2), ones3,
                   bias3[:, BAT["bout"]:BAT["bout"] + D].unsqueeze(1).broadcast_to([3, 2, D]), start=True, stop=False)
                for b in range(2):
                    for c in range(DC):
                        last = mm(bank[5][:, b * D:(b + 1) * D], attT[:, c, (2 * i + b) * L:(2 * i + b + 1) * L], wout_sb[:, c, :],
                                  start=False, stop=(b == 1 and c == DC - 1))
                last.then_inc(out_mm, 1)

            def sample_pe(q):
                for c in range(DC):
                    for u in range(UNITS):
                        sides(q, c, u)
                        if u == 2:
                            if c == 0:
                                pe.wait_ge(edge_ready, 2 * q + 2)
                            if late(q, 1):
                                pe.wait_ge(attT_copied, 2 * (q - 1) + c + 1)
                                if c == 1:
                                    pe.wait_ge(x3_done, 2 * q)
                            mm(bank[4 + c][:], v63m[:, c * 128:(c + 1) * 128], w63m[:].rearrange("p b t -> p (b t)"),
                               start=True, stop=True).then_inc(edge_used, 1)
                        if u >= 2:
                            if (u - 2) % 4 == 0:
                                pe.wait_ge(vz_ready, 4 * q + 2 * c + (u - 2) // 4 + 1)
                            take(q, c, u - 2)
                        elif c or late(q, 1):
                            take(q - 1 + c, 1 - c, UNITS - 2 + u)
                        if c == 0 and u in (4, 7) and late(q, 1):
                            project_att(q - 1, u // 7)

            pe.wait_ge(w63_kept, 2)
            pe.wait_ge(rows_kept[1], HB * B // GRP)
            sample_pe(0)
            with pe.Fori(1, NQ) as q:
                sample_pe(q)
            take(NQ - 1, 1, UNITS - 2)
            take(NQ - 1, 1, UNITS - 1)
            project_att(NQ - 1, 0)
            project_att(NQ - 1, 1)

            pe.wait_ge(attT_copied, 2 * NQ)

            def turn_xq(b, s):
                pe.wait_ge(xq_ready, b + 1)
                if late(b, 2):
                    pe.wait_ge(xq_kept, b - 1)
                for c in range(DC):
                    last = nc.tensor.transpose(bank[s][:, c * 128:(c + 1) * 128], xn[:, s, c * 128:(c + 1) * 128], IDN)
                last.then_inc(xq_turned, 1)

            staggered(pe, B, [(0, turn_xq)])

            def hidden(t, s, w):
                pe.wait_ge(xqs_ready, t + 1)
                for oc in range(IC):
                    if late(t, 1):
                        pe.wait_ge(hid_kept, (t - 1) * IC + oc + 1)
                    for c in range(DC):
                        last = mm(bank[2 + oc][:], w[:, c, oc * 128:(oc + 1) * 128], xqs[:, s, c, :], start=(c == 0), stop=(c == DC - 1))
                    last.then_inc(hid_mm, 1)

            for t in range(2):
                hidden(t, t, wuT)
            with pe.Fori(1, NQ // 2) as i:
                for u in range(2):
                    hidden(i * 2 + u, u, wuT)
            with pe.Fori(NQ // 2, NQ) as i:
                for u in range(2):
                    hidden(i * 2 + u, u, wgT)

            def down_product(b, s):
                pe.wait_ge(o_whole, b + 1)
                if late(b, 2):
                    pe.wait_ge(y_done, b - 1)
                for ic in range(IC):
                    last = mm(bank[s][:, 0:D], hid[:, s, ic, :], wdT[:, ic, :], start=(ic == 0), stop=(ic == IC - 1))
                last.then_inc(down_out, 1)

            pe.wait_ge(hid_kept, 2 * NQ * IC)
            staggered(pe, B, [(0, down_product)])

        @block.vector
        def _(dve):
            V = nc.vector

            def moments(b):
                V.bn_stats(stats[:, at(b), :].rearrange("p o s -> p (o s)"), x_sb[:, at(b), :].rearrange("p o d -> p (o d)")).then_inc(bn_done, 1)

            def ln_finish(n):
                me, ve, mo, vo = (stats[:, :, k] for k in (1, 2, 4, 5))
                dve.wait_ge(bn_done, B * n)
                k = 6 * (n - 1)
                V.tensor_tensor(lnt[:, 0, :], me, mo, ALU.add).then_inc(ln_step, 1)
                V.tensor_tensor(lnt[:, 1, :], me, mo, ALU.subtract).then_inc(ln_step, 1)
                V.tensor_tensor(lnt[:, 2, :], ve, vo, ALU.add).then_inc(ln_step, 1)
                dve.wait_ge(ln_step, k + 2)
                V.scalar_tensor_tensor(lnt[:, 3, :], lnt[:, 1, :], 0.25, lnt[:, 1, :], ALU.mult, ALU.mult).then_inc(ln_step, 1)
                dve.wait_ge(ln_step, k + 4)
                V.scalar_tensor_tensor(lnt[:, 2, :], lnt[:, 2, :], 1.0 / D, lnt[:, 3, :], ALU.mult, ALU.add).then_inc(ln_step, 1)
                dve.wait_ge(ln_step, k + 5)
                V.tensor_scalar(lnt[:, 4, :], lnt[:, 2, :], LN_EPS, None, ALU.add).then_inc(ln_step, 1)
                dve.wait_ge(pow_done, n)
                V.scalar_tensor_tensor(nmr[:], lnt[:, 0, :], -0.5, rstd[:], ALU.mult, ALU.mult).then_inc(ln_ready, 1)
                dve.wait_ge(ln_ready, n)

            def normalise(b, s, ready):
                V.tensor_scalar(xn[:, s, :], x_sb[:, at(b), :].rearrange("p o d -> p (o d)"), rstd[:, at(b)], nmr[:, at(b)],
                                ALU.mult, ALU.add).then_inc(ready, 1)

            for b in range(B):
                if b % XL == 0:
                    dve.wait_ge(load_x[b // XL], 16)
                moments(b)
            ln_finish(1)
            dve.wait_ge(load_c, 64)
            V.tensor_copy(small[:], small_f[:]).then_inc(small_cast, 1)
            V.tensor_copy(idn16[:], IDN).then_inc(small_cast, 1)

            dve.wait_ge(load_g, 48)
            ws = [deq[:, w].rearrange("p (n k) -> p n k", k=WBLK) for w in range(3)]
            NB_ = I * D // 128 // WBLK

            def spread(a):
                return a.unsqueeze(2).broadcast_to([128, NB_, WBLK])

            for w in range(3):
                V.tensor_reduce(dsc[:, w, 0, :], ws[w], AX.X, ALU.max, apply_absolute_value=True).then_inc(deq_step, 1)
            for w in range(3):
                dve.wait_ge(deq_step, w + 1)
                V.tensor_scalar(dsc[:, w, 1, :], dsc[:, w, 0, :], 1.0 / WMAX, 1e-12, ALU.mult, ALU.max).then_inc(deq_step, 1)
            for w in range(3):
                dve.wait_ge(deq_step, 3 + w + 1)
                V.reciprocal(dsc[:, w, 2, :], dsc[:, w, 1, :]).then_inc(deq_step, 1)
            for w in range(3):
                dve.wait_ge(deq_step, 6 + w + 1)
                V.tensor_tensor(ws[w], ws[w], spread(dsc[:, w, 2, :]), ALU.mult).then_inc(deq_step, 1)
            for w in range(3):
                dve.wait_ge(deq_step, 9 + w + 1)
                V.tensor_scalar(ws[w], ws[w], MAGIC, MAGIC, ALU.add, ALU.subtract).then_inc(deq_step, 1)
            for w in range(3):
                dve.wait_ge(deq_step, 12 + w + 1)
                V.tensor_scalar(ws[w], ws[w], WMAX, -WMAX - 1.0, ALU.min, ALU.max).then_inc(deq_step, 1)
            for w in range(3):
                dve.wait_ge(deq_step, 15 + w + 1)
                V.tensor_tensor(ws[w], ws[w], spread(dsc[:, w, 1, :]), ALU.mult).then_inc(deq_step, 1)

            def norm0(b, s):
                if late(b, 2):
                    dve.wait_ge(ft_done, b - 1)
                normalise(b, s, xn_ready)

            def products(b, s):
                dve.wait_ge(q_copied, b + 1)
                if late(b, 2):
                    dve.wait_ge(sab_done, b - 1)
                q, k = q_sb[:, s, :], bank[2 + s][:, D:2 * D]
                V.tensor_tensor(ab[:, s, 0, :], q, k, ALU.mult)
                V.tensor_tensor(ab[0:64, s, 1, :], q[0:64], k[64:128], ALU.mult)
                V.tensor_tensor(ab[64:128, s, 1, :], q[64:128], k[0:64], ALU.mult).then_inc(prod_done, 1)

            def head_sums(b, s):
                dve.wait_ge(prod_done, b + 1)
                V.tensor_reduce(sab[:, :, at(b * H, H)], ab[:, s].rearrange("p a (h d) -> p a h d", h=H), AX.X, ALU.add).then_inc(sab_done, 1)

            staggered(dve, B, [(0, norm0), (2, products), (3, head_sums)])

            dve.wait_ge(corr_done, 1)
            V.tensor_copy(corr[:], bank[0][:].rearrange("p (k t) -> p k t", k=4)).then_inc(dve_b, 1)
            dve.wait_ge(dve_b, 1)
            for k in range(4):
                V.max(top8[:, k, :], corr[:, k, :]).then_inc(dve_b, 1)
            for k in range(4):
                dve.wait_ge(dve_b, 2 + k)
                V.max_index(idx8[:, k, :], top8[:, k, :], corr[:, k, :]).then_inc(dve_b, 1)
            V.tensor_tensor(w4[:], top8[:, :, 0:TOPK], top8[:, :, 0:1].broadcast_to([128, 4, TOPK]), ALU.subtract).then_inc(d4_ready, 1)
            dve.wait_ge(dve_b, 9)
            V.tensor_copy(idxf[:], idx8[:, :, 0:TOPK])
            dve.wait_ge(exp4_done, 1)
            V.tensor_reduce(z4[:, 0, :], w4[:], AX.X, ALU.add).then_inc(dve_b, 1)
            dve.wait_ge(dve_b, 10)
            V.reciprocal(z4[:, 1, :], z4[:, 0, :]).then_inc(dve_b, 1)
            dve.wait_ge(dve_b, 11)
            V.tensor_tensor(w4[:], w4[:], z4[:, 1, :].unsqueeze(2).broadcast_to([128, 4, TOPK]), ALU.mult).then_inc(dve_b, 1)
            for k in range(4):
                dve.wait_ge(dve_b, 12 + k)
                if k:
                    dve.wait_ge(wrow_done, k)
                for i in range(TOPK):
                    last = V.tensor_scalar(hot[:, i, :], iota, idxf[:, k, i:i + 1], w4[:, k, i:i + 1], ALU.is_equal, ALU.mult)
                last.then_inc(dve_b, 1)
                dve.wait_ge(dve_b, 13 + k)
                V.tensor_reduce(wrow[:, k, :], hot[:].rearrange("p i t -> p t i"), AX.X, ALU.add).then_inc(wrow_done, 1)

            def product_a(b, s):
                if late(b, 2):
                    dve.wait_ge(inv_done, b - 1)
                V.tensor_tensor(ab[:, s, 0, :].rearrange("p (h d) -> p h d", h=H),
                                vhat[:, at(b), :].rearrange("p o (h d) -> p (o h) d", h=H),
                                what[:, 0, at(b * H, H)].unsqueeze(2).broadcast_to([128, H, DH]),
                                ALU.mult).then_inc(pa_done, 1)

            def add_x(b, s, done, source, landed):
                dve.wait_ge(done, b + 1)
                xb = x_sb[:, at(b), :].rearrange("p o d -> p (o d)")
                V.tensor_tensor(xb, source[:, 0:D], xb, ALU.add).then_inc(landed, 1)

            def moments_of(landed):
                def step(b, s):
                    dve.wait_ge(landed, b + 1)
                    moments(b)
                return step

            dve.wait_ge(what_done, 2)
            dve.wait_ge(v_copied, B)
            staggered(dve, B, [(0, product_a), (2, lambda b, s: add_x(b, s, wo_done, bank[6 + s], x1_done)), (3, moments_of(x1_done))])
            ln_finish(2)

            def norm2(b, s):
                if late(b, 2):
                    dve.wait_ge(tr2_done, b - 1)
                normalise(b, s, xn2_ready)

            staggered(dve, B, [(0, norm2), (2, lambda b, s: add_x(b, s, mm2_done, bank[2 + s], x2_done)), (3, moments_of(x2_done))])
            ln_finish(3)

            def norm3(b, s):
                if late(b, 2):
                    dve.wait_ge(tr3_done, b - 1)
                normalise(b, s, xn3_ready)

            def keep_off(b, s):
                dve.wait_ge(mm3_done, b + 1)
                dve.wait_ge(v_kept, b + 1)
                V.tensor_copy(off[:, at(b), :].rearrange("p o n -> p (o n)"), bank[2 + s][:, D:D + 3 * HP]).then_inc(off_kept, 1)

            staggered(dve, B, [(0, norm3), (2, keep_off)])
            dve.wait_ge(off_kept, B)
            dve.wait_ge(mm3_done, B)

            NS = 13

            def sampling_weights(g):
                o = off[:, at(g * GRP, GRP), :]
                offx, offy, att = o[:, :, 0:HP], o[:, :, HP:2 * HP], o[:, :, 2 * HP:]
                att4 = att.rearrange("p b (h k) -> p b h k", k=NP)

                def heads(a):
                    return a.rearrange("p (b h) -> p b h", b=GRP).unsqueeze(3).broadcast_to([128, GRP, H, NP])

                def point(a):
                    return a.rearrange("p b (h k) -> p b h k", k=NP)

                def after(k):
                    if k or late(g, 1):
                        dve.wait_ge(wstep, g * NS + k)

                after(0)
                V.tensor_reduce(ts[:, 0, :].rearrange("p (b h) -> p b h", b=GRP), att4, AX.X, ALU.max).then_inc(wstep, 1)
                V.tensor_scalar(tx[:], offx, 0.0, 1.0, ALU.max, ALU.min).then_inc(wstep, 1)
                V.tensor_scalar(ty[:], offy, refy, 0.0, ALU.add, ALU.max).then_inc(wstep, 1)
                after(1)
                V.tensor_tensor(point(te[:]), att4, heads(ts[:, 0, :]), ALU.subtract).then_inc(logit_ready, 1)
                after(2)
                V.tensor_scalar(tx[:], tx[:], 1.0, L / 2.0, ALU.add, ALU.mult).then_inc(wstep, 1)
                after(3)
                V.tensor_scalar(ty[:], ty[:], 1.0, 1.0, ALU.min, ALU.add).then_inc(wstep, 1)
                after(4)
                V.tensor_scalar(tx[:], tx[:], 0.5, None, ALU.subtract).then_inc(wstep, 1)
                after(5)
                V.tensor_scalar(ty[:], ty[:], 1.0, -0.5, ALU.subtract, ALU.mult).then_inc(wstep, 1)
                after(6)
                V.tensor_scalar(td[:], tx[:], -1.0, JH * 1.0, ALU.mult, ALU.add).then_inc(wstep, 1)
                dve.wait_ge(exp_done, g + 1)
                V.tensor_reduce(ts[:, 1, :].rearrange("p (b h) -> p b h", b=GRP), point(te[:]), AX.X, ALU.add).then_inc(wstep, 1)
                after(9)
                V.reciprocal(ts[:, 2, :], ts[:, 1, :]).then_inc(wstep, 1)
                after(10)
                V.tensor_tensor(point(te[:]), point(te[:]), heads(ts[:, 2, :]), ALU.mult).then_inc(wstep, 1)
                after(11)
                if late(g, 1):
                    dve.wait_ge(lo_done, g)
                def blocks(a):
                    return a.rearrange("p b (n t) -> p (b n) t", n=HB)
                V.scalar_tensor_tensor(ccx_blocks[:, :, 1, :], blocks(ty[:]), 1.0, blocks(te[:]), ALU.add, ALU.mult).then_inc(wstep, 1)
                after(12)
                V.tensor_tensor(ccx_blocks[:, :, 0, :], ccx_blocks[:, :, 1, :], blocks(tx[:]), ALU.mult).then_inc(ccx_ready, 1)
                V.scalar_tensor_tensor(blocks(tc[:]), blocks(td[:]), 0.0, ccx_blocks[:, :, 1, :], ALU.max, ALU.mult).then_inc(wstep, 1)
                after(13)
                V.tensor_reduce(w63[:, at(g * GRP * H, GRP * H)].rearrange("p (b h) -> p b h", b=GRP), point(tc[:]), AX.X, ALU.add).then_inc(w63_ready, 1)
                dve.wait_ge(hi_done, g + 1)
                V.tensor_tensor(ccx_rows, ccx_rows, parts[:, :, 0, :], ALU.subtract).then_inc(res_done, 1)
                keep_rows(dve, g, 1)

            sampling_weights(0)
            with dve.Fori(1, B // GRP) as g:
                sampling_weights(g)

            def sample_dve(q):
                for c in range(DC):
                    for u in range(UNITS):
                        for i in range(2):
                            n = (q * DC + c) * 2 * UNITS + 2 * u + i
                            dve.wait_ge(up_mm, n + 1)
                            dve.wait_ge(down_done, n + 1)
                            if i == 0 and (c or u >= 2 or late(q, 1)):
                                dve.wait_ge(taken, (q * DC + c) * UNITS + u - 1)
                            k = (u % 2) * 2 + i
                            V.scalar_tensor_tensor(hat[:, k, :], bank[k][:], 0.0, down[k], ALU.max, ALU.min).then_inc(hat_done, 1)
                        if late(q, 1):
                            if (c, u) in ((0, 5), (1, 0)):
                                add_out(q - 1, c)
                            if c == 1 and u in (2, 4):
                                moments_out(q - 1, u // 4)

            def add_out(q, i):
                dve.wait_ge(out_mm, 2 * q + i + 1)
                xb = x_sb[:, at(q * QUAD + 2 * i, 2), :]
                V.tensor_tensor(xb, bank[5][:].rearrange("p (b d) -> p b d", b=2), xb, ALU.add).then_inc(x3_done, 1)

            def moments_out(q, i):
                dve.wait_ge(x3_done, 2 * q + i + 1)
                for b in range(2):
                    moments(q * QUAD + 2 * i + b)

            sample_dve(0)
            with dve.Fori(1, NQ) as q:
                sample_dve(q)
            add_out(NQ - 1, 0)
            add_out(NQ - 1, 1)
            moments_out(NQ - 1, 0)
            moments_out(NQ - 1, 1)

            ln_finish(4)
            V.memset(unit[:, 5:8, :], 1.0).then_inc(unit_step, 1)
            dve.wait_ge(unit_step, 1)
            V.memset(unit[:, 7, 0:1], MAGIC)

            def norm4(b, s):
                V.tensor_scalar(xnorm_sb(b), x_sb[:, at(b), :].rearrange("p o d -> p (o d)"), rstd[:, at(b)], nmr[:, at(b)],
                                ALU.mult, ALU.add).then_inc(xn4_done, 1)

            def peak4(b, s):
                dve.wait_ge(xn4_done, b + 1)
                V.tensor_reduce(peak[:, 0, at(b)], xnorm_sb(b), AX.X, ALU.max, apply_absolute_value=True).then_inc(xpeak, 1)

            staggered(dve, B, [(0, norm4), (1, peak4)])

            def make_unit(n, count):
                V.tensor_reduce(unit[:, n, 0:1], peak[:, n, 0:count], AX.X, ALU.max).then_inc(peak_col, 1)
                dve.wait_ge(peak_all, n + 1)
                raw = unit[:, 5, n:n + 1]
                k = n * 5 + 1
                V.tensor_tensor(unit[:, n, 4:5], unit[:, n, 1:2], raw, ALU.mult).then_inc(unit_step, 1)
                dve.wait_ge(unit_step, k + 1)
                V.tensor_scalar(unit[:, n, 2:3], unit[:, n, 4:5], 1.0 / QMAX, 1e-12, ALU.mult, ALU.max).then_inc(unit_step, 1)
                dve.wait_ge(unit_step, k + 2)
                V.reciprocal(unit[:, n, 5:6], unit[:, n, 2:3]).then_inc(unit_step, 1)
                dve.wait_ge(unit_step, k + 3)
                V.tensor_tensor(unit[:, n, 3:4], unit[:, n, 5:6], raw, ALU.mult).then_inc(unit_step, 1)
                if n == 0:
                    V.tensor_copy(unit[:, 5, 1:3], unit[:, 0, 2:3].broadcast_to([128, 2])).then_inc(unit_step, 1)
                elif n == 2:
                    V.tensor_scalar(unit[:, 5, 3:4], unit[:, 2, 2:3], 1.0 / 65536, None, ALU.mult).then_inc(unit_step, 1)
                elif n == 3:
                    V.tensor_tensor(unit[:, 5, 4:5], unit[:, 3, 2:3], unit[:, 1, 2:3], ALU.mult).then_inc(unit_step, 1)
                else:
                    V.tensor_copy(unit[:, 6, n:n + 1], unit[:, n, 2:3]).then_inc(unit_step, 1)
                dve.wait_ge(unit_step, k + 5)

            dve.wait_ge(xpeak, B)
            make_unit(0, B)

            def quantise_x(b, s):
                if late(b, 2):
                    dve.wait_ge(xq_turned, b - 1)
                V.tensor_scalar(xn[:, s, :], xnorm_sb(b), unit[:, 0, 3:4], MAGIC, ALU.mult, ALU.add).then_inc(xq_ready, 1)

            staggered(dve, B, [(0, quantise_x)])

            def peak_hidden(t, n):
                dve.wait_ge(hid_kept, ((n - 1) * NQ + t + 1) * IC)
                V.tensor_reduce(peak[:, n, at(t)], wide[:, :, at_tokens(t)], AX.XY, ALU.max, apply_absolute_value=True).then_inc(hid_peak, 1)

            with dve.Fori(0, NQ) as t:
                peak_hidden(t, 1)
            dve.wait_ge(hid_peak, NQ)
            make_unit(1, NQ)

            def round_up(t):
                g = wide[:, :, at_tokens(t)]
                V.tensor_scalar(g, g, unit[:, 1, 3:4], MAGIC, ALU.mult, ALU.add).then_inc(up_round, 1)

            round_up(0)
            with dve.Fori(1, NQ) as t:
                round_up(t)
                peak_hidden(t - 1, 2)
            peak_hidden(NQ - 1, 2)
            dve.wait_ge(hid_peak, 2 * NQ)
            make_unit(2, NQ)

            def round_gate(t, s):
                g = wide[:, :, at_piece(t)]
                V.tensor_scalar(g, g, unit[:, 2, 3:4], MAGIC, ALU.mult, ALU.add).then_inc(g_round, 1)

            def whole_sigmoid(t, s):
                dve.wait_ge(sig_round, t + 1)
                V.tensor_scalar(sig[:, s], sig[:, s], MAGIC, 65535.0, ALU.subtract, ALU.min).then_inc(sig_whole, 1)

            def gated(t, s):
                dve.wait_ge(sig_whole, t + 1)
                g = wide[:, :, at_piece(t)]
                V.scalar_tensor_tensor(g, sig[:, s], 0.0, g, ALU.max, ALU.mult).then_inc(g2_done, 1)

            def peak_gated(t, s):
                dve.wait_ge(g2_done, t + 1)
                V.tensor_reduce(peak[:, 3, at(t)], wide[:, :, at_piece(t)], AX.XY, ALU.max, apply_absolute_value=True).then_inc(g2_peak, 1)

            staggered(dve, 2 * NQ, [(0, round_gate), (5, gated), (4, whole_sigmoid), (6, peak_gated)])
            dve.wait_ge(g2_peak, 2 * NQ)
            make_unit(3, 2 * NQ)

            def hidden_product(t, s):
                dve.wait_ge(g2_round, t + 1)
                g = wide[:, :, at_piece(t)]
                V.scalar_tensor_tensor(g, g, MAGIC, up16[:, :, at_piece(t)], ALU.subtract, ALU.mult).then_inc(o_done, 1)

            def peak_product(t, s):
                dve.wait_ge(o_done, t + 1)
                V.tensor_reduce(peak[:, 4, at(t)], wide[:, :, at_piece(t)], AX.XY, ALU.max, apply_absolute_value=True).then_inc(o_peak, 1)

            staggered(dve, 2 * NQ, [(0, hidden_product), (1, peak_product)])
            dve.wait_ge(o_peak, 2 * NQ)
            make_unit(4, 2 * NQ)

            def whole_hidden(b, s):
                dve.wait_ge(o_round, b + 1)
                if late(b, 2):
                    dve.wait_ge(down_out, b - 1)
                V.tensor_scalar(hid[:, s], hid[:, 2 + s], MAGIC, None, ALU.subtract).then_inc(o_whole, 1)

            def add_y(b, s):
                dve.wait_ge(down_out, b + 1)
                xb = x_sb[:, at(b), :].rearrange("p o d -> p (o d)")
                V.scalar_tensor_tensor(xb, bank[s][:, 0:D], unit[:, 4, 2:3], xb, ALU.mult, ALU.add).then_inc(y_done, 1)

            dve.wait_ge(reloaded, 16 * 8)
            staggered(dve, B, [(0, whole_hidden), (2, add_y)])


_INS = ["x", "ctx_1024", "L0_xattn_Wq", "L0_xattn_Wk", "L0_xattn_Wv", "L0_xattn_Wo", "L0_xattn_bq", "L0_xattn_bk",
        "L0_xattn_bv", "L0_xattn_bo", "L0_ffn_w_freq_real", "L0_ffn_w_freq_imag", "L0_ffn_bias", "L1_xattn_w_value",
        "L1_xattn_b_value", "L1_xattn_w_off", "L1_xattn_b_off", "L1_xattn_w_attw", "L1_xattn_b_attw", "L1_xattn_w_out",
        "L1_xattn_b_out", "L1_ffn_w_gate", "L1_ffn_w_up", "L1_ffn_w_down"]


def kernel(**inputs):
    import concourse.bacc as _bacc
    from concourse.bass_utils import run_bass_kernel_spmd as _run

    nc = _bacc.Bacc("TRN2", target_bir_lowering=False, num_devices=1)
    arrays, args = {}, []
    named = [(n, np.ascontiguousarray(inputs[n])) for n in _INS] + list(constants().items())
    for name, a in named:
        arrays[f"in_{name}_dram"] = a
        args.append(nc.dram_tensor(f"in_{name}_dram", a.shape, mybir.dt.from_np(a.dtype), kind="ExternalInput").ap())
    args.append(nc.dram_tensor("out_0_dram", (B, L, D), F32, kind="ExternalOutput").ap())
    build(nc, *args)
    return _run(nc, [arrays], core_ids=[0]).results[0]["out_0_dram"]
```

```python
from contextlib import ExitStack

import numpy as np

import concourse.bass as bass
from concourse import mybir

F32 = mybir.dt.float32
BF16 = mybir.dt.bfloat16
I16 = mybir.dt.int16
U32 = mybir.dt.uint32
ALU = mybir.AluOpType
ACT = mybir.ActivationFunctionType
AX = mybir.AxisListType

B, L, D = 32, 128, 256
H, DH = 16, 16
DC = D // 128
NP = 4
TOPK = 4
I = 768
IC = I // 128
WBLK = 32
QUAD = 4
NQ = B // QUAD
GRP = 8
HP = H * NP
PT = 16
HB = HP // PT
ROWS = 3 * 2 * PT
UNITS = 8
JH = L // 2
LN_EPS = 1e-5
LN_PARTS = (slice(0, 28), slice(28, B))
MAGIC = 1.5 * 2.0 ** 23
QMAX = 32767.0
WMAX = 7.0
DEQ = 2 * 3 * I * D // 128 // B


def constants():
    t = np.arange(L)
    f = np.arange(L // 2)
    w = 2 * np.pi * np.outer(t, f) / L
    fwd = np.zeros((L, L))
    fwd[:, :64] = np.cos(w)
    fwd[:, 64] = np.cos(np.pi * t)
    fwd[:, 65:] = np.sin(w[:, 1:])
    swp = np.concatenate([fwd[:, 64:], fwd[:, :64]], 1)
    cos2, sin2 = 2 * np.cos(w).T, 2 * np.sin(w).T
    cos2[0] = 1
    nyq = np.cos(np.pi * t)
    ma = np.concatenate([cos2, nyq[None], cos2[1:]]) / (L * DH)
    mb = np.concatenate([-sin2, np.zeros((1, L)), sin2[1:]]) / (L * DH)
    ia = np.concatenate([cos2, nyq[None], -cos2[1:]]) / L
    ib = np.concatenate([sin2, np.zeros((1, L)), sin2[1:]]) / L
    big = np.stack([fwd, swp, ma, mb, ia, ib, np.eye(L)], 1).astype(np.float32)

    n = np.arange(D)
    a = 2 * np.pi * (np.outer(n, n) % D) / D
    four = np.stack([np.cos(a), np.sin(a), -np.sin(a), np.cos(a) / D, -np.sin(a) / D])
    four = four.reshape(5, DC, 128, D).transpose(2, 0, 1, 3).astype(np.float32)

    small = np.zeros((3, 2, 128), np.float32)
    small[:, 0, 0] = L
    small[:, 1, :] = 1

    sel = np.zeros((3, 2, PT, PT // 2, 2, 2, JH), np.float32)
    j = L - JH + np.arange(JH)
    for n in range(PT // 2):
        for g in range(2):
            sel[:, 0, 2 * n + g, n, 0, g] = 1
            sel[:, 1, 2 * n + g, n, 0, g] = 1 - j
            sel[:, 0, 2 * n + g, n, 1, g] = -1
            sel[:, 1, 2 * n + g, n, 1, g] = 1 + j
    sel = sel.reshape(ROWS, PT // 2, 2, 128)

    mask = np.zeros((QUAD, H, D + QUAD), np.float32)
    for h in range(H):
        mask[:, h, h * DH:(h + 1) * DH] = 1
    for b in range(QUAD):
        mask[b, :, D + b] = 1
    mask = mask.reshape(QUAD * H, D + QUAD)

    col = np.zeros((128, 129), np.float32)
    col[:, 0] = np.linspace(0.0, 1.0, L)
    col[:, 1:] = np.arange(128)
    return {"c_big": big, "c_four": four, "c_small": small, "c_sel": sel, "c_mask": mask, "c_col": col}


BIASES = [("bq", D), ("bk", D), ("bv", D), ("bo", D), ("bf", D), ("bout", D), ("bval", D),
          ("boff", 2 * HP), ("batt", HP)]
NBIAS = sum(n for _, n in BIASES)
BAT = {}
_o = 0
for _n, _w in BIASES:
    BAT[_n] = _o
    _o += _w


def staggered(engine, n, steps):
    lag = max(k for k, _ in steps)
    head = lag + 2 + (lag % 2)
    turns = max(0, (n - head) // 2)

    def tick(t, parity, peeled):
        for k, step in steps:
            if not peeled or 0 <= t - k < n:
                step(t - k, (parity - k) % 2)

    for t in range(head):
        tick(t, t % 2, True)
    if turns:
        with engine.Fori(0, turns) as i:
            for u in range(2):
                tick(i * 2 + (head + u), u, False)
    for t in range(head + 2 * turns, n + lag):
        tick(t, t % 2, True)


def late(b, k):
    return not isinstance(b, int) or b >= k


def by_group(engine, tick):
    last = B // GRP
    for g in range(2):
        for j in range(GRP):
            tick(g, j)
    with engine.Fori(2, last) as g:
        for j in range(GRP):
            tick(g, j)
    for g in range(last, last + 2):
        for j in range(GRP):
            tick(g, j)


def by_quad(engine, step):
    for t in range(2):
        step(t, t)
    with engine.Fori(1, NQ // 2 - 1) as i:
        for u in range(2):
            step(i * 2 + u, u)
    for t in range(NQ - 2, NQ):
        step(t, t % 2)


def before_last(t):
    return not isinstance(t, int) or t < NQ - 1


def lagging(g, j, lag):
    b = g * GRP + (j - lag)
    return b if not isinstance(b, int) or 0 <= b < B else None


def is_group(g):
    return not isinstance(g, int) or 0 <= g < B // GRP


def at(b, n=1):
    return bass.ds(b, n) if not isinstance(b, int) else slice(b, b + n)


def build(nc, x, ctx_in, wq, wk, wv, wo, bq, bk, bv, bo, wfr, wfi, bf, wval, bval, woff, boff,
          watt, batt, wout, bout, wgate, wup, wdown, c_big, c_four, c_small, c_sel, c_mask, c_col, out):
    xr = x.rearrange("b l d -> l b d")
    cr = ctx_in.rearrange("b l d -> l b d")
    outr = out.rearrange("b l d -> l b d")
    with ExitStack() as ctx:
        def sem(name):
            return ctx.enter_context(nc.semaphore(name))

        def sb(name, shape, dt=F32, scope=ctx):
            return scope.enter_context(nc.sbuf_tensor(name, shape, dt))

        bank = [ctx.enter_context(nc.psum_tensor(f"bank{i}", [128, 512], F32)) for i in range(8)]

        big = sb("big", [128, 7, 128])
        FWD, SWP, MA, MB, IA, IB, IDN = (big[:, i, :] for i in range(7))
        stats = sb("stats", [128, B, 6])
        lnt = sb("lnt", [128, 5, B])
        ends = sb("ends", [128, 2, B])
        rstd, nmr = sb("rstd", [128, B]), sb("nmr", [128, B])
        half = sb("half", [128, B])
        sampling = ExitStack()
        down_a = sb("down_a", [128, 2, QUAD * L], F32, sampling)
        sampling.close()
        xn = sb("xn", [128, 2, D])
        tr_sb = sb("tr_sb", [128, 2, DC, 128])
        peak = sb("peak", [128, 5, 64])
        unit = sb("unit", [128, 8, 8])
        wgT = sb("wgT", [128, DC, I])
        wuT = sb("wuT", [128, DC, I])
        wdT = sb("wdT", [128, IC, D])

        x_sb = sb("x_sb", [128, B, D])

        ffn = ExitStack()
        wide = sb("wide", [128, IC, B * L], F32, ffn)
        xqT = sb("xqT", [128, DC, B * L], I16, ffn)
        xqs = sb("xqs", [128, 2, DC, QUAD * L], F32, ffn)
        sig_place = ExitStack()
        sig = sb("sig", [128, 2, IC, 256], F32, sig_place)
        sig_place.close()
        up_place = ExitStack()
        ups = sb("ups", [128, 2, IC, QUAD * L], F32, up_place)
        up_place.close()
        hid = sb("hid", [128, 4, IC, 128], F32, ffn)
        xn4 = sb("xn4", [128, 2, D], F32, ffn)
        ffn.close()

        small_f = sb("small_f", [3, 2, 128])
        small = sb("small", [3, 2, 128], BF16)
        dc3, ones3 = small[:, 0, :], small[:, 1, :]
        idn16 = sb("idn16", [128, 128], BF16)
        mask = sb("mask", [QUAD * H, D + QUAD])
        col = sb("col", [128, 129])
        refy, iota = col[:, 0:1], col[:, 1:129]
        bias3 = sb("bias3", [3, NBIAS], BF16)
        after0 = ExitStack()
        sel_place = ExitStack()
        sel_f = sb("sel_f", [ROWS, PT // 2, 2, 128], F32, sel_place)
        sel_place.close()
        parts_place = ExitStack()
        parts = sb("parts", [128, GRP * HB, 3, 2 * PT], BF16, parts_place)
        parts_place.close()
        vz = sb("vz", [128, 2, QUAD, D], F32, after0)
        attT = sb("attT", [128, DC, QUAD * L], F32, after0)
        after0.close()
        wT = sb("wT", [128, 4, DC, D])
        fold = sb("fold", [128, DC, D])
        wl1 = sb("wl1", [128, DC, 3 * HP])
        wval_sb = sb("wval_sb", [128, DC, D])
        wout_sb = sb("wout_sb", [128, DC, D])

        lay0 = ExitStack()
        c_sb = sb("c_sb", [128, B, D], F32, lay0)
        split = ExitStack()
        brow = sb("brow", [1, NBIAS], F32, split)
        bres = sb("bres", [1, NBIAS], F32, split)
        bpart = sb("bpart", [1, 3, NBIAS], BF16, split)
        split.close()
        vhat = sb("vhat", [128, B, D], F32, lay0)
        cst = sb("cst", [128, 2, D], F32, lay0)
        fold_place = ExitStack()
        pqT = sb("pqT", [128, 2, DC, D], F32, fold_place)
        fold_place.close()
        ft_sb = sb("ft_sb", [128, 2, 4, 128], F32, lay0)
        q_sb = sb("q_sb", [128, 2, D], F32, lay0)
        ab = sb("ab", [128, 2, 2, D], F32, lay0)
        deq = sb("deq", [128, 3, I * D // 128], F32, lay0)
        dsc = sb("dsc", [128, 3, DEQ // WBLK], F32, lay0)
        fnat = sb("fnat", [128, 2, DC, D], F32, lay0)
        setup = ExitStack()
        wnat = sb("wnat", [128, 4, DC, D], F32, setup)
        onat = sb("onat", [128, DC, 2 * HP], F32, setup)
        setup.close()
        sab = sb("sab", [128, 2, B * H], F32, lay0)
        corr = sb("corr", [128, 4, L], F32, lay0)
        top8 = sb("top8", [128, 4, 8], F32, lay0)
        idx8 = sb("idx8", [128, 4, 8], U32, lay0)
        idxf = sb("idxf", [128, 4, TOPK], F32, lay0)
        w4 = sb("w4", [128, 4, TOPK], F32, lay0)
        z4 = sb("z4", [128, 2, 4], F32, lay0)
        hot = sb("hot", [128, TOPK, L], F32, lay0)
        wrow = sb("wrow", [128, 4, L], F32, lay0)
        four_place = ExitStack()
        four = sb("four", [128, 5, DC, D], F32, four_place)
        four_place.close()
        wcol = sb("wcol", [128, 4 * L], F32, lay0)
        what = sb("what", [128, 2, B * H], F32, lay0)
        oT = sb("oT", [128, 2, DC, 128], F32, lay0)
        lay0.close()

        lay1 = ExitStack()
        ctx_place = ExitStack()
        rows = sb("rows", [ROWS, NQ, HB, QUAD * L], BF16, ctx_place)
        ctx_place.close()
        sb("ctx_keep", [128, B, D], F32, lay1)
        v_sb = sb("v_sb", [128, B, D], F32, lay1)
        v63 = sb("v63", [QUAD * H, NQ, D], F32, lay1)
        w63T = sb("w63T", [QUAD * H, NQ, L], F32, lay1)
        sel = sb("sel", [ROWS, PT // 2, 2, 128], BF16, lay1)
        weigh = ExitStack()
        cdup = sb("cdup", [128, 2, DC, 128], F32, weigh)
        cst1 = sb("cst1", [128, 2, D], F32, weigh)
        ccx = sb("ccx", [128, GRP, 2 * HP], F32, weigh)
        w63 = sb("w63", [128, B * H], F32, weigh)
        ctx63 = sb("ctx63", [128, DC, B * H], F32, weigh)
        off = sb("off", [128, GRP, 3 * HP], F32, weigh)
        tx, ty, te, tc, td = (sb(n, [128, GRP, HP], F32, weigh) for n in ("tx", "ty", "te", "tc", "td"))
        ts = sb("ts", [128, 3, GRP * H], F32, weigh)
        weigh.close()
        sample = ExitStack()
        v63m = sb("v63m", [QUAD * H, D], F32, sample)
        w63m = sb("w63m", [QUAD * H, QUAD, L], F32, sample)
        hat = sb("hat", [128, 4, QUAD * L], F32, sample)
        down_b = sb("down_b", [128, 2, QUAD * L], F32, sample)
        down = [down_a[:, 0, :], down_a[:, 1, :], down_b[:, 0, :], down_b[:, 1, :]]
        sample.close()
        lay1.close()

        load_c, load_x = sem("load_c"), [sem(f"load_x{i}") for i in range(8)]
        load_w, load_ctx, load_b = sem("load_w"), [sem(f"load_ctx{i}") for i in range(8)], sem("load_b")
        load_f, load_l = sem("load_f"), sem("load_l")
        half_set = sem("half_set")
        small_cast, bias_split, bias_placed = sem("small_cast"), sem("bias_split"), sem("bias_placed")
        wt_done, wt_copied = sem("wt_done"), sem("wt_copied")
        fold_mm, fold_copied = sem("fold_mm"), sem("fold_copied")
        l1_laid = sem("l1_laid")
        bn_done, ln_step, pow_done, ln_ready = sem("bn_done"), sem("ln_step"), sem("pow_done"), sem("ln_ready")
        ctx_staged = sem("ctx_staged")
        xn_ready, ft_done, ft_copied = sem("xn_ready"), sem("ft_done"), sem("ft_copied")
        proj_done, q_copied, v_copied = sem("proj_done"), sem("q_copied"), sem("v_copied")
        prod_done, sab_done = sem("prod_done"), sem("sab_done")
        corr_done, dve_b = sem("corr_done"), sem("dve_b")
        d4_ready, exp4_done, wrow_done = sem("d4_ready"), sem("exp4_done"), sem("wrow_done")
        wtr_done, wcol_done, what_mm, what_done = sem("wtr_done"), sem("wcol_done"), sem("what_mm"), sem("what_done")
        pa_done, pb_done, inv_done, oT_copied = sem("pa_done"), sem("pb_done"), sem("inv_done"), sem("oT_copied")
        wo_done, x1_done = sem("wo_done"), sem("x1_done")
        xn2_ready, tr2_done, tr2_copied, mm2_done, x2_done = (
            sem("xn2_ready"), sem("tr2_done"), sem("tr2_copied"), sem("mm2_done"), sem("x2_done"))
        stored = sem("stored")
        load_g, deq_step, gw_turned, gw_kept = sem("load_g"), sem("deq_step"), sem("gw_turned"), sem("gw_kept")
        xn4_done, ends_done, xq_ready, xq_turned, xq_kept = (
            sem("xn4_done"), sem("ends_done"), sem("xq_ready"), sem("xq_turned"), sem("xq_kept"))
        peak_col, peak_all, unit_step = sem("peak_col"), sem("peak_all"), sem("unit_step")
        xqs_ready, hid_mm, hid_kept, hid_peak = sem("xqs_ready"), sem("hid_mm"), sem("hid_kept"), sem("hid_peak")
        up_peak, up_round, up_whole = sem("up_peak"), sem("up_round"), sem("up_whole")
        g_round, g_whole, sig_done, sig_round, sig_whole, g2_done, g2_peak = (
            sem("g_round"), sem("g_whole"), sem("sig_done"), sem("sig_round"), sem("sig_whole"), sem("g2_done"), sem("g2_peak"))
        g2_round, o_done, o_peak = sem("g2_round"), sem("o_done"), sem("o_peak")
        o_round, o_whole, down_out, y_done = sem("o_round"), sem("o_whole"), sem("down_out"), sem("y_done")
        ctx1_staged, xn3_ready, tr3_done, tr3_copied = sem("ctx1_staged"), sem("xn3_ready"), sem("tr3_done"), sem("tr3_copied")
        mm3_done, v_kept, off_kept = sem("mm3_done"), sem("v_kept"), sem("off_kept")
        v63_mm, v63_kept = sem("v63_mm"), sem("v63_kept")
        wstep, logit_ready, exp_done = sem("wstep"), sem("logit_ready"), sem("exp_done")
        ccx_ready, w63_ready = sem("ccx_ready"), sem("w63_ready")
        load_sel, sel_ready = sem("load_sel"), sem("sel_ready")
        parts_turned, w63_turned, hi_done, res_done, mid_done, lo_done, w63_kept = (
            sem("parts_turned"), sem("w63_turned"), sem("hi_done"), sem("res_done"), sem("mid_done"), sem("lo_done"), sem("w63_kept"))
        rows_kept = [sem("rows_kept_act"), sem("rows_kept_dve")]
        edge_ready, edge_used = sem("edge_ready"), sem("edge_used")
        down_mm, up_mm, down_done, hat_done, taken = (
            sem("down_mm"), sem("up_mm"), sem("down_done"), sem("hat_done"), sem("taken"))
        attT_copied, out_mm, x3_done, vz_clear, vz_ready = (
            sem("attT_copied"), sem("out_mm"), sem("x3_done"), sem("vz_clear"), sem("vz_ready"))

        def at_seq(b):
            return bass.ds(b * L, L) if not isinstance(b, int) else slice(b * L, (b + 1) * L)

        def at_tokens(t):
            return bass.ds(t * QUAD * L, QUAD * L) if not isinstance(t, int) else slice(t * QUAD * L, (t + 1) * QUAD * L)

        def at_piece(t):
            return bass.ds(t * 256, 256) if not isinstance(t, int) else slice(t * 256, (t + 1) * 256)

        ccx_blocks = ccx[:].rearrange("p b (n k t) -> p (b n) k t", n=HB, k=2)
        ccx_rows = ccx[:].rearrange("p b (n r) -> p (b n) r", n=HB)

        def keep_rows(engine, g, u):
            engine.wait_ge(parts_turned, g * 2 + u + 1)
            for n in range(HB):
                out_rows = rows[:, at(g * 2 + u), n, :].rearrange("p o t -> p (o t)")
                if u == 0:
                    nc.scalar.activation(out_rows, bank[4 + n][0:ROWS, :], ACT.Copy).then_inc(rows_kept[0], 1)
                else:
                    nc.vector.tensor_copy(out_rows, bank[4 + n][0:ROWS, :]).then_inc(rows_kept[1], 1)

        block = ctx.enter_context(nc.Block())
        XL = B // 8

        @block.sync
        def _(sp):
            for i in range(8):
                sp.dma_start(x_sb[:, i * XL:(i + 1) * XL, :], xr[:, i * XL:(i + 1) * XL, :]).then_inc(load_x[i], 16)
            for i in range(8):
                sp.dma_start(c_sb[:, i * XL:(i + 1) * XL, :], cr[:, i * XL:(i + 1) * XL, :]).then_inc(load_ctx[i], 16)
            sp.wait_ge(bias_split, 4)
            sp.dma_start(bias3[:], bpart[:]).then_inc(bias_placed, 16)
            sp.wait_ge(wo_done, B)
            sp.dma_start(sel_f[:], c_sel).then_inc(load_sel, 16)
            sp.wait_ge(x3_done, 2 * NQ)
            for i in range(B // 2):
                sp.wait_ge(y_done, (i + 1) * 2)
                sp.dma_start(outr[:, i * 2:(i + 1) * 2, :], x_sb[:, i * 2:(i + 1) * 2, :]).then_inc(stored, 16)
            sp.wait_ge(stored, 16 * (B // 2))

        @block.gpsimd
        def _(pool):
            nc.gpsimd.memset(half[:], -0.5).then_inc(half_set, 1)

            def rstd_pow(n):
                pool.wait_ge(half_set, 1)
                for k in range(2):
                    pool.wait_ge(ln_step, 12 * (n - 1) + 6 * (k + 1))
                    nc.gpsimd.tensor_tensor(rstd[:, LN_PARTS[k]], lnt[:, 4, LN_PARTS[k]], half[:, LN_PARTS[k]], ALU.pow).then_inc(pow_done, 1)

            rstd_pow(1)

            def stage_ctx(b, s):
                if late(b, 2):
                    pool.wait_ge(ft_done, b - 1)
                nc.gpsimd.tensor_copy(cst[:, s, :], c_sb[:, at(b), :]).then_inc(ctx_staged, 1)

            def stage_pairs(first, last):
                for i in range(-(-first * 2 // XL), last * 2 // XL):
                    pool.wait_ge(load_ctx[i], 16)
                with pool.Fori(first, last) as k:
                    for u in range(2):
                        stage_ctx(k * 2 + u, u)

            pool.wait_ge(load_ctx[0], 16)
            for b in range(2):
                stage_ctx(b, b)
            stage_pairs(1, 4)
            stage_pairs(4, 8)
            stage_pairs(8, B // 2)

            pool.wait_ge(load_l, 16 * 6)
            ov = onat[:].rearrange("p c (n k) -> p c k n", k=2)
            nc.gpsimd.tensor_copy(wl1[:, :, 0:HP], ov[:, :, 0, :]).then_inc(l1_laid, 1)
            nc.gpsimd.tensor_copy(wl1[:, :, HP:2 * HP], ov[:, :, 1, :]).then_inc(l1_laid, 1)

            def product_b(b, s):
                if late(b, 2):
                    pool.wait_ge(inv_done, b - 1)
                nc.gpsimd.tensor_tensor(
                    ab[:, s, 1, :].rearrange("p (h d) -> p h d", h=H),
                    vhat[:, at(b), :].rearrange("p o (h d) -> p (o h) d", h=H),
                    what[:, 1, at(b * H, H)].unsqueeze(2).broadcast_to([128, H, DH]),
                    ALU.mult).then_inc(pb_done, 1)

            pool.wait_ge(what_done, 2)
            staggered(pool, B, [(0, product_b)])
            rstd_pow(2)
            rstd_pow(3)

            def stage_ctx1(b, s):
                if late(b, 2):
                    pool.wait_ge(tr3_done, b - 1)
                nc.gpsimd.tensor_copy(cst1[:, s, :], c_sb[:, at(b), :]).then_inc(ctx1_staged, 1)

            def tick_pool(g, j):
                b = lagging(g, j, 0)
                if b is not None:
                    stage_ctx1(b, j % 2)
                if j == 1 and is_group(g - 2):
                    pool.wait_ge(mid_done, g - 1)
                    nc.gpsimd.tensor_tensor(parts[:, :, 2, :], ccx_rows, parts[:, :, 1, :], ALU.subtract).then_inc(lo_done, 1)

            by_group(pool, tick_pool)
            pool.wait_ge(parts_turned, 2 * (B // GRP))
            nc.gpsimd.memset(vz[:], 0.0).then_inc(vz_clear, 1)

            pool.wait_ge(v63_kept, NQ)
            pool.wait_ge(w63_kept, 2)
            pool.wait_ge(v_kept, B)
            pool.wait_ge(vz_clear, 1)

            def part_heads(q, c):
                if late(q, 1):
                    pool.wait_ge(taken, (q - 1) * 2 * UNITS + (c + 1) * UNITS)
                for r in range(2):
                    def heads(a):
                        return a[:, :, c * 128:(c + 1) * 128].rearrange("p b (m r d) -> p b m r d", r=2, d=DH)[:, :, :, r, :]
                    nc.gpsimd.tensor_copy(heads(vz[:, r]), heads(v_sb[:, at(q * QUAD, QUAD), :])).then_inc(vz_ready, 1)

            def edge(q):
                part_heads(q, 0)
                if late(q, 1):
                    pool.wait_ge(edge_used, 2 * q)
                nc.gpsimd.tensor_tensor(v63m[:], v63[:, at(q), :].rearrange("p o d -> p (o d)"), mask[:, 0:D], ALU.mult).then_inc(edge_ready, 1)
                nc.gpsimd.tensor_tensor(w63m[:], w63T[:, at(q), :].broadcast_to([QUAD * H, QUAD, L]),
                                        mask[:, D:].unsqueeze(2).broadcast_to([QUAD * H, QUAD, L]), ALU.mult).then_inc(edge_ready, 1)
                part_heads(q, 1)

            edge(0)
            with pool.Fori(1, NQ) as q:
                edge(q)

            rstd_pow(4)

            def all_peak(n):
                pool.wait_ge(peak_col, n + 1)
                nc.gpsimd.partition_all_reduce(unit[:, n, 1:2], unit[:, n, 0:1], 128, bass.bass_isa.ReduceOp.max).then_inc(peak_all, 1)

            def widen(t, s, before=0):
                if before or late(t, 2):
                    pool.wait_ge(hid_mm, (before + t - 1) * IC)
                if not before:
                    pool.wait_ge(xq_kept, (t + 1) * QUAD)
                nc.gpsimd.tensor_copy(xqs[:, s], xqT[:, :, at_tokens(t)]).then_inc(xqs_ready, 1)

            all_peak(0)
            for t in range(2):
                widen(t, t)
            with pool.Fori(1, NQ // 2) as i:
                for u in range(2):
                    widen(i * 2 + u, u)
            all_peak(1)
            with pool.Fori(0, NQ // 2) as i:
                for u in range(2):
                    widen(i * 2 + u, u, NQ)
            all_peak(2)
            for t in range(2):
                widen(t, t, 2 * NQ)
            all_peak(3)
            with pool.Fori(1, NQ // 2) as i:
                for u in range(2):
                    widen(i * 2 + u, u, 2 * NQ)
            all_peak(4)

        @block.scalar
        def _(act):
            act.dma_start(big[:], c_big).then_inc(load_c, 16)
            act.dma_start(small_f[:], c_small).then_inc(load_c, 16)
            for i, w in enumerate((wq, wk, wv, wo)):
                act.dma_start(wnat[:, i], w.rearrange("(c p) d -> p c d", p=128)).then_inc(load_w, 16)
            for name, src in (("bq", bq), ("bk", bk), ("bv", bv), ("bo", bo), ("bf", bf), ("bval", bval), ("bout", bout)):
                act.dma_start(brow[:, BAT[name]:BAT[name] + D], src.rearrange("(a n) -> a n", a=1)).then_inc(load_b, 16)
            act.dma_start(brow[:, BAT["boff"]:BAT["boff"] + 2 * HP].rearrange("a (k n) -> a k n", k=2),
                          boff.rearrange("(a n k) -> a k n", a=1, k=2),
                          allow_slow_non_contiguous=True).then_inc(load_b, 16)
            act.dma_start(brow[:, BAT["batt"]:BAT["batt"] + HP], batt.rearrange("(a n) -> a n", a=1)).then_inc(load_b, 16)
            act.dma_start(deq[:, 0].rearrange("p (c d) -> p c d", d=D), wgate.rearrange("(c p) d -> p c d", p=128)).then_inc(load_g, 16)
            act.dma_start(deq[:, 1].rearrange("p (c d) -> p c d", d=D), wup.rearrange("(c p) d -> p c d", p=128)).then_inc(load_g, 16)
            act.dma_start(deq[:, 2].rearrange("p (c d) -> p c d", d=I), wdown.rearrange("(c p) d -> p c d", p=128)).then_inc(load_g, 16)
            act.dma_start(col[:], c_col).then_inc(load_l, 16)
            act.dma_start(mask[:], c_mask).then_inc(load_l, 16)
            act.dma_start(onat[:], woff.rearrange("(c p) n -> p c n", p=128)).then_inc(load_l, 16)
            act.dma_start(wl1[:, :, 2 * HP:], watt.rearrange("(c p) n -> p c n", p=128)).then_inc(load_l, 16)
            act.dma_start(wval_sb[:], wval.rearrange("(c p) n -> p c n", p=128)).then_inc(load_l, 16)
            act.dma_start(wout_sb[:], wout.rearrange("(c p) n -> p c n", p=128)).then_inc(load_l, 16)
            act.dma_start(four[:], c_four).then_inc(load_f, 16)
            act.dma_start(fnat[:, 0], wfr.rearrange("(c p) n -> p c n", p=128)).then_inc(load_f, 16)
            act.dma_start(fnat[:, 1], wfi.rearrange("(c p) n -> p c n", p=128)).then_inc(load_f, 16)

            for i in range(4):
                act.wait_ge(wt_done, i + 1)
                nc.scalar.activation(wT[:, i], bank[i][:].rearrange("p (c o) -> p c o", c=DC), ACT.Copy).then_inc(wt_copied, 1)
            def copy_ft(b, s):
                act.wait_ge(ft_done, b + 1)
                if late(b, 2):
                    act.wait_ge(proj_done, b - 1)
                nc.scalar.activation(ft_sb[:, s].rearrange("p c t -> p (c t)"), bank[s][:], ACT.Copy).then_inc(ft_copied, 1)

            def copy_qv(b, s):
                act.wait_ge(proj_done, b + 1)
                if late(b, 2):
                    act.wait_ge(prod_done, b - 1)
                nc.scalar.activation(q_sb[:, s, :], bank[2 + s][:, 0:D], ACT.Copy).then_inc(q_copied, 1)
                nc.scalar.activation(vhat[:, at(b), :].rearrange("p o d -> p (o d)"), bank[4 + s][:, 0:D], ACT.Copy).then_inc(v_copied, 1)

            staggered(act, B, [(0, copy_ft), (1, copy_qv)])

            for i in range(2):
                act.wait_ge(fold_mm, i + 1)
                nc.scalar.activation(pqT[:, i], bank[4 + i][:].rearrange("p (c o) -> p c o", c=DC), ACT.Copy).then_inc(fold_copied, 1)
            act.wait_ge(d4_ready, 1)
            nc.scalar.activation(w4[:], w4[:], ACT.Exp).then_inc(exp4_done, 1)
            act.wait_ge(fold_mm, 3)
            nc.scalar.activation(fold[:], bank[6][:].rearrange("p (c o) -> p c o", c=DC), ACT.Copy).then_inc(fold_copied, 1)
            for i in range(9):
                act.wait_ge(gw_turned, i + 1)
                nc.scalar.activation((wgT, wuT, wdT)[i // 3][:].rearrange("p c o -> p (c o)")[:, (i % 3) * 512:(i % 3 + 1) * 512],
                                     bank[6 + i % 2][:], ACT.Copy).then_inc(gw_kept, 1)

            act.wait_ge(wtr_done, 1)
            nc.scalar.activation(wcol[:], bank[1][:], ACT.Copy).then_inc(wcol_done, 1)
            for i in range(2):
                act.wait_ge(what_mm, i + 1)
                nc.scalar.activation(what[:, i, :], bank[2 + i][:], ACT.Copy).then_inc(what_done, 1)

            def copy_oT(b, s):
                act.wait_ge(inv_done, b + 1)
                if late(b, 2):
                    act.wait_ge(wo_done, b - 1)
                nc.scalar.activation(oT[:, s].rearrange("p c t -> p (c t)"), bank[4 + s][:, 0:D], ACT.Copy).then_inc(oT_copied, 1)

            staggered(act, B, [(0, copy_oT)])

            def copy_tr2(b, s):
                act.wait_ge(tr2_done, b + 1)
                if late(b, 2):
                    act.wait_ge(mm2_done, b - 1)
                nc.scalar.activation(tr_sb[:, s].rearrange("p c t -> p (c t)"), bank[s][:, 0:D], ACT.Copy).then_inc(tr2_copied, 1)

            staggered(act, B, [(0, copy_tr2)])

            def copy_tr3(b, s):
                act.wait_ge(tr3_done, b + 1)
                if late(b, 2):
                    act.wait_ge(mm3_done, b - 1)
                nc.scalar.activation(tr_sb[:, s].rearrange("p c t -> p (c t)"), bank[s][:, 0:D], ACT.Copy).then_inc(tr3_copied, 1)
                cT = bank[s][:, D:].rearrange("p (c t) -> p c t", c=DC)
                nc.scalar.activation(cdup[:, s].rearrange("p c (g j) -> p c g j", g=2),
                                     cT[:, :, JH:].unsqueeze(2).broadcast_to([128, DC, 2, JH]), ACT.Copy).then_inc(tr3_copied, 1)
                nc.scalar.activation(ctx63[:, :, at(b * H, H)], cT[:, :, JH - 1:JH].broadcast_to([128, DC, H]), ACT.Copy).then_inc(tr3_copied, 1)

            def keep_v(b, s):
                act.wait_ge(mm3_done, b + 1)
                nc.scalar.activation(v_sb[:, at(b), :].rearrange("p o d -> p (o d)"), bank[2 + s][:, 0:D], ACT.Copy).then_inc(v_kept, 1)

            act.wait_ge(load_sel, 16)
            nc.scalar.activation(sel[:], sel_f[:], ACT.Copy).then_inc(sel_ready, 1)
            act.wait_ge(sel_ready, 1)

            def tick_act(g, j):
                b = lagging(g, j, 0)
                if b is not None:
                    copy_tr3(b, j % 2)
                b = lagging(g, j, 1)
                if b is not None:
                    keep_v(b, (j - 1) % 2)
                if is_group(g - 1):
                    if j == 3:
                        act.wait_ge(logit_ready, g)
                        nc.scalar.activation(te[:], te[:], ACT.Exp).then_inc(exp_done, 1)
                    if j == 6:
                        act.wait_ge(ccx_ready, g)
                        if is_group(g - 2):
                            act.wait_ge(parts_turned, 2 * (g - 1))
                        nc.scalar.activation(parts[:, :, 0, :], ccx_rows, ACT.Copy).then_inc(hi_done, 1)
                if is_group(g - 2):
                    if j == 0:
                        act.wait_ge(res_done, g - 1)
                        nc.scalar.activation(parts[:, :, 1, :], ccx_rows, ACT.Copy).then_inc(mid_done, 1)
                    if j == 3:
                        keep_rows(act, g - 2, 0)
                if isinstance(g, int) and g == B // GRP and j == 4:
                    for q in range(NQ):
                        act.wait_ge(v63_mm, q + 1)
                        nc.scalar.activation(v63[:, q, :], bank[q % 2][0:QUAD * H, 0:D], ACT.Copy).then_inc(v63_kept, 1)

            by_group(act, tick_act)
            act.wait_ge(w63_turned, 1)
            for u in range(2):
                nc.scalar.activation(w63T[:].rearrange("p (g u) t -> p g u t", u=2)[:, :, u, :],
                                     bank[0][u * QUAD * H:(u + 1) * QUAD * H, :].rearrange("p (g t) -> p g t", t=L), ACT.Copy).then_inc(w63_kept, 1)

            def sample_act(q):
                for c in range(DC):
                    for u in range(UNITS):
                        for i in range(2):
                            n = (q * DC + c) * 2 * UNITS + 2 * u + i
                            act.wait_ge(down_mm, n + 1)
                            if c or u >= 2 or late(q, 1):
                                act.wait_ge(hat_done, n - 3)
                            nc.scalar.activation(down[(u % 2) * 2 + i], bank[6 + i][:], ACT.Relu).then_inc(down_done, 1)
                        if u == 3 and c == 1:
                            keep_attT(q, 0)
                        if u == 3 and c == 0 and late(q, 1):
                            keep_attT(q - 1, 1)

            def keep_attT(q, c):
                act.wait_ge(taken, (q * DC + c + 1) * UNITS)
                if c == 0 and late(q, 1):
                    act.wait_ge(out_mm, 2 * q)
                nc.scalar.activation(attT[:, c, :], bank[4 + c][:], ACT.Copy).then_inc(attT_copied, 1)

            sample_act(0)
            with act.Fori(1, NQ) as q:
                sample_act(q)
            keep_attT(NQ - 1, 1)

            def keep_xq(b, s):
                act.wait_ge(xq_turned, b + 1)
                nc.scalar.activation(xqT[:, :, at_seq(b)], bank[s][:, 0:D].rearrange("p (c t) -> p c t", c=DC),
                                     ACT.Copy, bias=-MAGIC).then_inc(xq_kept, 1)


            def keep_gate(t):
                for oc in range(IC):
                    act.wait_ge(hid_mm, t * IC + oc + 1)
                    nc.scalar.activation(wide[:, oc, at_tokens(t)], bank[2 + oc][:], ACT.Copy).then_inc(hid_kept, 1)

            def keep_quad(t, u):
                if before_last(t):
                    for k in range(QUAD):
                        keep_xq((t + 1) * QUAD + k, k % 2)
                keep_gate(t)

            for k in range(QUAD):
                keep_xq(k, k % 2)
            by_quad(act, keep_quad)

            def round_gate(t, s):
                g = wide[:, :, at_piece(t)]
                nc.scalar.activation(g, g, ACT.Identity, scale=unit[:, 1, 3:4], bias=unit[:, 7, 0:1]).then_inc(g_round, 1)

            def whole_gate(t, s):
                act.wait_ge(g_round, t + 1)
                g = wide[:, :, at_piece(t)]
                nc.scalar.activation(g, g, ACT.Copy, bias=-MAGIC).then_inc(g_whole, 1)

            def sigmoid(t, s):
                act.wait_ge(g_whole, t + 1)
                if late(t, 2):
                    act.wait_ge(g2_done, t - 1)
                nc.scalar.activation(sig[:, s], wide[:, :, at_piece(t)], ACT.Sigmoid, scale=unit[:, 1, 2:3]).then_inc(sig_done, 1)

            def round_sigmoid(t, s):
                act.wait_ge(sig_done, t + 1)
                nc.scalar.activation(sig[:, s], sig[:, s], ACT.Copy, scale=65536.0, bias=MAGIC).then_inc(sig_round, 1)

            act.wait_ge(unit_step, 1 + 2 * 5)
            staggered(act, 2 * NQ, [(0, round_gate), (2, whole_gate), (5, round_sigmoid), (4, sigmoid)])

            def round_up(t, s):
                if late(t, 2):
                    act.wait_ge(o_done, t - 1)
                for oc in range(IC):
                    act.wait_ge(hid_mm, (2 * NQ + t) * IC + oc + 1)
                    nc.scalar.activation(ups[:, s, oc, :], bank[2 + oc][:], ACT.Identity,
                                         scale=unit[:, 2, 3:4], bias=unit[:, 7, 0:1]).then_inc(up_round, 1)

            def round_g2(t, s):
                if isinstance(t, int) and t == 0:
                    act.wait_ge(unit_step, 1 + 4 * 5)
                g = wide[:, :, at_tokens(t)]
                nc.scalar.activation(g, g, ACT.Identity, scale=unit[:, 3, 3:4], bias=unit[:, 7, 0:1]).then_inc(g2_round, 1)

            act.wait_ge(unit_step, 1 + 3 * 5)
            staggered(act, NQ, [(0, round_up), (0, round_g2)])

            def round_o(b, s):
                if late(b, 2):
                    act.wait_ge(o_whole, b - 1)
                nc.scalar.activation(hid[:, 2 + s], wide[:, :, at_seq(b)], ACT.Identity, scale=unit[:, 4, 3:4], bias=unit[:, 7, 0:1]).then_inc(o_round, 1)

            act.wait_ge(unit_step, 1 + 5 * 5)
            staggered(act, B, [(0, round_o)])

        @block.tensor
        def _(pe):
            mm = nc.tensor.matmul

            pe.wait_ge(load_c, 32)
            pe.wait_ge(load_w, 16 * 4)
            for i in range(4):
                for oc in range(DC):
                    for dc in range(DC):
                        last = nc.tensor.transpose(bank[i][:, dc * D + oc * 128:dc * D + oc * 128 + 128],
                                                   wnat[:, i, oc, dc * 128:(dc + 1) * 128], IDN)
                last.then_inc(wt_done, 1)
            pe.wait_ge(wt_copied, 4)
            pe.wait_ge(small_cast, 2)
            pe.wait_ge(bias_placed, 16)

            def transform(b, s):
                pe.wait_ge(xn_ready, b + 1)
                pe.wait_ge(ctx_staged, b + 1)
                if late(b, 2):
                    pe.wait_ge(ft_copied, b - 1)
                for c in range(DC):
                    mm(bank[s][:, c * 128:(c + 1) * 128], xn[:, s, c * 128:(c + 1) * 128], FWD, start=True, stop=True)
                for c in range(DC):
                    last = mm(bank[s][:, D + c * 128:D + (c + 1) * 128], cst[:, s, c * 128:(c + 1) * 128], FWD,
                              start=True, stop=True)
                last.then_inc(ft_done, 1)

            def project(b, s):
                pe.wait_ge(ft_copied, b + 1)
                if late(b, 2):
                    pe.wait_ge(prod_done, b - 1)
                    pe.wait_ge(v_copied, b - 1)
                mm(bank[2 + s][:], dc3, bias3[:, BAT["bq"]:BAT["bq"] + 2 * D], start=True, stop=False)
                for i in range(2):
                    for c in range(DC):
                        mm(bank[2 + s][:, i * D:(i + 1) * D], ft_sb[:, s, i * DC + c, :], wT[:, i, c, :],
                           start=False, stop=(i == 1 and c == DC - 1))
                mm(bank[4 + s][:, 0:D], dc3, bias3[:, BAT["bv"]:BAT["bv"] + D], start=True, stop=False)
                for c in range(DC):
                    last = mm(bank[4 + s][:, 0:D], ft_sb[:, s, DC + c, :], wT[:, 2, c, :], start=False, stop=(c == DC - 1))
                last.then_inc(proj_done, 1)

            staggered(pe, B, [(0, transform), (1, project)])

            pe.wait_ge(sab_done, B)
            for k in range(4):
                mm(bank[0][:, k * L:(k + 1) * L], sab[:, 0, k * 128:(k + 1) * 128], MA, start=True, stop=False)
                last = mm(bank[0][:, k * L:(k + 1) * L], sab[:, 1, k * 128:(k + 1) * 128], MB, start=False, stop=True)
            last.then_inc(corr_done, 1)
            pe.wait_ge(load_f, 48)
            pe.wait_ge(v_copied, B)
            C_, S_, NS_, CD, NSD = (four[:, k] for k in range(5))
            wr, wi = fnat[:, 0], fnat[:, 1]
            for i, terms in enumerate((((wr, C_), (wi, S_)), ((wi, C_), (wr, NS_)))):
                for kc in range(DC):
                    for n, (w, m) in enumerate(terms):
                        for c in range(DC):
                            last = mm(bank[4 + i][:, kc * D:(kc + 1) * D], w[:, c, kc * 128:(kc + 1) * 128], m[:, c, :],
                                      start=(n == 0 and c == 0), stop=(n == 1 and c == DC - 1))
                last.then_inc(fold_mm, 1)
            pe.wait_ge(fold_copied, 2)
            for ncn in range(DC):
                for i, m in enumerate((CD, NSD)):
                    for c in range(DC):
                        last = mm(bank[6][:, ncn * D:(ncn + 1) * D], pqT[:, i, c, ncn * 128:(ncn + 1) * 128], m[:, c, :],
                                  start=(i == 0 and c == 0), stop=(i == 1 and c == DC - 1))
            last.then_inc(fold_mm, 1)
            pe.wait_ge(deq_step, 4 * B)
            pe.wait_ge(fold_copied, 3)
            blocks = ([(w, c, oc, D) for w in range(2) for c in range(DC) for oc in range(IC)]
                      + [(2, ic, oc, I) for ic in range(IC) for oc in range(DC)])
            for i in range(9):
                if i >= 2:
                    pe.wait_ge(gw_kept, i - 1)
                for k in range(4):
                    w, c, oc, width = blocks[i * 4 + k]
                    last = nc.tensor.transpose(bank[6 + i % 2][:, k * 128:(k + 1) * 128],
                                               deq[:, w, oc * width + c * 128:oc * width + (c + 1) * 128], IDN)
                last.then_inc(gw_turned, 1)

            pe.wait_ge(wrow_done, 4)
            for k in range(4):
                last = nc.tensor.transpose(bank[1][:, k * 128:(k + 1) * 128], wrow[:, k, :], IDN)
            last.then_inc(wtr_done, 1)
            pe.wait_ge(wcol_done, 1)
            for i, m in enumerate((FWD, SWP)):
                mm(bank[2 + i][:], m, wcol[:], start=True, stop=True).then_inc(what_mm, 1)

            def inverse(b, s):
                pe.wait_ge(pa_done, b + 1)
                pe.wait_ge(pb_done, b + 1)
                if late(b, 2):
                    pe.wait_ge(oT_copied, b - 1)
                for c in range(DC):
                    mm(bank[4 + s][:, c * 128:(c + 1) * 128], ab[:, s, 0, c * 128:(c + 1) * 128], IA, start=True, stop=False)
                    last = mm(bank[4 + s][:, c * 128:(c + 1) * 128], ab[:, s, 1, c * 128:(c + 1) * 128], IB, start=False, stop=True)
                last.then_inc(inv_done, 1)

            def project_out(b, s):
                pe.wait_ge(oT_copied, b + 1)
                if late(b, 2):
                    pe.wait_ge(x1_done, b - 1)
                mm(bank[6 + s][:, 0:D], ones3, bias3[:, BAT["bo"]:BAT["bo"] + D], start=True, stop=False)
                for c in range(DC):
                    last = mm(bank[6 + s][:, 0:D], oT[:, s, c, :], wT[:, 3, c, :], start=False, stop=(c == DC - 1))
                last.then_inc(wo_done, 1)

            staggered(pe, B, [(0, inverse), (1, project_out)])

            def turn2(b, s):
                pe.wait_ge(xn2_ready, b + 1)
                if late(b, 2):
                    pe.wait_ge(tr2_copied, b - 1)
                for c in range(DC):
                    last = nc.tensor.transpose(bank[s][:, c * 128:(c + 1) * 128], xn[:, s, c * 128:(c + 1) * 128], IDN)
                last.then_inc(tr2_done, 1)

            def frequency_ffn(b, s):
                pe.wait_ge(tr2_copied, b + 1)
                if late(b, 2):
                    pe.wait_ge(x2_done, b - 1)
                mm(bank[2 + s][:, 0:D], ones3, bias3[:, BAT["bf"]:BAT["bf"] + D], start=True, stop=False)
                for c in range(DC):
                    last = mm(bank[2 + s][:, 0:D], tr_sb[:, s, c, :], fold[:, c, :], start=False, stop=(c == DC - 1))
                last.then_inc(mm2_done, 1)

            staggered(pe, B, [(0, turn2), (1, frequency_ffn)])

            def turn3(b, s):
                pe.wait_ge(xn3_ready, b + 1)
                pe.wait_ge(ctx1_staged, b + 1)
                if late(b, 2):
                    pe.wait_ge(tr3_copied, 3 * (b - 1))
                for i, src in enumerate((xn, cst1)):
                    for c in range(DC):
                        last = nc.tensor.transpose(bank[s][:, i * D + c * 128:i * D + (c + 1) * 128],
                                                   src[:, s, c * 128:(c + 1) * 128], IDN)
                last.then_inc(tr3_done, 1)

            def project3(b, s):
                pe.wait_ge(tr3_copied, 3 * (b + 1))
                if late(b, 2):
                    pe.wait_ge(v_kept, b - 1)
                    pe.wait_ge(off_kept, b - 1)
                mm(bank[2 + s][:, 0:D + 3 * HP], ones3, bias3[:, BAT["bval"]:BAT["bval"] + D + 3 * HP], start=True, stop=False)
                for c in range(DC):
                    mm(bank[2 + s][:, 0:D], cdup[:, s, c, :], wval_sb[:, c, :], start=False, stop=False)
                for c in range(DC):
                    last = mm(bank[2 + s][:, D:D + 3 * HP], tr_sb[:, s, c, :], wl1[:, c, :], start=False, stop=(c == DC - 1))
                last.then_inc(mm3_done, 1)

            pe.wait_ge(l1_laid, 2)

            def turn_parts(g, u):
                pe.wait_ge(lo_done, g + 1)
                if u:
                    pe.wait_ge(rows_kept[0], (g + 1) * HB)
                elif late(g, 1):
                    pe.wait_ge(rows_kept[1], g * HB)
                for n in range(HB):
                    for b in range(QUAD):
                        last = mm(bank[4 + n][0:ROWS, b * L:(b + 1) * L],
                                  parts[:, (u * QUAD + b) * HB + n, :, :].rearrange("p a r -> p (a r)"), idn16[:],
                                  start=(b == 0), stop=(b == QUAD - 1))
                last.then_inc(parts_turned, 1)

            def values63(q):
                if q >= 2:
                    pe.wait_ge(v63_kept, q - 1)
                else:
                    pe.wait_ge(tr3_copied, 3 * B)
                o = bank[q % 2][0:QUAD * H, 0:D]
                mm(o, ones3[:, 0:QUAD * H], bias3[:, BAT["bval"]:BAT["bval"] + D], start=True, stop=False)
                for c in range(DC):
                    last = mm(o, ctx63[:, c, q * QUAD * H:(q + 1) * QUAD * H], wval_sb[:, c, :], start=False, stop=(c == DC - 1))
                last.then_inc(v63_mm, 1)

            def tick_pe(g, j):
                b = lagging(g, j, 0)
                if b is not None:
                    turn3(b, j % 2)
                b = lagging(g, j, 1)
                if b is not None:
                    project3(b, (j - 1) % 2)
                if is_group(g - 2) and j in (2, 4):
                    turn_parts(g - 2, j // 4)
                if isinstance(g, int) and g == B // GRP and j == 3:
                    for q in range(NQ):
                        values63(q)

            by_group(pe, tick_pe)
            pe.wait_ge(rows_kept[1], HB * B // GRP)
            pe.wait_ge(w63_ready, B // GRP)
            pe.wait_ge(v63_kept, NQ)
            for g in range(B // GRP):
                last = nc.tensor.transpose(bank[0][:, g * 128:(g + 1) * 128], w63[:, g * 128:(g + 1) * 128], IDN)
            last.then_inc(w63_turned, 1)

            def of_unit(u, i):
                m, r, pp = 2 * (u % 2) + i, u // 4, (u // 2) % 2
                return m, r, pp

            def sides(q, c, u):
                for i in range(2):
                    n = (q * DC + c) * 2 * UNITS + 2 * u + i
                    m, r, pp = of_unit(u, i)
                    pair = (2 * (m % 2) + r) * 2 + pp
                    row = rows[:, at(q), 2 * c + m // 2, :].rearrange("p o t -> p (o t)")
                    if c or u or late(q, 1):
                        pe.wait_ge(down_done, n - 1)
                    mm(bank[6 + i][:], sel[:, pair, 1, :], row, start=True, stop=True).then_inc(down_mm, 1)
                    if c or u >= 2 or late(q, 1):
                        pe.wait_ge(hat_done, n - 3)
                    mm(bank[(u % 2) * 2 + i][:], sel[:, pair, 0, :], row, start=True, stop=True).then_inc(up_mm, 1)

            def take(q, c, u):
                pe.wait_ge(hat_done, (q * DC + c) * 2 * UNITS + 2 * u + 2)
                for b in range(QUAD):
                    for i in range(2):
                        m, r, _ = of_unit(u, i)
                        w = c * 128 + 32 * m
                        last = mm(bank[4 + c][32 * m:32 * m + 32, b * 128:(b + 1) * 128], vz[:, r, b, w:w + 32],
                                  hat[:, (u % 2) * 2 + i, b * 128:(b + 1) * 128],
                                  start=False, stop=(u >= UNITS - 2 and b == QUAD - 1), skip_group_check=True)
                last.then_inc(taken, 1)

            def project_att(q, i):
                pe.wait_ge(attT_copied, 2 * q + 2)
                if i:
                    pe.wait_ge(x3_done, 2 * q + 1)
                mm(bank[5][:].rearrange("p (b d) -> p b d", b=2), ones3,
                   bias3[:, BAT["bout"]:BAT["bout"] + D].unsqueeze(1).broadcast_to([3, 2, D]), start=True, stop=False)
                for b in range(2):
                    for c in range(DC):
                        last = mm(bank[5][:, b * D:(b + 1) * D], attT[:, c, (2 * i + b) * L:(2 * i + b + 1) * L], wout_sb[:, c, :],
                                  start=False, stop=(b == 1 and c == DC - 1))
                last.then_inc(out_mm, 1)

            def sample_pe(q):
                for c in range(DC):
                    for u in range(UNITS):
                        sides(q, c, u)
                        if u == 2:
                            if c == 0:
                                pe.wait_ge(edge_ready, 2 * q + 2)
                            if late(q, 1):
                                pe.wait_ge(attT_copied, 2 * (q - 1) + c + 1)
                                if c == 1:
                                    pe.wait_ge(x3_done, 2 * q)
                            mm(bank[4 + c][:], v63m[:, c * 128:(c + 1) * 128], w63m[:].rearrange("p b t -> p (b t)"),
                               start=True, stop=True).then_inc(edge_used, 1)
                        if u >= 2:
                            if (u - 2) % 4 == 0:
                                pe.wait_ge(vz_ready, 4 * q + 2 * c + (u - 2) // 4 + 1)
                            take(q, c, u - 2)
                        elif c or late(q, 1):
                            take(q - 1 + c, 1 - c, UNITS - 2 + u)
                        if c == 0 and u in (4, 7) and late(q, 1):
                            project_att(q - 1, u // 7)

            pe.wait_ge(w63_kept, 2)
            pe.wait_ge(rows_kept[1], HB * B // GRP)
            sample_pe(0)
            with pe.Fori(1, NQ) as q:
                sample_pe(q)
            take(NQ - 1, 1, UNITS - 2)
            take(NQ - 1, 1, UNITS - 1)
            project_att(NQ - 1, 0)
            project_att(NQ - 1, 1)

            pe.wait_ge(attT_copied, 2 * NQ)

            def turn_xq(b, s):
                pe.wait_ge(xq_ready, b + 1)
                if late(b, 2):
                    pe.wait_ge(xq_kept, b - 1)
                for c in range(DC):
                    last = nc.tensor.transpose(bank[s][:, c * 128:(c + 1) * 128], xn[:, s, c * 128:(c + 1) * 128], IDN)
                last.then_inc(xq_turned, 1)


            def hidden(t, s, w, before, freed):
                pe.wait_ge(xqs_ready, before + t + 1)
                for oc in range(IC):
                    if late(t, 1):
                        pe.wait_ge(freed, (t - 1) * IC + oc + 1)
                    for c in range(DC):
                        last = mm(bank[2 + oc][:], w[:, c, oc * 128:(oc + 1) * 128], xqs[:, s, c, :], start=(c == 0), stop=(c == DC - 1))
                    last.then_inc(hid_mm, 1)

            def gate_quad(t, u):
                if before_last(t):
                    for k in range(QUAD):
                        turn_xq((t + 1) * QUAD + k, k % 2)
                hidden(t, u, wgT, 0, hid_kept)

            for k in range(QUAD):
                turn_xq(k, k % 2)
            by_quad(pe, gate_quad)

            for k, freed, last_freed in ((1, up_peak, hid_kept), (2, up_round, up_peak)):
                pe.wait_ge(last_freed, NQ * IC)
                for t in range(2):
                    hidden(t, t, wuT, k * NQ, freed)
                with pe.Fori(1, NQ // 2) as i:
                    for u in range(2):
                        hidden(i * 2 + u, u, wuT, k * NQ, freed)

            def down_product(b, s):
                pe.wait_ge(o_whole, b + 1)
                if late(b, 2):
                    pe.wait_ge(y_done, b - 1)
                for ic in range(IC):
                    last = mm(bank[s][:, 0:D], hid[:, s, ic, :], wdT[:, ic, :], start=(ic == 0), stop=(ic == IC - 1))
                last.then_inc(down_out, 1)

            pe.wait_ge(up_round, NQ * IC)
            staggered(pe, B, [(0, down_product)])

        @block.vector
        def _(dve):
            V = nc.vector

            def moments(b):
                V.bn_stats(stats[:, at(b), :].rearrange("p o s -> p (o s)"), x_sb[:, at(b), :].rearrange("p o d -> p (o d)")).then_inc(bn_done, 1)

            def split_biases():
                dve.wait_ge(load_b, 16 * len(BIASES))
                split3 = [bpart[:, k, :] for k in range(3)]
                V.tensor_copy(split3[0], brow[:]).then_inc(bias_split, 1)
                dve.wait_ge(bias_split, 1)
                V.tensor_tensor(bres[:], brow[:], split3[0], ALU.subtract).then_inc(bias_split, 1)
                dve.wait_ge(bias_split, 2)
                V.tensor_copy(split3[1], bres[:]).then_inc(bias_split, 1)
                dve.wait_ge(bias_split, 3)
                V.tensor_tensor(split3[2], bres[:], split3[1], ALU.subtract).then_inc(bias_split, 1)

            def ln_variance(n, part):
                p = LN_PARTS[part]
                me, ve, mo, vo = (stats[:, p, k] for k in (1, 2, 4, 5))
                r0, r1, r2, r3, r4 = (lnt[:, k, p] for k in range(5))
                dve.wait_ge(bn_done, B * (n - 1) + p.stop)
                k = 12 * (n - 1) + 6 * part
                V.tensor_tensor(r0, me, mo, ALU.add).then_inc(ln_step, 1)
                V.tensor_tensor(r1, me, mo, ALU.subtract).then_inc(ln_step, 1)
                V.tensor_tensor(r2, ve, vo, ALU.add).then_inc(ln_step, 1)
                dve.wait_ge(ln_step, k + 2)
                V.scalar_tensor_tensor(r3, r1, 0.25, r1, ALU.mult, ALU.mult).then_inc(ln_step, 1)
                dve.wait_ge(ln_step, k + 4)
                V.scalar_tensor_tensor(r2, r2, 1.0 / D, r3, ALU.mult, ALU.add).then_inc(ln_step, 1)
                dve.wait_ge(ln_step, k + 5)
                V.tensor_scalar(r4, r2, LN_EPS, None, ALU.add).then_inc(ln_step, 1)

            def ln_finish(n):
                ln_variance(n, 1)
                if n == 1:
                    split_biases()
                dve.wait_ge(pow_done, 2 * n)
                V.scalar_tensor_tensor(nmr[:], lnt[:, 0, :], -0.5, rstd[:], ALU.mult, ALU.mult).then_inc(ln_ready, 1)
                dve.wait_ge(ln_ready, n)

            def normalise(b, s, ready):
                V.tensor_scalar(xn[:, s, :], x_sb[:, at(b), :].rearrange("p o d -> p (o d)"), rstd[:, at(b)], nmr[:, at(b)],
                                ALU.mult, ALU.add).then_inc(ready, 1)

            for b in range(B):
                if b % XL == 0:
                    dve.wait_ge(load_x[b // XL], 16)
                moments(b)
                if b == LN_PARTS[0].stop:
                    ln_variance(1, 0)
            ln_finish(1)
            dve.wait_ge(load_c, 32)
            V.tensor_copy(small[:], small_f[:]).then_inc(small_cast, 1)
            V.tensor_copy(idn16[:], IDN).then_inc(small_cast, 1)

            def dequantise(b, s):
                def after(j):
                    if j or late(b, 1):
                        dve.wait_ge(deq_step, b * 4 + j)

                flat = deq[:].rearrange("p w n -> p (w n)")
                first = (b - s) * (DEQ // 2)
                w = (flat[:, first:first + DEQ] if isinstance(b, int) else flat[:, bass.ds(first, DEQ)]).rearrange("p (n k) -> p n k", k=WBLK)
                peaks, scale, inverse = (dsc[:, j, :] for j in range(3))

                def spread(a):
                    return a.unsqueeze(2).broadcast_to([128, DEQ // WBLK, WBLK])

                if s == 0:
                    if isinstance(b, int) and b == 0:
                        dve.wait_ge(load_g, 48)
                    after(0)
                    V.tensor_reduce(peaks, w, AX.X, ALU.max, apply_absolute_value=True).then_inc(deq_step, 1)
                    after(1)
                    V.tensor_scalar(scale, peaks, 1.0 / WMAX, 1e-12, ALU.mult, ALU.max).then_inc(deq_step, 1)
                    after(2)
                    V.reciprocal(inverse, scale).then_inc(deq_step, 1)
                    after(3)
                    V.tensor_tensor(w, w, spread(inverse), ALU.mult).then_inc(deq_step, 1)
                else:
                    after(0)
                    V.tensor_scalar(w, w, MAGIC, MAGIC, ALU.add, ALU.subtract).then_inc(deq_step, 1)
                    after(1)
                    V.tensor_scalar(w, w, WMAX, -WMAX - 1.0, ALU.min, ALU.max).then_inc(deq_step, 1)
                    after(2)
                    V.tensor_tensor(w, w, spread(scale), ALU.mult).then_inc(deq_step, 2)

            def norm0(b, s):
                if late(b, 2):
                    dve.wait_ge(ft_done, b - 1)
                normalise(b, s, xn_ready)

            def products(b, s):
                dve.wait_ge(q_copied, b + 1)
                if late(b, 2):
                    dve.wait_ge(sab_done, b - 1)
                q, k = q_sb[:, s, :], bank[2 + s][:, D:2 * D]
                V.tensor_tensor(ab[:, s, 0, :], q, k, ALU.mult)
                V.tensor_tensor(ab[0:64, s, 1, :], q[0:64], k[64:128], ALU.mult)
                V.tensor_tensor(ab[64:128, s, 1, :], q[64:128], k[0:64], ALU.mult).then_inc(prod_done, 1)

            def head_sums(b, s):
                dve.wait_ge(prod_done, b + 1)
                V.tensor_reduce(sab[:, :, at(b * H, H)], ab[:, s].rearrange("p a (h d) -> p a h d", h=H), AX.X, ALU.add).then_inc(sab_done, 1)

            staggered(dve, B, [(0, norm0), (2, products), (3, head_sums), (4, dequantise)])
            dve.wait_ge(load_l, 16 * 6)

            dve.wait_ge(corr_done, 1)
            V.tensor_copy(corr[:], bank[0][:].rearrange("p (k t) -> p k t", k=4)).then_inc(dve_b, 1)
            dve.wait_ge(dve_b, 1)
            for k in range(4):
                V.max(top8[:, k, :], corr[:, k, :]).then_inc(dve_b, 1)
            for k in range(4):
                dve.wait_ge(dve_b, 2 + k)
                V.max_index(idx8[:, k, :], top8[:, k, :], corr[:, k, :]).then_inc(dve_b, 1)
            V.tensor_tensor(w4[:], top8[:, :, 0:TOPK], top8[:, :, 0:1].broadcast_to([128, 4, TOPK]), ALU.subtract).then_inc(d4_ready, 1)
            dve.wait_ge(dve_b, 9)
            V.tensor_copy(idxf[:], idx8[:, :, 0:TOPK])
            dve.wait_ge(exp4_done, 1)
            V.tensor_reduce(z4[:, 0, :], w4[:], AX.X, ALU.add).then_inc(dve_b, 1)
            dve.wait_ge(dve_b, 10)
            V.reciprocal(z4[:, 1, :], z4[:, 0, :]).then_inc(dve_b, 1)
            dve.wait_ge(dve_b, 11)
            V.tensor_tensor(w4[:], w4[:], z4[:, 1, :].unsqueeze(2).broadcast_to([128, 4, TOPK]), ALU.mult).then_inc(dve_b, 1)
            for k in range(4):
                dve.wait_ge(dve_b, 12 + k)
                if k == 0:
                    dve.wait_ge(l1_laid, 2)
                if k:
                    dve.wait_ge(wrow_done, k)
                for i in range(TOPK):
                    last = V.tensor_scalar(hot[:, i, :], iota, idxf[:, k, i:i + 1], w4[:, k, i:i + 1], ALU.is_equal, ALU.mult)
                last.then_inc(dve_b, 1)
                dve.wait_ge(dve_b, 13 + k)
                V.tensor_reduce(wrow[:, k, :], hot[:].rearrange("p i t -> p t i"), AX.X, ALU.add).then_inc(wrow_done, 1)

            def product_a(b, s):
                if late(b, 2):
                    dve.wait_ge(inv_done, b - 1)
                V.tensor_tensor(ab[:, s, 0, :].rearrange("p (h d) -> p h d", h=H),
                                vhat[:, at(b), :].rearrange("p o (h d) -> p (o h) d", h=H),
                                what[:, 0, at(b * H, H)].unsqueeze(2).broadcast_to([128, H, DH]),
                                ALU.mult).then_inc(pa_done, 1)

            def add_x(b, s, done, source, landed):
                dve.wait_ge(done, b + 1)
                xb = x_sb[:, at(b), :].rearrange("p o d -> p (o d)")
                V.tensor_tensor(xb, source[:, 0:D], xb, ALU.add).then_inc(landed, 1)

            def moments_of(landed, n):
                def step(b, s):
                    dve.wait_ge(landed, b + 1)
                    moments(b)
                    if isinstance(b, int) and b == LN_PARTS[0].stop + 1:
                        ln_variance(n, 0)
                return step

            dve.wait_ge(what_done, 2)
            dve.wait_ge(v_copied, B)
            staggered(dve, B, [(0, product_a), (2, lambda b, s: add_x(b, s, wo_done, bank[6 + s], x1_done)), (3, moments_of(x1_done, 2))])
            ln_finish(2)

            def norm2(b, s):
                if late(b, 2):
                    dve.wait_ge(tr2_done, b - 1)
                normalise(b, s, xn2_ready)

            staggered(dve, B, [(0, norm2), (2, lambda b, s: add_x(b, s, mm2_done, bank[2 + s], x2_done)), (3, moments_of(x2_done, 3))])
            ln_finish(3)

            def norm3(b, s):
                if late(b, 2):
                    dve.wait_ge(tr3_done, b - 1)
                normalise(b, s, xn3_ready)

            def keep_off(b, s, j):
                dve.wait_ge(mm3_done, b + 1)
                dve.wait_ge(v_kept, b + 1)
                V.tensor_copy(off[:, j, :], bank[2 + s][:, D:D + 3 * HP]).then_inc(off_kept, 1)

            NS = 13

            def sampling_weights(g, j):
                o = off[:]
                offx, offy, att = o[:, :, 0:HP], o[:, :, HP:2 * HP], o[:, :, 2 * HP:]
                att4 = att.rearrange("p b (h k) -> p b h k", k=NP)

                def heads(a):
                    return a.rearrange("p (b h) -> p b h", b=GRP).unsqueeze(3).broadcast_to([128, GRP, H, NP])

                def point(a):
                    return a.rearrange("p b (h k) -> p b h k", k=NP)

                def blocks(a):
                    return a.rearrange("p b (n t) -> p (b n) t", n=HB)

                def after(k):
                    if k or late(g, 1):
                        dve.wait_ge(wstep, g * NS + k)

                if j == 1:
                    dve.wait_ge(off_kept, (g + 1) * GRP)
                    after(0)
                    V.tensor_reduce(ts[:, 0, :].rearrange("p (b h) -> p b h", b=GRP), att4, AX.X, ALU.max).then_inc(wstep, 1)
                    V.tensor_scalar(tx[:], offx, 0.0, 1.0, ALU.max, ALU.min).then_inc(wstep, 1)
                    V.tensor_scalar(ty[:], offy, refy, 0.0, ALU.add, ALU.max).then_inc(wstep, 1)
                    after(1)
                    V.tensor_tensor(point(te[:]), att4, heads(ts[:, 0, :]), ALU.subtract).then_inc(logit_ready, 1)
                if j == 2:
                    after(2)
                    V.tensor_scalar(tx[:], tx[:], 1.0, L / 2.0, ALU.add, ALU.mult).then_inc(wstep, 1)
                    after(3)
                    V.tensor_scalar(ty[:], ty[:], 1.0, 1.0, ALU.min, ALU.add).then_inc(wstep, 1)
                if j == 3:
                    after(4)
                    V.tensor_scalar(tx[:], tx[:], 0.5, None, ALU.subtract).then_inc(wstep, 1)
                    after(5)
                    V.tensor_scalar(ty[:], ty[:], 1.0, -0.5, ALU.subtract, ALU.mult).then_inc(wstep, 1)
                    after(6)
                    V.tensor_scalar(td[:], tx[:], -1.0, JH * 1.0, ALU.mult, ALU.add).then_inc(wstep, 1)
                if j == 4:
                    dve.wait_ge(exp_done, g + 1)
                    V.tensor_reduce(ts[:, 1, :].rearrange("p (b h) -> p b h", b=GRP), point(te[:]), AX.X, ALU.add).then_inc(wstep, 1)
                    after(9)
                    V.reciprocal(ts[:, 2, :], ts[:, 1, :]).then_inc(wstep, 1)
                if j == 5:
                    after(10)
                    V.tensor_tensor(point(te[:]), point(te[:]), heads(ts[:, 2, :]), ALU.mult).then_inc(wstep, 1)
                    after(11)
                    if late(g, 1):
                        dve.wait_ge(lo_done, g)
                    V.scalar_tensor_tensor(ccx_blocks[:, :, 1, :], blocks(ty[:]), 1.0, blocks(te[:]), ALU.add, ALU.mult).then_inc(wstep, 1)
                    after(12)
                    V.tensor_tensor(ccx_blocks[:, :, 0, :], ccx_blocks[:, :, 1, :], blocks(tx[:]), ALU.mult).then_inc(ccx_ready, 1)
                if j == 6:
                    V.scalar_tensor_tensor(blocks(tc[:]), blocks(td[:]), 0.0, ccx_blocks[:, :, 1, :], ALU.max, ALU.mult).then_inc(wstep, 1)
                    after(13)
                    V.tensor_reduce(w63[:, at(g * GRP * H, GRP * H)].rearrange("p (b h) -> p b h", b=GRP), point(tc[:]), AX.X, ALU.add).then_inc(w63_ready, 1)
                if j == 7:
                    dve.wait_ge(hi_done, g + 1)
                    V.tensor_tensor(ccx_rows, ccx_rows, parts[:, :, 0, :], ALU.subtract).then_inc(res_done, 1)

            def tick_dve(g, j):
                b = lagging(g, j, 0)
                if b is not None:
                    norm3(b, j % 2)
                b = lagging(g, j, 2)
                if b is not None:
                    if j == 2 and is_group(g - 1):
                        dve.wait_ge(wstep, (g - 1) * NS + 3)
                        dve.wait_ge(logit_ready, g)
                    keep_off(b, (j - 2) % 2, (j - 2) % GRP)
                if is_group(g - 1):
                    sampling_weights(g - 1, j)
                if is_group(g - 2) and j == 5:
                    keep_rows(dve, g - 2, 1)

            by_group(dve, tick_dve)

            def sample_dve(q):
                for c in range(DC):
                    for u in range(UNITS):
                        for i in range(2):
                            n = (q * DC + c) * 2 * UNITS + 2 * u + i
                            dve.wait_ge(up_mm, n + 1)
                            dve.wait_ge(down_done, n + 1)
                            if i == 0 and (c or u >= 2 or late(q, 1)):
                                dve.wait_ge(taken, (q * DC + c) * UNITS + u - 1)
                            k = (u % 2) * 2 + i
                            V.scalar_tensor_tensor(hat[:, k, :], bank[k][:], 0.0, down[k], ALU.max, ALU.min).then_inc(hat_done, 1)
                        if late(q, 1):
                            if (c, u) in ((0, 5), (1, 0)):
                                add_out(q - 1, c)
                            if c == 1 and u in (2, 4):
                                moments_out(q - 1, u // 4)

            def add_out(q, i):
                dve.wait_ge(out_mm, 2 * q + i + 1)
                xb = x_sb[:, at(q * QUAD + 2 * i, 2), :]
                V.tensor_tensor(xb, bank[5][:].rearrange("p (b d) -> p b d", b=2), xb, ALU.add).then_inc(x3_done, 1)

            def moments_out(q, i):
                dve.wait_ge(x3_done, 2 * q + i + 1)
                for b in range(2):
                    moments(q * QUAD + 2 * i + b)
                two = q * QUAD + 2 * i
                V.tensor_reduce(ends[:, 0, at(two, 2)], x_sb[:, at(two, 2), :], AX.X, ALU.max).then_inc(ends_done, 1)
                V.tensor_reduce(ends[:, 1, at(two, 2)], x_sb[:, at(two, 2), :], AX.X, ALU.min).then_inc(ends_done, 1)

            sample_dve(0)
            with dve.Fori(1, NQ) as q:
                sample_dve(q)
            ln_variance(4, 0)
            add_out(NQ - 1, 0)
            add_out(NQ - 1, 1)
            moments_out(NQ - 1, 0)
            moments_out(NQ - 1, 1)

            ln_finish(4)
            V.memset(unit[:, 5:8, :], 1.0).then_inc(unit_step, 1)
            dve.wait_ge(unit_step, 1)
            V.memset(unit[:, 7, 0:1], MAGIC)

            dve.wait_ge(ends_done, B)
            for k in range(2):
                V.tensor_tensor(lnt[:, k, :], ends[:, k, :], rstd[:], ALU.mult).then_inc(ends_done, 1)
            for k in range(2):
                dve.wait_ge(ends_done, B + 1 + k)
                V.tensor_tensor(ends[:, k, :], lnt[:, k, :], nmr[:], ALU.add).then_inc(ends_done, 1)
            dve.wait_ge(ends_done, B + 4)
            V.tensor_reduce(peak[:, 0, 0:1], ends[:], AX.XY, ALU.max, apply_absolute_value=True).then_inc(ends_done, 1)

            def make_unit(n, count):
                V.tensor_reduce(unit[:, n, 0:1], peak[:, n, 0:count], AX.X, ALU.max).then_inc(peak_col, 1)
                dve.wait_ge(peak_all, n + 1)
                raw = unit[:, 5, n:n + 1]
                k = n * 5 + 1
                V.tensor_tensor(unit[:, n, 4:5], unit[:, n, 1:2], raw, ALU.mult).then_inc(unit_step, 1)
                dve.wait_ge(unit_step, k + 1)
                V.tensor_scalar(unit[:, n, 2:3], unit[:, n, 4:5], 1.0 / QMAX, 1e-12, ALU.mult, ALU.max).then_inc(unit_step, 1)
                dve.wait_ge(unit_step, k + 2)
                V.reciprocal(unit[:, n, 5:6], unit[:, n, 2:3]).then_inc(unit_step, 1)
                dve.wait_ge(unit_step, k + 3)
                V.tensor_tensor(unit[:, n, 3:4], unit[:, n, 5:6], raw, ALU.mult).then_inc(unit_step, 1)
                if n == 0:
                    V.tensor_copy(unit[:, 5, 1:3], unit[:, 0, 2:3].broadcast_to([128, 2])).then_inc(unit_step, 1)
                elif n == 1:
                    V.tensor_scalar(unit[:, 5, 3:4], unit[:, 1, 2:3], 1.0 / 65536, None, ALU.mult).then_inc(unit_step, 1)
                elif n == 3:
                    V.tensor_tensor(unit[:, 5, 4:5], unit[:, 3, 2:3], unit[:, 2, 2:3], ALU.mult).then_inc(unit_step, 1)
                else:
                    V.tensor_copy(unit[:, 6, n:n + 1], unit[:, n, 2:3]).then_inc(unit_step, 1)
                dve.wait_ge(unit_step, k + 5)

            dve.wait_ge(ends_done, B + 5)
            make_unit(0, 1)

            def norm4(b, s):
                if late(b, 2):
                    dve.wait_ge(xq_ready, b - 1)
                V.tensor_scalar(xn4[:, s, :], x_sb[:, at(b), :].rearrange("p o d -> p (o d)"), rstd[:, at(b)], nmr[:, at(b)],
                                ALU.mult, ALU.add).then_inc(xn4_done, 1)

            def quantise_x(b, s):
                dve.wait_ge(xn4_done, b + 1)
                if late(b, 2):
                    dve.wait_ge(xq_turned, b - 1)
                V.tensor_scalar(xn[:, s, :], xn4[:, s, :], unit[:, 0, 3:4], MAGIC, ALU.mult, ALU.add).then_inc(xq_ready, 1)


            def peak_gate(t):
                dve.wait_ge(hid_kept, (t + 1) * IC)
                V.tensor_reduce(peak[:, 1, at(t)], wide[:, :, at_tokens(t)], AX.XY, ALU.max, apply_absolute_value=True).then_inc(hid_peak, 1)

            def quantise_quad(t):
                for k in range(QUAD + 1):
                    if k < QUAD:
                        norm4(t * QUAD + k, k % 2)
                    if k:
                        quantise_x(t * QUAD + k - 1, (k - 1) % 2)

            def peak_quad(t, u):
                if before_last(t):
                    quantise_quad(t + 1)
                if late(t, 1):
                    peak_gate(t - 1)

            quantise_quad(0)
            by_quad(dve, peak_quad)
            peak_gate(NQ - 1)
            dve.wait_ge(hid_peak, NQ)
            make_unit(1, NQ)

            def peak_up(t, s):
                for j in range(IC // 2):
                    dve.wait_ge(hid_mm, NQ * IC + t * (IC // 2) + j + 1)
                    V.tensor_reduce(peak[:, 2, at(t * (IC // 2) + j)], bank[2 + s * (IC // 2) + j][:], AX.X, ALU.max,
                                    apply_absolute_value=True).then_inc(up_peak, 1)

            def whole_sigmoid(t, s):
                dve.wait_ge(sig_round, t + 1)
                V.tensor_scalar(sig[:, s], sig[:, s], MAGIC, 65535.0, ALU.subtract, ALU.min).then_inc(sig_whole, 1)

            def gated(t, s):
                dve.wait_ge(sig_whole, t + 1)
                g = wide[:, :, at_piece(t)]
                V.scalar_tensor_tensor(g, sig[:, s], 0.0, g, ALU.max, ALU.mult).then_inc(g2_done, 1)

            def peak_gated(t, s):
                dve.wait_ge(g2_done, t + 1)
                V.tensor_reduce(peak[:, 3, at(t)], wide[:, :, at_piece(t)], AX.XY, ALU.max, apply_absolute_value=True).then_inc(g2_peak, 1)

            staggered(dve, 2 * NQ, [(0, peak_up), (1, gated), (0, whole_sigmoid), (2, peak_gated)])
            dve.wait_ge(up_peak, NQ * IC)
            make_unit(2, NQ * IC)
            dve.wait_ge(g2_peak, 2 * NQ)
            make_unit(3, 2 * NQ)

            def whole_up(t, s):
                dve.wait_ge(up_round, (t + 1) * IC)
                V.tensor_scalar(ups[:, s], ups[:, s], MAGIC, None, ALU.subtract).then_inc(up_whole, 1)

            def hidden_product(t, s):
                dve.wait_ge(up_whole, t + 1)
                dve.wait_ge(g2_round, t + 1)
                g = wide[:, :, at_tokens(t)]
                V.scalar_tensor_tensor(g, g, MAGIC, ups[:, s], ALU.subtract, ALU.mult).then_inc(o_done, 1)

            def peak_product(t, s):
                dve.wait_ge(o_done, t + 1)
                V.tensor_reduce(peak[:, 4, at(t)], wide[:, :, at_tokens(t)], AX.XY, ALU.max, apply_absolute_value=True).then_inc(o_peak, 1)

            staggered(dve, NQ, [(0, whole_up), (0, hidden_product), (1, peak_product)])
            dve.wait_ge(o_peak, NQ)
            make_unit(4, NQ)

            def whole_hidden(b, s):
                dve.wait_ge(o_round, b + 1)
                if late(b, 2):
                    dve.wait_ge(down_out, b - 1)
                V.tensor_scalar(hid[:, s], hid[:, 2 + s], MAGIC, None, ALU.subtract).then_inc(o_whole, 1)

            def add_y(b, s):
                dve.wait_ge(down_out, b + 1)
                xb = x_sb[:, at(b), :].rearrange("p o d -> p (o d)")
                V.scalar_tensor_tensor(xb, bank[s][:, 0:D], unit[:, 4, 2:3], xb, ALU.mult, ALU.add).then_inc(y_done, 1)

            staggered(dve, B, [(0, whole_hidden), (2, add_y)])


_INS = ["x", "ctx_1024", "L0_xattn_Wq", "L0_xattn_Wk", "L0_xattn_Wv", "L0_xattn_Wo", "L0_xattn_bq", "L0_xattn_bk",
        "L0_xattn_bv", "L0_xattn_bo", "L0_ffn_w_freq_real", "L0_ffn_w_freq_imag", "L0_ffn_bias", "L1_xattn_w_value",
        "L1_xattn_b_value", "L1_xattn_w_off", "L1_xattn_b_off", "L1_xattn_w_attw", "L1_xattn_b_attw", "L1_xattn_w_out",
        "L1_xattn_b_out", "L1_ffn_w_gate", "L1_ffn_w_up", "L1_ffn_w_down"]


def kernel(**inputs):
    import concourse.bacc as _bacc
    from concourse.bass_utils import run_bass_kernel_spmd as _run

    nc = _bacc.Bacc("TRN2", target_bir_lowering=False, num_devices=1)
    arrays, args = {}, []
    named = [(n, np.ascontiguousarray(inputs[n])) for n in _INS] + list(constants().items())
    for name, a in named:
        arrays[f"in_{name}_dram"] = a
        args.append(nc.dram_tensor(f"in_{name}_dram", a.shape, mybir.dt.from_np(a.dtype), kind="ExternalInput").ap())
    args.append(nc.dram_tensor("out_0_dram", (B, L, D), F32, kind="ExternalOutput").ap())
    build(nc, *args)
    return _run(nc, [arrays], core_ids=[0]).results[0]["out_0_dram"]
```
